# Optimizing a Trainium2 kernel written in Bass

```python
import numpy as np
import jax
import jax.numpy as jnp

def _softmax(x, axis=-1):
    return jax.nn.softmax(x, axis=axis)

def _gelu(x):
    return jax.nn.gelu(x, approximate=True)

def _silu(x):
    return jax.nn.silu(x)

def _sigmoid(x):
    return jax.nn.sigmoid(x)

def _layernorm(x, axis=-1, eps=1e-05):
    m = jnp.mean(x, axis=axis, keepdims=True)
    v = jnp.var(x, axis=axis, keepdims=True)
    return (x - m) / jnp.sqrt(v + eps)

def _scatter_add(tgt, idx, src, axis=0):
    return tgt.at[idx].add(src)

def _segment_sum(src, seg, n):
    return jax.ops.segment_sum(src, seg, n)
kernel_name = 'mk_gps_d2_gnn_r16_69972f'

def setup_inputs(seed: int=0):
    np.random.seed(seed)
    _w = jnp.asarray

    def _rec_inputs():
        import jax
        import jax.numpy as jnp
        _gk = jax.random.key(seed)
        x = -0.0006008 + 1.001 * jax.random.normal(jax.random.fold_in(_gk, 1), (3125, 256), jnp.float32)
        src = jax.random.randint(jax.random.fold_in(_gk, 2), (100000,), 0, 3125, jnp.int32)
        dst = jnp.minimum((3125 * jax.random.uniform(jax.random.fold_in(_gk, 3), (100000,)) ** 2.0).astype(jnp.int32), 49999)
        _o = jnp.argsort(dst, stable=True)
        src = src[_o]
        dst = dst[_o]
        edge_attr_64 = 0.000312547 + 1.00004 * jax.random.normal(jax.random.fold_in(_gk, 12), (100000, 64), jnp.float32)
        edge_type_16 = jax.random.randint(jax.random.fold_in(_gk, 14), (100000,), 0, 16, jnp.int32)
        edge_weight1 = jax.random.uniform(jax.random.fold_in(_gk, 15), (100000, 1), jnp.float32, 0.0, 0.999998)
        return (x, src, dst, edge_attr_64, edge_type_16, edge_weight1)
    x, src, dst, edge_attr_64, edge_type_16, edge_weight1 = _rec_inputs()

    def _L0_gnn_setup():
        import jax, jax.numpy as jnp
        import numpy as np
        N, E, H, DE = (625, 15625, 256, 64)
        EPS = 1e-05

        def _lin_init(k, fan_in, shape):
            s = 1.0 / np.sqrt(fan_in)
            return jax.random.uniform(k, shape, jnp.float32, -s, s)
        key = jax.random.key(seed)
        ks = jax.random.split(key, 12)
        x = jax.random.normal(ks[0], (N, H), jnp.float32)
        edge_index = jax.random.randint(ks[1], (2, E), 0, N)
        edge_attr = jax.random.normal(ks[2], (E, DE), jnp.float32)
        d_in = H + DE
        W1 = _lin_init(ks[3], d_in, (d_in, H))
        b1 = _lin_init(ks[4], d_in, (H,))
        W2 = _lin_init(ks[5], H, (H, H))
        b2 = _lin_init(ks[6], H, (H,))
        Wg = _lin_init(ks[7], d_in, (d_in, H))
        bg = _lin_init(ks[8], d_in, (H,))
        gamma = jnp.ones((H,), jnp.float32)
        beta = jnp.zeros((H,), jnp.float32)
        return {'x': x, 'edge_index': edge_index, 'edge_attr': edge_attr, 'W1': W1, 'b1': b1, 'W2': W2, 'b2': b2, 'Wg': Wg, 'bg': bg, 'gamma': gamma, 'beta': beta}
    _L0_gnn_all = _L0_gnn_setup()
    _L0_gnn_in = {k: v for k, v in _L0_gnn_all.items() if k in ('W1', 'b1', 'W2', 'b2', 'Wg', 'bg', 'gamma', 'beta')}
    del _L0_gnn_all

    def _L0_mix_setup():
        import jax, jax.numpy as jnp
        import numpy as np
        BN_EPS = 1e-05
        key = jax.random.key(seed)
        ks = jax.random.split(key, 4)
        B, N, D = (8, 512, 256)
        outD = 256
        s = 1.0 / np.sqrt(D)
        return {'feature': jax.random.normal(ks[0], (B, N, D), dtype=jnp.float32), 'W_qk': jax.random.normal(ks[1], (2, D, D), dtype=jnp.float32) * s, 'b_qk': jnp.zeros((2, D), dtype=jnp.float32), 'W_v': jax.random.normal(ks[2], (D, outD), dtype=jnp.float32) * s, 'b_v': jnp.zeros((outD,), dtype=jnp.float32), 'gamma': jnp.ones((D,), dtype=jnp.float32), 'beta': jnp.zeros((D,), dtype=jnp.float32)}
    _L0_mix_all = _L0_mix_setup()
    _L0_mix_in = {k: v for k, v in _L0_mix_all.items() if k in ('W_qk', 'b_qk', 'W_v', 'b_v', 'gamma', 'beta')}
    del _L0_mix_all

    def _L0_ffn_setup():
        import jax, jax.numpy as jnp
        import numpy as np
        NUM_EXPERTS = 8
        TOP_K = 2
        B, S, D = (8, 512, 256)

        def _moe(tokens, router_w, w1, b1, w2, b2):
            N = tokens.shape[0]
            E = router_w.shape[0]
            logits = tokens.astype(jnp.float32) @ router_w.astype(jnp.float32).T
            probs = jax.nn.softmax(logits, axis=-1)
            rw, re = jax.lax.top_k(probs, TOP_K)
            if TOP_K > 1:
                rw = rw / jnp.maximum(rw.sum(-1, keepdims=True), 1e-12)
            rw = rw.astype(tokens.dtype)
            combine = jnp.zeros((N, E), tokens.dtype).at[jnp.arange(N)[:, None], re].set(rw)
            out = tokens
            for e in range(E):
                h = jax.nn.gelu(tokens @ w1[e] + b1[e], approximate=False)
                y = h @ w2[e] + b2[e]
                out = out + combine[:, e:e + 1] * y
            return out
        key = jax.random.key(seed)
        ks = jax.random.split(key, 4)
        scale = 1.0 / np.sqrt(D).astype(np.float32)
        return {'input_embeddings': jax.random.normal(ks[0], (B, S, D), jnp.float32), 'router_w': jax.random.normal(ks[1], (NUM_EXPERTS, D), jnp.float32) * scale, 'w1': jax.random.normal(ks[2], (NUM_EXPERTS, D, D), jnp.float32) * scale, 'b1': jnp.zeros((NUM_EXPERTS, D), jnp.float32), 'w2': jax.random.normal(ks[3], (NUM_EXPERTS, D, D), jnp.float32) * scale, 'b2': jnp.zeros((NUM_EXPERTS, D), jnp.float32)}
    _L0_ffn_all = _L0_ffn_setup()
    _L0_ffn_in = {k: v for k, v in _L0_ffn_all.items() if k in ('router_w', 'w1', 'b1', 'w2', 'b2')}
    del _L0_ffn_all

    def _L1_gnn_setup():
        import jax, jax.numpy as jnp
        import numpy as np
        N_NODES = 1250
        N_EDGES = 20000
        NUM_RELS = 16
        IN_FEAT = 256
        OUT_FEAT = 256
        key = jax.random.key(seed)
        k_h, k_w, k_n, k_s, k_d, k_r = jax.random.split(key, 6)
        h = jax.random.normal(k_h, (N_NODES, IN_FEAT), dtype=jnp.float32)
        weight = jax.random.normal(k_w, (NUM_RELS, IN_FEAT, OUT_FEAT), dtype=jnp.float32)
        norm = jax.random.uniform(k_n, (N_EDGES, 1), dtype=jnp.float32)
        src = jax.random.randint(k_s, (N_EDGES,), 0, N_NODES, dtype=jnp.int32)
        dst = jax.random.randint(k_d, (N_EDGES,), 0, N_NODES, dtype=jnp.int32)
        rel_type = jax.random.randint(k_r, (N_EDGES,), 0, NUM_RELS, dtype=jnp.int32)
        return {'h': h, 'weight': weight, 'norm': norm, 'src': src, 'dst': dst, 'rel_type': rel_type}
    _L1_gnn_all = _L1_gnn_setup()
    _L1_gnn_in = {k: v for k, v in _L1_gnn_all.items() if k in ('weight',)}
    del _L1_gnn_all

    def _L1_mix_setup():
        import jax, jax.numpy as jnp
        import numpy as np
        NUM_HEADS = 8
        key = jax.random.key(seed)
        ks = jax.random.split(key, 5)
        B, N, C = (8, 1024, 256)
        x = jax.random.normal(ks[0], (B, N, C), dtype=jnp.float32)
        Wq = jax.random.normal(ks[1], (C, C), dtype=jnp.float32) * 0.02
        Wkv = jax.random.normal(ks[2], (2 * C, C), dtype=jnp.float32) * 0.02
        Wproj = jax.random.normal(ks[3], (C, C), dtype=jnp.float32) * 0.02
        bproj = jnp.zeros((C,), dtype=jnp.float32)
        return {'x': x, 'Wq': Wq, 'Wkv': Wkv, 'Wproj': Wproj, 'bproj': bproj}
    _L1_mix_all = _L1_mix_setup()
    _L1_mix_in = {k: v for k, v in _L1_mix_all.items() if k in ('Wq', 'Wkv', 'Wproj', 'bproj')}
    del _L1_mix_all

    def _L1_ffn_setup():
        import jax, jax.numpy as jnp
        import numpy as np
        B, N, D = (16, 256, 256)
        NUM_EXPERTS, TOP_K, HEADS = (4, 2, 4)
        N_EDGES = 65536
        LN_EPS = 1e-05

        def _layernorm(x, g, b):
            mu = x.mean(-1, keepdims=True)
            var = ((x - mu) ** 2).mean(-1, keepdims=True)
            return (x - mu) * jax.lax.rsqrt(var + LN_EPS) * g + b

        def _forward(x, edge_index, W_gat, att_src, att_dst, b_gat, ln_gamma, ln_beta, W1, b1, W2, b2):
            Bc, Nc, Dc = x.shape
            M = Bc * Nc
            x_flat = x.reshape(M, Dc)
            h = (x_flat @ W_gat).reshape(M, HEADS, NUM_EXPERTS)
            loops = jnp.arange(M, dtype=edge_index.dtype)
            src = jnp.concatenate([edge_index[0], loops])
            dst = jnp.concatenate([edge_index[1], loops])
            a_src = (h * att_src).sum(-1)
            a_dst = (h * att_dst).sum(-1)
            e = jax.nn.leaky_relu(a_src[src] + a_dst[dst], negative_slope=0.2)
            e_max = jax.ops.segment_max(e, dst, num_segments=M)
            ee = jnp.exp(e - e_max[dst])
            denom = jax.ops.segment_sum(ee, dst, num_segments=M)
            alpha = ee / (denom[dst] + 1e-16)
            msg = h[src] * alpha[:, :, None]
            agg = jax.ops.segment_sum(msg, dst, num_segments=M).reshape(M, HEADS * NUM_EXPERTS) + b_gat
            scores = _layernorm(agg, ln_gamma, ln_beta).reshape(M, HEADS, NUM_EXPERTS).mean(1)
            scores = scores.reshape(Bc, Nc, NUM_EXPERTS)
            topk_s, topk_i = jax.lax.top_k(scores, TOP_K)
            w = jax.nn.softmax(topk_s, axis=-1)
            out = jnp.zeros_like(x)
            for ei in range(NUM_EXPERTS):
                g = jnp.where(topk_i == ei, w, 0.0).sum(-1)
                hh = jax.nn.gelu(x @ W1[ei] + b1[ei], approximate=False)
                out = out + g[..., None] * (hh @ W2[ei] + b2[ei])
            return out
        key = jax.random.key(seed)
        ks = jax.random.split(key, 8)
        s = 0.05
        return {'x': jax.random.normal(ks[0], (B, N, D), jnp.float32), 'W_gat': jax.random.normal(ks[1], (D, HEADS * NUM_EXPERTS), jnp.float32) * s, 'att_src': jax.random.normal(ks[2], (HEADS, NUM_EXPERTS), jnp.float32) * s, 'att_dst': jax.random.normal(ks[3], (HEADS, NUM_EXPERTS), jnp.float32) * s, 'b_gat': jnp.zeros((HEADS * NUM_EXPERTS,), jnp.float32), 'ln_gamma': jnp.ones((HEADS * NUM_EXPERTS,), jnp.float32), 'ln_beta': jnp.zeros((HEADS * NUM_EXPERTS,), jnp.float32), 'W1': jax.random.normal(ks[4], (NUM_EXPERTS, D, 2 * D), jnp.float32) * s, 'b1': jnp.zeros((NUM_EXPERTS, 2 * D), jnp.float32), 'W2': jax.random.normal(ks[5], (NUM_EXPERTS, 2 * D, D), jnp.float32) * s, 'b2': jnp.zeros((NUM_EXPERTS, D), jnp.float32), 'edge_index': jax.random.randint(ks[6], (2, N_EDGES), 0, B * N, jnp.int32)}
    _L1_ffn_all = _L1_ffn_setup()
    _L1_ffn_in = {k: v for k, v in _L1_ffn_all.items() if k in ('W_gat', 'att_src', 'att_dst', 'b_gat', 'ln_gamma', 'ln_beta', 'W1', 'b1', 'W2', 'b2', 'edge_index')}
    del _L1_ffn_all
    return {'x': x, 'src': src, 'dst': dst, 'edge_attr_64': edge_attr_64, 'edge_type_16': edge_type_16, 'edge_weight1': edge_weight1, 'L0_gnn_W1': _L0_gnn_in['W1'], 'L0_gnn_b1': _L0_gnn_in['b1'], 'L0_gnn_W2': _L0_gnn_in['W2'], 'L0_gnn_b2': _L0_gnn_in['b2'], 'L0_gnn_Wg': _L0_gnn_in['Wg'], 'L0_gnn_bg': _L0_gnn_in['bg'], 'L0_gnn_gamma': _L0_gnn_in['gamma'], 'L0_gnn_beta': _L0_gnn_in['beta'], 'L0_mix_W_qk': _L0_mix_in['W_qk'], 'L0_mix_b_qk': _L0_mix_in['b_qk'], 'L0_mix_W_v': _L0_mix_in['W_v'], 'L0_mix_b_v': _L0_mix_in['b_v'], 'L0_mix_gamma': _L0_mix_in['gamma'], 'L0_mix_beta': _L0_mix_in['beta'], 'L0_ffn_router_w': _L0_ffn_in['router_w'], 'L0_ffn_w1': _L0_ffn_in['w1'], 'L0_ffn_b1': _L0_ffn_in['b1'], 'L0_ffn_w2': _L0_ffn_in['w2'], 'L0_ffn_b2': _L0_ffn_in['b2'], 'L1_gnn_weight': _L1_gnn_in['weight'], 'L1_mix_Wq': _L1_mix_in['Wq'], 'L1_mix_Wkv': _L1_mix_in['Wkv'], 'L1_mix_Wproj': _L1_mix_in['Wproj'], 'L1_mix_bproj': _L1_mix_in['bproj'], 'L1_ffn_W_gat': _L1_ffn_in['W_gat'], 'L1_ffn_att_src': _L1_ffn_in['att_src'], 'L1_ffn_att_dst': _L1_ffn_in['att_dst'], 'L1_ffn_b_gat': _L1_ffn_in['b_gat'], 'L1_ffn_ln_gamma': _L1_ffn_in['ln_gamma'], 'L1_ffn_ln_beta': _L1_ffn_in['ln_beta'], 'L1_ffn_W1': _L1_ffn_in['W1'], 'L1_ffn_b1': _L1_ffn_in['b1'], 'L1_ffn_W2': _L1_ffn_in['W2'], 'L1_ffn_b2': _L1_ffn_in['b2'], 'L1_ffn_edge_index': _L1_ffn_in['edge_index']}

def reference(x, src, dst, edge_attr_64, edge_type_16, edge_weight1, L0_gnn_W1, L0_gnn_b1, L0_gnn_W2, L0_gnn_b2, L0_gnn_Wg, L0_gnn_bg, L0_gnn_gamma, L0_gnn_beta, L0_mix_W_qk, L0_mix_b_qk, L0_mix_W_v, L0_mix_b_v, L0_mix_gamma, L0_mix_beta, L0_ffn_router_w, L0_ffn_w1, L0_ffn_b1, L0_ffn_w2, L0_ffn_b2, L1_gnn_weight, L1_mix_Wq, L1_mix_Wkv, L1_mix_Wproj, L1_mix_bproj, L1_ffn_W_gat, L1_ffn_att_src, L1_ffn_att_dst, L1_ffn_b_gat, L1_ffn_ln_gamma, L1_ffn_ln_beta, L1_ffn_W1, L1_ffn_b1, L1_ffn_W2, L1_ffn_b2, L1_ffn_edge_index):
    import jax
    import jax.numpy as jnp

    def _L0_gnn_ref(x, edge_index, edge_attr, W1, b1, W2, b2, Wg, bg, gamma, beta):
        import jax, jax.numpy as jnp
        import numpy as np
        N, E, H, DE = (625, 15625, 256, 64)
        EPS = 1e-05

        def _lin_init(k, fan_in, shape):
            s = 1.0 / np.sqrt(fan_in)
            return jax.random.uniform(k, shape, jnp.float32, -s, s)
        src, dst = (edge_index[0], edge_index[1])
        ei = jnp.concatenate([x[src], edge_attr], axis=-1)
        core = jnp.maximum(ei @ W1 + b1, 0.0) @ W2 + b2
        gate = jax.nn.sigmoid(ei @ Wg + bg)
        msg = gate * core
        agg = jax.ops.segment_sum(msg, dst, num_segments=x.shape[0])
        out = agg + x
        mu = jnp.mean(out, axis=-1, keepdims=True)
        var = jnp.var(out, axis=-1, keepdims=True)
        out = (out - mu) * jax.lax.rsqrt(var + EPS) * gamma + beta
        return out

    def _L0_mix_ref(feature, W_qk, b_qk, W_v, b_v, gamma, beta):
        import jax, jax.numpy as jnp
        import numpy as np
        BN_EPS = 1e-05
        QK = jnp.einsum('bnd,kde->bkne', feature, W_qk) + b_qk[None, :, None, :]
        value = jnp.einsum('bnd,de->bne', feature, W_v) + b_v
        query = QK[:, 0]
        key = QK[:, 1]
        sm = jax.nn.softmax(key, axis=1)
        lam = jnp.einsum('bnd,bne->bde', sm, value)
        mean = jnp.mean(lam, axis=(0, 2), keepdims=True)
        var = jnp.var(lam, axis=(0, 2), keepdims=True)
        bn = (lam - mean) * jax.lax.rsqrt(var + BN_EPS)
        bn = bn * gamma[None, :, None] + beta[None, :, None]
        return jnp.einsum('bnd,bde->bne', query, bn)

    def _L0_ffn_ref(input_embeddings, router_w, w1, b1, w2, b2):
        import jax, jax.numpy as jnp
        import numpy as np
        NUM_EXPERTS = 8
        TOP_K = 2
        B, S, D = (8, 512, 256)

        def _moe(tokens, router_w, w1, b1, w2, b2):
            N = tokens.shape[0]
            E = router_w.shape[0]
            logits = tokens.astype(jnp.float32) @ router_w.astype(jnp.float32).T
            probs = jax.nn.softmax(logits, axis=-1)
            rw, re = jax.lax.top_k(probs, TOP_K)
            if TOP_K > 1:
                rw = rw / jnp.maximum(rw.sum(-1, keepdims=True), 1e-12)
            rw = rw.astype(tokens.dtype)
            combine = jnp.zeros((N, E), tokens.dtype).at[jnp.arange(N)[:, None], re].set(rw)
            out = tokens
            for e in range(E):
                h = jax.nn.gelu(tokens @ w1[e] + b1[e], approximate=False)
                y = h @ w2[e] + b2[e]
                out = out + combine[:, e:e + 1] * y
            return out
        b, s, d = input_embeddings.shape
        tokens = input_embeddings.reshape(b * s, d)
        return _moe(tokens, router_w, w1, b1, w2, b2).reshape(b, s, d)

    def _L1_gnn_ref(h, weight, norm, src, dst, rel_type):
        import jax, jax.numpy as jnp
        import numpy as np
        N_NODES = 1250
        N_EDGES = 20000
        NUM_RELS = 16
        IN_FEAT = 256
        OUT_FEAT = 256
        transformed = jnp.einsum('ni,rio->rno', h, weight)
        msg = transformed[rel_type, src] * norm
        out = jax.ops.segment_sum(msg, dst, num_segments=h.shape[0])
        return out

    def _L1_mix_ref(x, Wq, Wkv, Wproj, bproj):
        import jax, jax.numpy as jnp
        import numpy as np
        NUM_HEADS = 8
        B, N, C = x.shape
        h = NUM_HEADS
        d = C // h
        q = jnp.einsum('bnc,oc->bno', x, Wq).reshape(B, N, h, d).transpose(0, 2, 1, 3)
        kv = jnp.einsum('bnc,oc->bno', x, Wkv).reshape(B, N, 2, h, d)
        k = kv[:, :, 0].transpose(0, 2, 1, 3)
        v = kv[:, :, 1].transpose(0, 2, 1, 3)
        q = jax.nn.elu(q) + 1.0
        k = jax.nn.elu(k) + 1.0
        k_sum = k.sum(axis=2)
        D_inv = 1.0 / jnp.maximum(jnp.einsum('bhnd,bhd->bhn', q, k_sum), 1e-06)
        context = jnp.einsum('bhnd,bhne->bhde', k, v)
        attn = jnp.einsum('bhnd,bhde->bhne', q, context) * D_inv[..., None]
        out = attn.transpose(0, 2, 1, 3).reshape(B, N, C)
        out = jnp.einsum('bnc,oc->bno', out, Wproj) + bproj
        return out

    def _L1_ffn_ref(x, W_gat, att_src, att_dst, b_gat, ln_gamma, ln_beta, W1, b1, W2, b2, edge_index):
        import jax, jax.numpy as jnp
        import numpy as np
        B, N, D = (16, 256, 256)
        NUM_EXPERTS, TOP_K, HEADS = (4, 2, 4)
        N_EDGES = 65536
        LN_EPS = 1e-05

        def _layernorm(x, g, b):
            mu = x.mean(-1, keepdims=True)
            var = ((x - mu) ** 2).mean(-1, keepdims=True)
            return (x - mu) * jax.lax.rsqrt(var + LN_EPS) * g + b

        def _forward(x, edge_index, W_gat, att_src, att_dst, b_gat, ln_gamma, ln_beta, W1, b1, W2, b2):
            Bc, Nc, Dc = x.shape
            M = Bc * Nc
            x_flat = x.reshape(M, Dc)
            h = (x_flat @ W_gat).reshape(M, HEADS, NUM_EXPERTS)
            loops = jnp.arange(M, dtype=edge_index.dtype)
            src = jnp.concatenate([edge_index[0], loops])
            dst = jnp.concatenate([edge_index[1], loops])
            a_src = (h * att_src).sum(-1)
            a_dst = (h * att_dst).sum(-1)
            e = jax.nn.leaky_relu(a_src[src] + a_dst[dst], negative_slope=0.2)
            e_max = jax.ops.segment_max(e, dst, num_segments=M)
            ee = jnp.exp(e - e_max[dst])
            denom = jax.ops.segment_sum(ee, dst, num_segments=M)
            alpha = ee / (denom[dst] + 1e-16)
            msg = h[src] * alpha[:, :, None]
            agg = jax.ops.segment_sum(msg, dst, num_segments=M).reshape(M, HEADS * NUM_EXPERTS) + b_gat
            scores = _layernorm(agg, ln_gamma, ln_beta).reshape(M, HEADS, NUM_EXPERTS).mean(1)
            scores = scores.reshape(Bc, Nc, NUM_EXPERTS)
            topk_s, topk_i = jax.lax.top_k(scores, TOP_K)
            w = jax.nn.softmax(topk_s, axis=-1)
            out = jnp.zeros_like(x)
            for ei in range(NUM_EXPERTS):
                g = jnp.where(topk_i == ei, w, 0.0).sum(-1)
                hh = jax.nn.gelu(x @ W1[ei] + b1[ei], approximate=False)
                out = out + g[..., None] * (hh @ W2[ei] + b2[ei])
            return out
        return _forward(x, edge_index, W_gat, att_src, att_dst, b_gat, ln_gamma, ln_beta, W1, b1, W2, b2)
    edge_index = jnp.stack([src, dst])
    xn = _layernorm(x, axis=-1)
    x = x + _L0_gnn_ref(xn, edge_index, edge_attr_64, L0_gnn_W1, L0_gnn_b1, L0_gnn_W2, L0_gnn_b2, L0_gnn_Wg, L0_gnn_bg, L0_gnn_gamma, L0_gnn_beta) + _L0_mix_ref(xn[None], L0_mix_W_qk, L0_mix_b_qk, L0_mix_W_v, L0_mix_b_v, L0_mix_gamma, L0_mix_beta)[0]
    x = x + _L0_ffn_ref(_layernorm(x, axis=-1)[None], L0_ffn_router_w, L0_ffn_w1, L0_ffn_b1, L0_ffn_w2, L0_ffn_b2)[0]
    xn = _layernorm(x, axis=-1)
    x = x + _L1_gnn_ref(xn, L1_gnn_weight, edge_weight1, src, dst, edge_type_16) + _L1_mix_ref(xn[None], L1_mix_Wq, L1_mix_Wkv, L1_mix_Wproj, L1_mix_bproj)[0]
    x = x + _L1_ffn_ref(_layernorm(x, axis=-1)[None], L1_ffn_W_gat, L1_ffn_att_src, L1_ffn_att_dst, L1_ffn_b_gat, L1_ffn_ln_gamma, L1_ffn_ln_beta, L1_ffn_W1, L1_ffn_b1, L1_ffn_W2, L1_ffn_b2, L1_ffn_edge_index)[0]
    return x

_drawn_inputs = setup_inputs


def setup_inputs(seed=0):
    import zlib

    import numpy as np

    out = dict(_drawn_inputs(seed))
    spreads = {'L0_gnn_gamma': (1.0, 0.576),
     'L0_gnn_beta': (0.0, 0.524),
     'L0_mix_b_qk': (0.0, 0.1),
     'L0_mix_b_v': (0.0, 0.1),
     'L0_mix_gamma': (1.0, 0.2),
     'L0_mix_beta': (0.0, 0.311),
     'L0_ffn_b1': (0.0, 0.8),
     'L0_ffn_b2': (0.0, 0.8),
     'L1_mix_bproj': (0.0, 0.8),
     'L1_ffn_b_gat': (0.0, 0.8),
     'L1_ffn_ln_gamma': (1.0, 0.6),
     'L1_ffn_ln_beta': (0.0, 0.8),
     'L1_ffn_b1': (0.0, 0.8),
     'L1_ffn_b2': (0.0, 2.0)}
    factors = {'edge_attr_64': 6.858,
     'L0_gnn_W1': 3.509,
     'L0_gnn_b1': 33.817,
     'L0_gnn_Wg': 8.0,
     'L0_gnn_bg': 50.458,
     'L1_mix_Wq': 8.0,
     'L1_mix_Wkv': 8.0,
     'L1_mix_Wproj': 8.0,
     'L1_ffn_W_gat': 8.0,
     'L1_ffn_att_src': 8.0,
     'L1_ffn_att_dst': 8.0,
     'L1_ffn_W1': 8.0,
     'L1_ffn_W2': 7.772,
     'L0_gnn_b2': 8.0}
    for name, (base, spread) in spreads.items():
        noise = np.random.default_rng([zlib.crc32(name.encode()), seed]).standard_normal(out[name].shape)
        drawn = base * np.exp(spread * noise) if base else spread * noise
        out[name] = jnp.asarray(drawn.astype(out[name].dtype))
    for name, factor in factors.items():
        out[name] = (out[name] * factor).astype(out[name].dtype)
    return out
```

```python
import concourse.bass as bass
from concourse import mybir
from contextlib import ExitStack

F32, F32R, I32 = mybir.dt.float32, mybir.dt.float32r, mybir.dt.int32
ALU, ACT = mybir.AluOpType, mybir.ActivationFunctionType
AX = mybir.AxisListType

NODES, D, EDGES, DE = 3125, 256, 100000, 64
TP = 125
NT = NODES // TP
GROUP = 5
KB = D // 128
HALVES = ((0, 313), (313, 312))
GC = GROUP * TP
ET = 128
SUP = 4
ES = ET * SUP
NSUP = -(-EDGES // ES)
NET = NSUP * SUP
RELS, HEADS, HD = 16, 8, 32
WIN = 64
FAR_WIN = 512
PASSES = 1 - -(NODES - WIN) // FAR_WIN
WRAP = WIN + (PASSES - 1) * FAR_WIN
AGGW = 2 * WRAP
E0, E1 = 8, 4
F1 = 2 * D
GE, GSUP = 65536, 65536 // (128 * 4)
GH = 4
EPS = 1e-5
HUGE = 1e30
SPAN = 60.0


class Chain:

    def __init__(self, eng, sem, base=0):
        self.eng, self.sem, self.base, self.n = eng, sem, base, 0

    def __call__(self, ins):
        self.n += 1
        ins.then_inc(self.sem, 1)
        self.eng.wait_ge(self.sem, self.base + self.n)


def bc(ap, dim, n):
    a = ap.unsqueeze(dim)
    shape = list(a.shape)
    shape[dim] = n
    return a.broadcast_to(shape)


def blocks(ap):
    return ap.rearrange("(b p) n -> p b n", p=128)


class Core:

    def __init__(self, nc, ctx, ins, out):
        self.nc, self.ctx, self.i, self.out = nc, ctx, ins, out
        self.live = []
        self.X = self.sb("X", [TP, NT, D])
        self.C = self.sb("C", [TP, NT, D])
        self.CT = self.sb("CT", [128, KB, NODES])
        self.big = self.sb("big", [128, 21504])
        self.ident = self.sb("ident", [128, 128])
        self.same_head = self.sb("same_head", [128, 128])
        self.mix = self.sb("mix", [128, KB, D])
        self.mix_c = self.sb("mix_c", [128, D])
        self.ones = self.sb("ones", [128, 128])
        self.iota = self.sb("iota", [128, 128])
        self.gate = self.sb("gate", [TP, NT, 16])
        self.eps = self.sb("eps", [128, 1])
        self.agg = self.big[:, 0:KB * AGGW].rearrange("p (b n) -> p b n", b=KB)
        self.kv = self.big[0:TP, 0:NT * 514].rearrange("p (t n) -> p t n", t=NT)
        self.sq = self.big[0:TP, 0:NT * D].rearrange("p (t n) -> p t n", t=NT)
        self.wt = self.big[:, 12864:12864 + 8192].rearrange("p (b n) -> p b n", b=KB)
        self.ready = nc.alloc_semaphore("constants_ready")
        self.psum = ctx.enter_context(nc.psum_tensor("psum", [128, 8, 512], F32))
        self.ps = [self.psum[:, i, :] for i in range(8)]
        self.table0 = nc.dram_tensor("table0", (NODES, 2 * D), F32, kind="Internal").ap()
        self.table1 = nc.dram_tensor("table1", (NODES * RELS, D), F32, kind="Internal").ap()
        self.gsrc = nc.dram_tensor("gsrc", (NODES, 20), F32, kind="Internal").ap()
        self.gdst = nc.dram_tensor("gdst", (NODES, 8), F32, kind="Internal").ap()

    def sb(self, name, shape, dt=F32, ctx=None):
        return (ctx or self.ctx).enter_context(self.nc.sbuf_tensor(name, shape, dt))

    def sem(self, name):
        self.live.append(self.nc.alloc_semaphore(name))
        return self.live[-1]

    def retire(self):
        self.nc.clear_and_free_semaphores(self.live)
        self.live = []
        self.nc.all_engine_barrier()

    def fence(self, eng):
        eng.wait_ge(self.ready, 1)


def stage_constants(c):
    nc = c.nc
    made, x_in = c.sem("const_steps"), c.sem("x_loaded")
    with nc.Block() as block:
        @block.sync
        def _(sp):
            sp.dma_start(c.X[:, :, :], c.i["x"].rearrange("(t p) d -> p t d", p=TP)).then_inc(x_in, 16)
            sp.wait_ge(x_in, 16)

        @block.gpsimd
        def _(pool):
            step = Chain(pool, made)
            step(pool.memset(c.ident[:, :], 0.0))
            step(pool.affine_select(out=c.ident[:, :], in_=c.ident[:, :], compare_op=ALU.not_equal, fill=1.0,
                                    base=0, pattern=[[-1, 128]], channel_multiplier=1))
            step(pool.memset(c.ones[:, :], 1.0))
            step(pool.memset(c.eps[:, :], EPS))
            step(pool.iota(c.iota[:, :], pattern=[[1, 128]], base=0, channel_multiplier=0,
                           allow_small_or_imprecise_dtypes=True))
            step(pool.memset(c.same_head[:, :], 0.0))
            for h in range(128 // HD):
                step(pool.memset(c.same_head[h * HD:(h + 1) * HD, h * HD:(h + 1) * HD], 1.0))
            pool.sem_inc(c.ready, 1)


def stage_norm(c, tag, groups):
    nc = c.nc
    ctx = ExitStack()
    with ctx:
        mean = c.sb(tag + "mean", [TP, NT], ctx=ctx)
        var = c.sb(tag + "var", [TP, NT], ctx=ctx)
        std = c.sb(tag + "std", [TP, NT], ctx=ctx)
        rstd = c.sb(tag + "rstd", [TP, NT], ctx=ctx)
        stage = c.sb(tag + "stage", [TP, GROUP, D], ctx=ctx)
        stage_t = c.sb(tag + "stageT", [128, GROUP, KB, TP], ctx=ctx)
        dram = [g for g in groups if g["out"] is None]
        width = sum(g["n"] for g in dram)
        table = c.table0 if width == 512 else c.table1.rearrange("(n r) d -> n (r d)", r=RELS)
        rows = c.sb(tag + "rows", [TP, 2, max(width // 2, 1)], ctx=ctx)
        loads = [(g["w"], g["w_in"]) for g in groups] + [(g["bias"], g["bias_in"]) for g in groups if g["bias"] is not None]
        n_act = sum(g["bias"] is None and i % 2 == 0 for i, g in enumerate(groups))
        n_dve = len(groups) - n_act
        who, seen = [], [0, 0]
        for i, g in enumerate(groups):
            e = 0 if g["bias"] is None and i % 2 == 0 else 1
            seen[e] += 1
            who.append((e, seen[e]))
        w_in, dve_step = c.sem(tag + "w_in"), c.sem(tag + "dve_step")
        var_ready, std_ready, c_ready = c.sem(tag + "var"), c.sem(tag + "std"), c.sem(tag + "c_ready")
        staged = c.sem(tag + "staged")
        turned, unturned = c.sem(tag + "turned"), c.sem(tag + "unturned")
        t_ready = c.sem(tag + "t_ready")
        prod, ev = c.sem(tag + "prod"), [c.sem(tag + "ev_act"), c.sem(tag + "ev_dve")]
        stored, rows_free = ([c.sem(f"{tag}{n}{h}") for h in range(2)] for n in ("stored", "rows_free"))
        nev = (n_act, n_dve)
        begun = c.sem(tag + "begun_storing")
        banks = 7

        def evac(eng, k, u, mine):
            t = k * GROUP + u
            col = 0
            for i, g in enumerate(groups):
                n = g["n"]
                if who[i][0] == mine:
                    eng.wait_ge(prod, (t + GROUP) * len(groups) + i + 1)
                    src = c.ps[1 + i % banks][0:TP, 0:n]
                    if g["out"] is None:
                        h, off = divmod(col, max(width // 2, 1))
                        if width > 512:
                            eng.wait_ge(rows_free[h], t + 1)
                            dst = rows[:, h, off:off + n]
                        else:
                            eng.wait_ge(rows_free[0], t + 1)
                            dst = rows[:, :, :].rearrange("p a b -> p (a b)")
                    else:
                        dst = g["out"][:, bass.ds(t, 1), 0:n].rearrange("p a n -> p (a n)")
                    c.fence(eng)
                    if mine == 0:
                        ins = eng.activation(dst, src, ACT.Copy)
                    elif g["bias"] is not None:
                        ins = eng.tensor_tensor(dst, src, g["bias"], ALU.add)
                    else:
                        ins = eng.tensor_copy(dst, src)
                    ins.then_inc(ev[mine], 1)
                if g["out"] is None:
                    col += n

        with nc.Block() as block:
            @block.sync
            def _(sp):
                for dst, src in loads:
                    sp.dma_start(dst, src).then_inc(w_in, 16)
                if dram:
                    for h in range(2 if width > 512 else 1):
                        sp.sem_inc(rows_free[h], 1)
                    with sp.Fori(0, NT) as t:
                        for h in range(2 if width > 512 else 1):
                            for e in range(2):
                                last = max([who[i][1] for i in range((len(dram) // 2) * (h + 1) if width > 512 else 1)
                                            if who[i][0] == e], default=0)
                                if last:
                                    sp.wait_ge(ev[e], t * nev[e] + nev[e] + last)
                                    sp.sem_inc(begun, 1)
                            if width > 512:
                                sp.dma_start(table[bass.ds(t * TP, TP), h * (width // 2):(h + 1) * (width // 2)],
                                             rows[:, h, :]).then_inc(stored[h], 16)
                            else:
                                sp.dma_start(table[bass.ds(t * TP, TP), :],
                                             rows[:, :, :].rearrange("p a b -> p (a b)")).then_inc(stored[0], 16)
                            sp.wait_ge(stored[h], 16 * t + 16)
                            sp.sem_inc(rows_free[h], 1)

            @block.vector
            def _(dve):
                dve.sem_inc(unturned, 1)
                if nev[1]:
                    dve.sem_inc(ev[1], nev[1])
                step = Chain(dve, dve_step)
                step(dve.tensor_reduce(mean[:, :], c.X[:, :, :], AX.X, ALU.add))
                step(dve.tensor_scalar(mean[:, :], mean[:, :], 1.0 / D, None, ALU.mult))
                step(dve.tensor_tensor(c.C[:, :, :], c.X[:, :, :], bc(mean[:, :], 2, D), ALU.subtract))
                step(dve.tensor_tensor(c.sq, c.C[:, :, :], c.C[:, :, :], ALU.mult))
                step(dve.tensor_reduce(var[:, :], c.sq, AX.X, ALU.add))
                dve.tensor_scalar(var[:, :], var[:, :], 1.0 / D, EPS, ALU.mult, ALU.add).then_inc(var_ready, 1)
                dve.wait_ge(std_ready, 1)
                step(dve.reciprocal(rstd[:, :], std[:, :]))
                dve.tensor_tensor(c.C[:, :, :], c.C[:, :, :], bc(rstd[:, :], 2, D), ALU.mult).then_inc(c_ready, 1)
                if loads:
                    dve.wait_ge(w_in, 16 * len(loads))
                with dve.Fori(0, NT // GROUP) as k:
                    for u in range(GROUP):
                        t = k * GROUP + u
                        psT = c.ps[0][:, 0:KB * TP].rearrange("p (b n) -> p b n", b=KB)
                        dve.wait_ge(turned, t + 1 + GROUP)
                        if groups:
                            dve.wait_ge(prod, (t + 1) * len(groups))
                            c.fence(dve)
                            dve.tensor_copy(stage_t[:, u, :, :], psT).then_inc(t_ready, 1)
                        dve.tensor_copy(c.CT[:, :, bass.ds(t * TP, TP)], psT).then_inc(unturned, 1)
                        evac(dve, k, u, 1)

            @block.scalar
            def _(act):
                if nev[0]:
                    act.sem_inc(ev[0], nev[0])
                act.wait_ge(var_ready, 1)
                act.activation(std[:, :], var[:, :], ACT.Sqrt).then_inc(std_ready, 1)
                act.wait_ge(c_ready, 1)
                with act.Fori(0, NT // GROUP) as k:
                    for u in range(GROUP):
                        t = k * GROUP + u
                        act.wait_ge(turned, t + 1)
                        c.fence(act)
                        act.activation(stage[:, u, :], c.C[:, bass.ds(t, 1), :].rearrange("p a d -> p (a d)"),
                                       ACT.Copy).then_inc(staged, 1)
                        evac(act, k, u, 0)

            @block.tensor
            def _(pe):
                pe.sem_inc(turned, GROUP)
                if groups:
                    pe.sem_inc(prod, GROUP * len(groups))
                if loads:
                    pe.wait_ge(w_in, 16 * len(loads))
                with pe.Fori(0, NT // GROUP) as k:
                    for u in range(GROUP):
                        t = k * GROUP + u
                        pe.wait_ge(staged, t + 1)
                        pe.wait_ge(unturned, t + 1)
                        for b in range(KB):
                            last = pe.transpose(c.ps[0][:, b * TP:(b + 1) * TP], stage[:, u, b * 128:(b + 1) * 128],
                                                c.ident[0:TP, 0:TP])
                        last.then_inc(turned, 1)
                        if groups:
                            pe.wait_ge(t_ready, t + 1)
                        for i, g in enumerate(groups):
                            if i >= banks:
                                e, n = who[i - banks]
                                pe.wait_ge(ev[e], t * nev[e] + nev[e] + n)
                            else:
                                e, n = who[max(j for j in range(len(groups)) if j % banks == i % banks)]
                                pe.wait_ge(ev[e], t * nev[e] + n)
                            for b in range(KB):
                                last = pe.matmul(c.ps[1 + i % banks][0:TP, 0:g["n"]], stage_t[:, u, b, :],
                                                 g["w"][:, b, :], start=(b == 0), stop=(b == KB - 1))
                            last.then_inc(prod, 1)


def stage_edges(c, tag, relational):
    nc = c.nc
    ctx = ExitStack()
    W = D if relational else 2 * D
    BODY = 2 * SUP
    NB = NET // BODY
    with ctx:
        def sb(name, shape, dt=F32):
            return c.sb(tag + name, shape, dt, ctx=ctx)

        base_i, base_f = sb("base_i", [128, NSUP], I32), sb("base_f", [128, NSUP])
        src_i, rel = sb("src_i", [128, NET], I32), sb("rel", [128, NET])
        dst_i, neg = sb("dst_i", [128, NET], I32), sb("neg", [128, NET])
        far, far_i, most = sb("far", [1, 1]), sb("far_i", [1, 1], I32), sb("most", [128, 1])
        idx = sb("idx", [128, 2, SUP], I32)
        G = c.big[:, KB * AGGW:KB * AGGW + 2 * SUP * W].rearrange("p (j q w) -> p j q w", j=2, q=SUP)
        near_hot = sb("near_hot", [128, 2, WIN])
        far_hot = c.big[:, KB * AGGW + 2 * SUP * 2 * D + 2 * ES:][:, 0:2 * FAR_WIN].rearrange("p (j n) -> p j n", j=2)

        wide_iota = c.big[:, KB * AGGW + 2 * SUP * 2 * D + 2 * ES + 2 * FAR_WIN:][:, 0:FAR_WIN]

        def window(s, j):
            if s is sems[0]:
                return WIN, near_hot, c.ps[6 + j].rearrange("p (b n) -> p b n", b=KB)[:, :, 0:WIN]
            return FAR_WIN, far_hot, c.psum[:, 6:6 + KB, 0:FAR_WIN]

        loads = [(base_i[:, :], c.i["dst_base"]), (src_i[:, :], c.i["src_t"]), (dst_i[:, :], c.i["dst_t"])]
        if relational:
            type_i, norm = sb("type_i", [128, NET], I32), sb("norm", [128, NET])
            loads += [(type_i[:, :], c.i["type_t"]), (norm[:, :], c.i["norm_t"])]
        else:
            wb_hi, wb_lo = sb("wb_hi", [128, W], F32R), sb("wb_lo", [128, W], F32R)
            w2_hi, w2_lo = sb("w2_hi", [128, KB, D], F32R), sb("w2_lo", [128, KB, D], F32R)
            b2_parts, two = sb("b2_parts", [128, D], F32R), sb("two", [128, 128], F32R)
            parts = sb("attr_parts", [128, 2, ES], F32R)
            attr = c.big[:, KB * AGGW + 2 * SUP * W:][:, 0:2 * ES].rearrange("p (j e) -> p j e", j=2)
            Z, gate = sb("Z", [128, 2, W]), sb("gate", [128, 2, D])
            hT_hi, hT_lo = sb("hT_hi", [128, 2, KB, 128], F32R), sb("hT_lo", [128, 2, KB, 128], F32R)
            msg = sb("msg", [128, 2, D])
            w2_in = Z[:, 0, :].rearrange("p (b n) -> p b n", b=KB)
            loads += [(Z[0:DE, 1, :], c.i["edge_w0"]), (Z[DE:2 * DE, 1, :], c.i["edge_w0"]), (w2_in, blocks(c.i["w2_0"])),
                      (gate[:, 0, :], c.i["b2_0"])]
        loaded, prep, maxed, turned, flag, zeroed, first_done, cut = (
            c.sem(tag + n) for n in ("loaded", "prep", "maxed", "max_turned", "flag", "zeroed", "first_done", "cut"))
        names = ("idx_ready", "G_in0", "G_in1", "hot_ready", "hot_used", "added", "attr_in0",
                 "attr_in1", "attr_rounded", "attr_ready", "z_ready", "zs_ready", "z_turned",
                 "h_rounded", "h_ready", "gate_ready", "core_ready", "msg_ready", "shifted")
        if relational:
            names = ("idx_ready", "G_in0", "G_in1", "hot_ready", "hot_used", "added", "shifted")
        sems = [{n: c.sem(f"{tag}{n}_{j}") for n in names} for j in range(2)]
        begun_adding, begun_gathering = c.sem(tag + "begun_adding"), c.sem(tag + "begun_gathering")
        table = c.table1 if relational else c.table0

        def loop(step):
            def whole(eng):
                for u in range(-3, BODY):
                    step(0, u)
                with eng.Fori(1, NB - 1) as k:
                    for u in range(BODY):
                        step(k, u)
                for u in range(BODY + 3):
                    step(NB - 1, u)
            return whole

        def at(k, u):
            k, u = k + u // BODY, u % BODY
            if isinstance(k, int) and not 0 <= k < NB:
                return None
            return k, u, k * BODY + u, k * 2 + u // SUP, u // SUP, u % SUP

        def sp_pass(sp, s, p):
            if not relational:
                with sp.Fori(0, NSUP // 2) as k:
                    for j in range(2):
                        sp.wait_ge(s["attr_ready"], p * NSUP + k * 2 + j + 1)
                        for half in range(2):
                            c.fence(sp)
                            sp.dma_start(attr[half * DE:(half + 1) * DE, j, :],
                                         c.i["attr_t"][:, bass.ds((k * 2 + j) * ES, ES)]).then_inc(s[f"attr_in{j}"], 16)

        def pool_pass(pool, s, p):
            with pool.Fori(0, NSUP // 2) as k:
                for j in range(2):
                    pool.wait_ge(s["idx_ready"], p * NSUP + k * 2 + j + 1)
                    if relational:
                        pool.wait_ge(s["added"], p * NSUP + k * 2 + j + 1)
                    else:
                        pool.wait_ge(s["zs_ready"], p * NET + (k * 2 + j) * SUP + SUP)
                    pool.sem_inc(begun_gathering, 1)
                    for q in range(SUP):
                        pool.indirect_dma_start(G[:, j, q, :], None, table,
                                                bass.IndirectOffsetOnAxis(idx[:, j, q:q + 1], 0)).then_inc(
                            s[f"G_in{j}"], 16)

        def pe_pass(pe, s, p):
            def edge_part(a):
                k, u, i, sp_, j, q = a
                if q == 0:
                    pe.wait_ge(s["attr_ready"], p * NSUP + sp_ + 3)
                pe.wait_ge(s["zs_ready"], p * NET + i + 2 * SUP - 1)
                tile = parts[:, j, q * ET:(q + 1) * ET]
                pe.matmul(c.ps[u % 2], tile, wb_hi[:, :], start=True, stop=False)
                pe.matmul(c.ps[u % 2], tile, wb_lo[:, :], start=False, stop=True).then_inc(s["z_ready"], 1)

            def turn(a):
                k, u, i, sp_, j, q = a
                pe.wait_ge(s["zs_ready"], p * NET + i + 2 * SUP + 1)
                pe.wait_ge(s["h_ready"], p * NET + i + 1)
                for b in range(KB):
                    last = pe.transpose(c.ps[2 + u % 2][:, b * 128:(b + 1) * 128], Z[:, u % 2, b * 128:(b + 1) * 128], c.ident[:, :])
                last.then_inc(s["z_turned"], 1)

            def core(a):
                k, u, i, sp_, j, q = a
                pe.wait_ge(s["h_ready"], p * NET + i + 3)
                pe.wait_ge(s["msg_ready"], p * NET + i + 1)
                pe.matmul(c.ps[4 + u % 2][:, 0:D], two[:, :], b2_parts[:, :], start=True, stop=False)
                for b in range(KB):
                    hi, lo = hT_hi[:, u % 2, b, :], hT_lo[:, u % 2, b, :]
                    for x, y in ((hi, w2_hi), (hi, w2_lo), (lo, w2_hi)):
                        last = pe.matmul(c.ps[4 + u % 2][:, 0:D], x, y[:, b, :], start=False, stop=b == KB - 1 and x is lo)
                last.then_inc(s["core_ready"], 1)

            def total(a):
                k, u, i, sp_, j, q = a
                pe.wait_ge(s["hot_ready"], p * NET + i + 1)
                if relational:
                    if q == 0:
                        pe.wait_ge(s[f"G_in{j}"], (p * (NSUP // 2) + k + 1) * 64)
                else:
                    pe.wait_ge(s["msg_ready"], p * NET + i + 3)
                if q == 0:
                    pe.wait_ge(s["added"], p * NSUP + sp_ + (1 if s is sems[0] else 2))
                _, onehot, acc = window(s, j)
                for b in range(KB):
                    lhs = G[:, j, q, b * 128:(b + 1) * 128] if relational else msg[:, u % 2, b * 128:(b + 1) * 128]
                    last = pe.matmul(acc[:, b, :], lhs, onehot[:, u % 2, :], start=q == 0 and (b == 0 or s is sems[1]),
                                     stop=q == SUP - 1, skip_group_check=True)
                last.then_inc(s["hot_used"], 1)

            def step(k, u):
                for ahead, part in ((1, turn), (-1 if relational else -2, total), (0, core), (3, edge_part)):
                    a = at(k, u + ahead)
                    if a and (part is total or not relational):
                        part(a)
            loop(step)(pe)

        def act_pass(act, s, p):
            def step(k, u):
                a = at(k, u + 1)
                if not a:
                    return
                k, u, i, sp_, j, q = a
                act.wait_ge(s["z_turned"], p * NET + i + 3)
                act.wait_ge(s["core_ready"], p * NET + i + 1)
                act.activation(hT_hi[:, u % 2, :, :].rearrange("p b n -> p (b n)"),
                               c.ps[2 + u % 2][:, 0:KB * 128], ACT.Relu).then_inc(s["h_rounded"], 1)
                act.wait_ge(s["zs_ready"], p * NET + i + 2 * SUP + 1)
                act.wait_ge(s["msg_ready"], p * NET + i + 1)
                act.activation(gate[:, u % 2, :], Z[:, u % 2, D:2 * D], ACT.Sigmoid).then_inc(s["gate_ready"], 1)
                if q == SUP - 1 and not (isinstance(k, int) and sp_ + 2 >= NSUP):
                    rounded(sp_ + 2, j, k + 1)

            def rounded(sup, j, k):
                act.wait_ge(s["z_ready"], p * NET + sup * SUP + SUP)
                act.wait_ge(s[f"attr_in{j}"], (p * (NSUP // 2) + k + 1) * 32)
                act.activation(parts[:, j, :], attr[:, j, :], ACT.Copy).then_inc(s["attr_rounded"], 1)
            if not relational:
                rounded(0, 0, 0)
                rounded(1, 1, 0)
                loop(step)(act)

        def dve_pass(dve, s, p):
            def indices(sup, j, uses):
                if relational and not (isinstance(uses, int) and uses == 0):
                    dve.wait_ge(s[f"G_in{j}"], (p * (NSUP // 2) + uses) * 64)
                c.fence(dve)
                dve.tensor_copy(idx[:, j, :], src_i[:, bass.ds(sup * SUP, SUP)]).then_inc(s["idx_ready"], 1)

            def whole_row(a):
                k, u, i, sp_, j, q = a
                dve.wait_ge(s["z_ready"], p * NET + i + 2 * SUP + 1)
                if q == 0:
                    dve.wait_ge(s[f"G_in{j}"], (p * (NSUP // 2) + k + 1) * 64)
                dve.wait_ge(s["z_turned"], p * NET + i + 1)
                dve.wait_ge(s["gate_ready"], p * NET + i + 1)
                dve.tensor_tensor(Z[:, u % 2, :], c.ps[u % 2], G[:, j, q, :], ALU.add).then_inc(s["zs_ready"], 1)
                if q == SUP - 1:
                    nxt = at(k, u + BODY)
                    if nxt and not (isinstance(k, int) and sp_ + 2 >= NSUP):
                        indices(sp_ + 2, j, k + 1)

            def attr_lo(sup, j):
                dve.wait_ge(s["attr_rounded"], p * NSUP + sup + 1)
                dve.tensor_tensor(parts[DE:2 * DE, j, :], attr[DE:2 * DE, j, :], parts[DE:2 * DE, j, :].bitcast(F32),
                                  ALU.subtract).then_inc(s["attr_ready"], 1)

            def hidden_lo(a):
                k, u, i, sp_, j, q = a
                dve.wait_ge(s["h_rounded"], p * NET + i + 1)
                dve.wait_ge(s["core_ready"], p * NET + i + 1)
                dve.scalar_tensor_tensor(out=hT_lo[:, u % 2, :, :].rearrange("p b n -> p (b n)"),
                                         in0=c.ps[2 + u % 2][:, 0:KB * 128], scalar=0.0,
                                         in1=hT_hi[:, u % 2, :, :].rearrange("p b n -> p (b n)").bitcast(F32),
                                         op0=ALU.max, op1=ALU.subtract).then_inc(s["h_ready"], 1)

            def hot(a):
                k, u, i, sp_, j, q = a
                dve.wait_ge(s["hot_used"], p * NET + i + 1)
                width, onehot, _ = window(s, j)
                c.fence(dve)
                if relational:
                    dve.tensor_scalar(onehot[:, u % 2, :], wide_iota[:, 0:width], rel[:, bass.ds(i, 1)],
                                      norm[:, bass.ds(i, 1)], ALU.is_equal, ALU.mult).then_inc(s["hot_ready"], 1)
                else:
                    dve.tensor_scalar(onehot[:, u % 2, :], wide_iota[:, 0:width], rel[:, bass.ds(i, 1)], None,
                                      ALU.is_equal).then_inc(s["hot_ready"], 1)

            def message(a):
                k, u, i, sp_, j, q = a
                dve.wait_ge(s["gate_ready"], p * NET + i + 3)
                dve.wait_ge(s["core_ready"], p * NET + i + 3)
                dve.wait_ge(s["hot_used"], p * NET + i + 1)
                dve.tensor_tensor(msg[:, u % 2, :], c.ps[4 + u % 2][:, 0:D], gate[:, u % 2, :], ALU.mult).then_inc(
                    s["msg_ready"], 1)

            def add_window(a):
                k, u, i, sp_, j, q = a
                dve.wait_ge(s["hot_used"], p * NET + i + 3)
                dve.wait_ge(s["added"], p * NSUP + sp_ + 2)
                dve.sem_inc(begun_adding, 1)
                at_node = dve.value_load(base_i[0:1, bass.ds(sp_, 1)], min_val=0, max_val=NODES - 1)
                width, _, acc = window(s, j)
                cols = c.agg[:, :, bass.ds(at_node + (0 if s is sems[0] else WIN + p * FAR_WIN), width)]
                c.fence(dve)
                dve.tensor_tensor(cols, cols, acc, ALU.add).then_inc(s["added"], 1)

            def step(k, u):
                if relational:
                    a = at(k, u)
                    if a:
                        hot(a)
                        if a[5] == 0 and not (isinstance(a[0], int) and a[3] + 1 >= NSUP):
                            indices(a[3] + 1, 1 - a[4], a[0] + a[4])
                else:
                    for ahead, part in ((-1, message), (2, whole_row), (-1, hot), (1, hidden_lo)):
                        a = at(k, u + ahead)
                        if a:
                            part(a)
                    a = at(k, u)
                    if a and a[5] == SUP - 1 and not (isinstance(a[0], int) and a[3] + 2 >= NSUP):
                        attr_lo(a[3] + 2, a[4])
                a = at(k, u - (2 if relational else 3))
                if a and a[5] == SUP - 1:
                    add_window(a)

            indices(0, 0, 0)
            if not relational:
                indices(1, 1, 0)
                attr_lo(0, 0)
                attr_lo(1, 1)
            loop(step)(dve)

        def both(eng, one):
            one(eng, sems[0], 0)
            eng.wait_ge(flag, 1)
            more = eng.value_load(far_i[0:1, 0:1], min_val=0, max_val=1)
            with eng.If(more > 0):
                eng.wait_ge(first_done, 1)
                with eng.Fori(0, PASSES - 1) as p:
                    one(eng, sems[1], p)

        with nc.Block() as block:
            @block.sync
            def _(sp):
                for dst, src in loads:
                    sp.dma_start(dst, src).then_inc(loaded, 16)
                both(sp, sp_pass)

            @block.gpsimd
            def _(pool):
                both(pool, pool_pass)

            @block.vector
            def _(dve):
                for s in sems:
                    dve.sem_inc(s["added"], 2)
                    if not relational:
                        dve.sem_inc(s["zs_ready"], 2 * SUP)
                        dve.sem_inc(s["msg_ready"], 2)
                        dve.sem_inc(s["h_ready"], 2)
                        dve.sem_inc(s["attr_ready"], 2)
                dve.memset(c.agg, 0.0).then_inc(zeroed, 1)
                dve.wait_ge(loaded, 16 * len(loads))
                do = Chain(dve, prep)
                for n in range(FAR_WIN // 128):
                    do(dve.tensor_scalar(wide_iota[:, n * 128:(n + 1) * 128], c.iota[:, :], float(n * 128), None, ALU.add))
                do(dve.tensor_copy(base_f[:, :], base_i[:, :]))
                do(dve.tensor_copy(rel[:, :], dst_i[:, :]))
                rel3 = rel[:, :].rearrange("p (s q) -> p s q", q=SUP)
                do(dve.tensor_tensor(rel3, rel3, bc(base_f[:, :], 2, SUP), ALU.subtract))
                do(dve.tensor_scalar(neg[:, :], rel[:, :], 0.0, float(WRAP), ALU.is_lt, ALU.mult))
                do(dve.tensor_tensor(rel[:, :], rel[:, :], neg[:, :], ALU.add))
                if relational:
                    do(dve.tensor_scalar(neg[:, :], src_i[:, :], float(RELS), None, ALU.mult))
                    do(dve.tensor_tensor(src_i[:, :], neg[:, :], type_i[:, :], ALU.add))
                else:
                    for hi, lo, w in ((wb_hi[:, :], wb_lo[:, :], Z[:, 1, :]), (w2_hi[:, :, :], w2_lo[:, :, :], w2_in)):
                        do(dve.tensor_copy(hi, w))
                        do(dve.tensor_tensor(lo, w, hi.bitcast(F32), ALU.subtract))
                    do(dve.tensor_copy(b2_parts[:, :], gate[:, 0, :]))
                    low = b2_parts[32:64, :]
                    do(dve.tensor_tensor(low, gate[32:64, 0, :], low.bitcast(F32), ALU.subtract))
                    do(dve.memset(two[:, :].bitcast(F32), 0.0))
                    for row in (0, 32):
                        do(dve.memset(two[row:row + 1, :].bitcast(F32), 1.0))
                    dve.sem_inc(cut, 1)
                dve.tensor_reduce(most[:, :], rel[:, :], AX.X, ALU.max).then_inc(maxed, 1)
                dve.wait_ge(turned, 1)
                do(dve.tensor_reduce(far[:, :], c.ps[7][0:1, 0:128], AX.X, ALU.max))
                do(dve.tensor_scalar(far[:, :], far[:, :], float(WIN), None, ALU.is_ge))
                dve.tensor_copy(far_i[:, :], far[:, :]).then_inc(flag, 1)
                dve.wait_ge(zeroed, 1)

                def one(dve, s, p):
                    dve_pass(dve, s, p)
                    dve.wait_ge(s["added"], (p + 1) * NSUP + 2)
                    if s is sems[0]:
                        dve.sem_inc(first_done, 1)
                    dve.tensor_scalar(rel[:, :], rel[:, :], -float(WIN if s is sems[0] else FAR_WIN), None,
                                      ALU.add).then_inc(s["shifted"], 1)
                    dve.wait_ge(s["shifted"], p + 1)
                both(dve, one)

            @block.scalar
            def _(act):
                if not relational:
                    for s in sems:
                        act.sem_inc(s["gate_ready"], 2)
                    act.wait_ge(cut, 1)
                both(act, act_pass)

            @block.tensor
            def _(pe):
                for s in sems:
                    pe.sem_inc(s["hot_used"], 2)
                    if not relational:
                        pe.sem_inc(s["z_ready"], 2 * SUP)
                        pe.sem_inc(s["z_turned"], 2)
                        pe.sem_inc(s["core_ready"], 2)
                pe.wait_ge(maxed, 1)
                pe.transpose(c.ps[7][0:1, 0:128], most[:, :], c.ident[:, :]).then_inc(turned, 1)
                pe.wait_ge(loaded, 16 * len(loads))
                if not relational:
                    pe.wait_ge(cut, 1)
                both(pe, pe_pass)


def stage_context(c, tag, softmax):
    nc = c.nc
    ctx = ExitStack()
    with ctx:
        def sb(name, shape, dt=F32):
            return c.sb(tag + name, shape, dt, ctx=ctx)

        stage = sb("stage", [TP, GROUP, D])
        k_top, top = sb("k_top", [TP, D]), sb("top", [128, KB])
        diag, top_all = sb("diag", [128, KB, 128]), sb("top_all", [TP, D])
        lam, lam_sq = sb("lam", [128, KB, D]), sb("lam_sq", [128, KB, D])
        st = sb("stats", [128, 8, KB])
        gb, wqT, bq = sb("gb", [128, 2, KB]), sb("wqT", [128, KB, D]), sb("bq", [128, KB, TP])
        K, V1 = c.kv[:, :, 0:D], c.kv[:, :, D:2 * D + 1]
        tmp = c.big[0:TP, 12864:12864 + NT * D].rearrange("p (t d) -> p t d", t=NT)
        loaded, do_dve = c.sem(tag + "loaded"), c.sem(tag + "dve_step")
        top_ready, turned, diag_ready, spread = (c.sem(tag + n) for n in ("top", "turned", "diag", "spread"))
        low_ready, exp_ready, k_ready = (c.sem(tag + n) for n in ("low", "exp", "k_ready"))
        staged, unstaged, summed = (c.sem(tag + n) for n in ("staged", "unstaged", "summed"))
        var_ready, std_ready, bn_ready, mixed = (c.sem(tag + n) for n in ("var", "std", "bn", "mixed"))

        with nc.Block() as block:
            @block.sync
            def _(sp):
                if softmax:
                    sp.dma_start(gb[:, 0, :], c.i["mix0_gamma"]).then_inc(loaded, 16)
                    sp.dma_start(gb[:, 1, :], c.i["mix0_beta"]).then_inc(loaded, 16)
                    sp.dma_start(wqT[:, :, :], blocks(c.i["wq0_t"])).then_inc(loaded, 16)
                    sp.dma_start(bq[:, :, :], blocks(c.i["bq0"])).then_inc(loaded, 16)

            @block.vector
            def _(dve):
                do = Chain(dve, do_dve)
                do(dve.memset(c.kv[:, :, 2 * D:2 * D + 2], 1.0))
                if softmax:
                    dve.tensor_reduce(k_top[:, :], K.rearrange("p t d -> p d t"), AX.X, ALU.max).then_inc(top_ready, 1)
                    dve.wait_ge(turned, 1)
                    do(dve.tensor_reduce(top[:, :], c.ps[0][:, 0:KB * TP].rearrange("p (b n) -> p b n", b=KB),
                                         AX.X, ALU.max))
                    for b in range(KB):
                        dve.tensor_scalar(diag[:, b, :], c.ident[:, :], top[:, b:b + 1], None,
                                          ALU.mult).then_inc(diag_ready, 1)
                    dve.wait_ge(spread, 1)
                    do(dve.tensor_copy(top_all[:, :], c.ps[1][0:TP, 0:D]))
                    dve.tensor_tensor(K, K, bc(top_all[:, :], 1, NT), ALU.subtract).then_inc(k_ready, 1)
                else:
                    dve.tensor_scalar(tmp, K, 0.0, None, ALU.min).then_inc(low_ready, 1)
                    dve.wait_ge(exp_ready, 1)
                    dve.scalar_tensor_tensor(out=K, in0=K, scalar=0.0, in1=tmp, op0=ALU.max,
                                             op1=ALU.add).then_inc(k_ready, 1)
                dve.wait_ge(summed, 1)
                sums = c.psum[:, 2:4, 0:D]
                if softmax:
                    dve.wait_ge(loaded, 64)
                    mean, var, std, rstd, sc, rs = (st[:, n, :] for n in range(6))
                    do(dve.reciprocal(rs, c.psum[:, 2:4, D:D + 1].rearrange("p b o -> p (b o)")))
                    do(dve.tensor_tensor(lam[:, :, :], sums, bc(rs, 2, D), ALU.mult))
                    do(dve.tensor_reduce(mean, lam[:, :, :], AX.X, ALU.add))
                    do(dve.tensor_scalar(mean, mean, 1.0 / D, None, ALU.mult))
                    do(dve.tensor_tensor(lam[:, :, :], lam[:, :, :], bc(mean, 2, D), ALU.subtract))
                    do(dve.tensor_tensor(lam_sq[:, :, :], lam[:, :, :], lam[:, :, :], ALU.mult))
                    do(dve.tensor_reduce(var, lam_sq[:, :, :], AX.X, ALU.add))
                    dve.tensor_scalar(var, var, 1.0 / D, EPS, ALU.mult, ALU.add).then_inc(var_ready, 1)
                    dve.wait_ge(std_ready, 1)
                    do(dve.reciprocal(rstd, std))
                    do(dve.tensor_tensor(sc, rstd, gb[:, 0, :], ALU.mult))
                    for b in range(KB):
                        dve.tensor_scalar(lam[:, b, :], lam[:, b, :], sc[:, b:b + 1], gb[:, 1, b:b + 1], ALU.mult,
                                          ALU.add).then_inc(bn_ready, 1)
                    dve.wait_ge(mixed, 1)
                    do(dve.tensor_copy(c.mix[:, :, :], c.psum[:, 4:6, 0:D]))
                    do(dve.tensor_copy(c.mix_c[0:TP, :], c.ps[6][0:TP, 0:D]))
                else:
                    for b in range(KB):
                        do(dve.tensor_tensor(c.mix[:, b, 0:128], c.psum[:, 2 + b, b * 128:(b + 1) * 128],
                                             c.same_head[:, :], ALU.mult))
                        do(dve.tensor_copy(st[:, b, 0:1], c.psum[:, 2 + b, D:D + 1]))
                        do(dve.tensor_scalar(c.mix[:, b, 128:256], c.same_head[:, :], st[:, b, 0:1], None, ALU.mult))

            @block.scalar
            def _(act):
                if not softmax:
                    act.wait_ge(low_ready, 1)
                    act.activation(tmp, tmp, ACT.Exp).then_inc(exp_ready, 1)
                act.wait_ge(k_ready, 1)
                with act.Fori(0, NT // GROUP) as k:
                    for u in range(GROUP):
                        t = k * GROUP + u
                        act.wait_ge(unstaged, t + 1)
                        c.fence(act)
                        act.activation(stage[:, u, :], c.kv[:, bass.ds(t, 1), 0:D].rearrange("p a d -> p (a d)"),
                                       ACT.Exp if softmax else ACT.Copy).then_inc(staged, 1)
                if softmax:
                    act.wait_ge(var_ready, 1)
                    act.activation(st[:, 2, :], st[:, 1, :], ACT.Sqrt).then_inc(std_ready, 1)

            @block.tensor
            def _(pe):
                pe.sem_inc(unstaged, GROUP)
                if softmax:
                    pe.wait_ge(top_ready, 1)
                    for b in range(KB):
                        last = pe.transpose(c.ps[0][:, b * TP:(b + 1) * TP], k_top[:, b * 128:(b + 1) * 128],
                                            c.ident[0:TP, 0:TP])
                    last.then_inc(turned, 1)
                    pe.wait_ge(diag_ready, KB)
                    for b in range(KB):
                        last = pe.matmul(c.ps[1][0:TP, b * 128:(b + 1) * 128], c.ones[:, 0:TP], diag[:, b, :],
                                         start=True, stop=True)
                    last.then_inc(spread, 1)
                pe.wait_ge(do_dve, 1)

                def group(k, first=False, final=False):
                    for u in range(GROUP):
                        t = k * GROUP + u
                        pe.wait_ge(staged, t + 1)
                        for b in range(KB):
                            last = pe.matmul(c.ps[2 + b][:, 0:D + 1], stage[:, u, b * 128:(b + 1) * 128],
                                             V1[:, bass.ds(t, 1), :].rearrange("p a n -> p (a n)"),
                                             start=first and u == 0, stop=final and u == GROUP - 1)
                        last.then_inc(unstaged, 1)
                group(0, first=True)
                with pe.Fori(1, NT // GROUP - 1) as k:
                    group(k)
                group(NT // GROUP - 1, final=True)
                pe.wait_ge(unstaged, NT + GROUP)
                pe.sem_inc(summed, 1)
                if softmax:
                    pe.wait_ge(bn_ready, KB)
                    pe.wait_ge(loaded, 64)
                    for kb in range(KB):
                        for b in range(KB):
                            pe.matmul(c.ps[4 + kb][:, 0:D], wqT[:, b, kb * 128:(kb + 1) * 128], lam[:, b, :],
                                      start=(b == 0), stop=(b == KB - 1))
                    for b in range(KB):
                        last = pe.matmul(c.ps[6][0:TP, 0:D], bq[:, b, :], lam[:, b, :], start=(b == 0),
                                         stop=(b == KB - 1))
                    last.then_inc(mixed, 1)


def stage_attend(c, tag):
    nc = c.nc
    ctx = ExitStack()
    N = HALVES[0][1]
    with ctx:
        def sb(name, shape, dt=F32):
            return c.sb(tag + name, shape, dt, ctx=ctx)

        wq, wp, bp = sb("wq", [128, KB, D]), sb("wp", [128, KB, D]), sb("bp", [128, KB])
        low, q = sb("low", [128, KB, N]), sb("q", [128, KB, N])
        inv, at = sb("inv", [128, KB, N]), sb("at", [128, KB, N])
        loaded = c.sem(tag + "loaded")
        q_in, low_ready, exp_ready, q_ready, ctx_ready, at_ready, out_ready, added, part = (
            c.sem(tag + n) for n in ("q_in", "low", "exp", "q_ready", "ctx", "at", "out", "added", "part"))

        def steps(k):
            for h, (h0, n) in enumerate(HALVES):
                yield k * 2 + h, k * GC + h0, n

        with nc.Block() as block:
            @block.sync
            def _(sp):
                sp.dma_start(wq[:, :, :], blocks(c.i["wq1_t"])).then_inc(loaded, 16)
                sp.dma_start(wp[:, :, :], blocks(c.i["wproj_t"])).then_inc(loaded, 16)
                sp.dma_start(bp[:, :], c.i["bproj"]).then_inc(loaded, 16)

            @block.tensor
            def _(pe):
                for sem in (ctx_ready, out_ready):
                    pe.sem_inc(sem, 1)
                pe.wait_ge(loaded, 48)
                with pe.Fori(0, NT // GROUP) as k:
                    for i, col, n in steps(k):
                        pe.wait_ge(q_ready, i + 1)
                        for b in range(KB):
                            for kb in range(KB):
                                last = pe.matmul(c.ps[b][:, 0:n], wq[:, kb, b * 128:(b + 1) * 128],
                                                 c.CT[:, kb, bass.ds(col, n)], start=(kb == 0), stop=(kb == KB - 1))
                        last.then_inc(q_in, 1)
                        pe.wait_ge(q_ready, i + 2)
                        pe.wait_ge(at_ready, i + 1)
                        for b in range(KB):
                            pe.matmul(c.ps[2 + b][:, 0:n], c.mix[:, b, 0:128], q[:, b, 0:n], start=True, stop=True)
                            last = pe.matmul(c.ps[4 + b][:, 0:n], c.mix[:, b, 128:256], q[:, b, 0:n], start=True, stop=True)
                        last.then_inc(ctx_ready, 1)
                        pe.wait_ge(at_ready, i + 2)
                        pe.wait_ge(added, i + 1)
                        for b in range(KB):
                            for kb in range(KB):
                                last = pe.matmul(c.ps[6 + b][:, 0:n], wp[:, kb, b * 128:(b + 1) * 128], at[:, kb, 0:n],
                                                 start=(kb == 0), stop=(kb == KB - 1))
                        last.then_inc(out_ready, 1)

            @block.scalar
            def _(act):
                with act.Fori(0, NT // GROUP) as k:
                    for i, col, n in steps(k):
                        act.wait_ge(low_ready, i + 1)
                        act.activation(low[:, :, 0:n], low[:, :, 0:n], ACT.Exp).then_inc(exp_ready, 1)

            @block.vector
            def _(dve):
                cols = c.agg[:, :, 0:NODES]
                for sem in (q_ready, at_ready, added):
                    dve.sem_inc(sem, 1)
                dve.wait_ge(loaded, 48)
                dve.tensor_tensor(cols, cols, c.agg[:, :, WRAP:WRAP + NODES], ALU.add).then_inc(part, 1)
                with dve.Fori(0, NT // GROUP) as k:
                    for i, col, n in steps(k):
                        dve.wait_ge(q_in, i + 1)
                        dve.tensor_scalar(low[:, :, 0:n], c.psum[:, 0:2, 0:n], 0.0, None, ALU.min).then_inc(low_ready, 1)
                        dve.wait_ge(exp_ready, i + 1)
                        dve.wait_ge(ctx_ready, i + 1)
                        dve.scalar_tensor_tensor(out=q[:, :, 0:n], in0=c.psum[:, 0:2, 0:n], scalar=0.0,
                                                 in1=low[:, :, 0:n], op0=ALU.max, op1=ALU.add).then_inc(q_ready, 1)
                        dve.wait_ge(ctx_ready, i + 2)
                        dve.tensor_scalar(inv[:, :, 0:n], c.psum[:, 4:6, 0:n], 1e-6, None, ALU.max).then_inc(part, 1)
                        dve.wait_ge(part, i * 2 + 2)
                        dve.reciprocal(inv[:, :, 0:n], inv[:, :, 0:n]).then_inc(part, 1)
                        dve.wait_ge(part, i * 2 + 3)
                        dve.wait_ge(out_ready, i + 1)
                        dve.tensor_tensor(at[:, :, 0:n], c.psum[:, 2:4, 0:n], inv[:, :, 0:n], ALU.mult).then_inc(at_ready, 1)
                        dve.wait_ge(out_ready, i + 2)
                        for b in range(KB):
                            cols = c.agg[:, b, bass.ds(col, n)]
                            c.fence(dve)
                            ins = dve.scalar_tensor_tensor(out=cols, in0=c.ps[6 + b][:, 0:n], scalar=bp[:, b:b + 1],
                                                           in1=cols, op0=ALU.add, op1=ALU.add)
                        ins.then_inc(added, 1)


def stage_sum(c, tag, first):
    nc = c.nc
    ctx = ExitStack()
    with ctx:
        stage = c.sb(tag + "stage", [128, GROUP, 2 * KB, TP], ctx=ctx)
        stats = c.sb(tag + "stats", [TP, 4, NT], ctx=ctx)
        gb = c.sb(tag + "gb", [TP, 2, D], ctx=ctx)
        mean, var, std, rstd = (stats[:, n, :] for n in range(4))
        folded, staged, turned, unturned, step_ready, var_ready, std_ready, loaded = (
            c.sem(tag + n) for n in ("folded", "staged", "turned", "unturned", "step", "var", "std", "loaded"))
        agg2 = c.big[0:TP, 0:NT * D].rearrange("p (t d) -> p t d", t=NT)
        with nc.Block() as block:
            @block.sync
            def _(sp):
                if first:
                    sp.dma_start(gb[:, 0, :], c.i["gnn0_gamma"]).then_inc(loaded, 16)
                    sp.dma_start(gb[:, 1, :], c.i["gnn0_beta"]).then_inc(loaded, 16)

            @block.scalar
            def _(act):
                act.wait_ge(folded, 1)
                with act.Fori(0, NT // GROUP) as k:
                    for u in range(GROUP):
                        t = k * GROUP + u
                        act.wait_ge(turned, t + 1)
                        c.fence(act)
                        act.activation(stage[:, u, 0:KB, :], c.agg[:, :, bass.ds(t * TP, TP)], ACT.Copy).then_inc(staged, 1)
                        if first:
                            c.fence(act)
                            act.activation(stage[:, u, KB:2 * KB, :], c.CT[:, :, bass.ds(t * TP, TP)],
                                           ACT.Copy).then_inc(staged, 1)
                if first:
                    act.wait_ge(var_ready, 1)
                    act.activation(std, var, ACT.Sqrt).then_inc(std_ready, 1)

            @block.tensor
            def _(pe):
                pe.sem_inc(turned, GROUP)
                with pe.Fori(0, NT // GROUP) as k:
                    for u in range(GROUP):
                        t = k * GROUP + u
                        pe.wait_ge(staged, (t + 1) * (1 + first))
                        pe.wait_ge(unturned, t * (1 + first) + 1)
                        for b in range(KB):
                            last = pe.transpose(c.ps[0][0:TP, b * 128:(b + 1) * 128], stage[:, u, b, :], c.ident[:, :])
                        if first:
                            for b in range(KB):
                                last = pe.matmul(c.ps[1][0:TP, 0:D], stage[:, u, KB + b, :], c.mix[:, b, :],
                                                 start=(b == 0), stop=(b == KB - 1))
                        last.then_inc(turned, 1)

            @block.vector
            def _(dve):
                if first:
                    cols = c.agg[:, :, 0:NODES]
                    dve.tensor_tensor(cols, cols, c.agg[:, :, WRAP:WRAP + NODES], ALU.add).then_inc(folded, 1)
                else:
                    dve.sem_inc(folded, 1)
                dve.sem_inc(unturned, 1)
                with dve.Fori(0, NT // GROUP) as k:
                    for u in range(GROUP):
                        t = k * GROUP + u
                        dve.wait_ge(turned, t + 1 + GROUP)
                        pairs = ((c.ps[0], c.C if first else c.X),) + (((c.ps[1], c.X),) if first else ())
                        for src, dst in pairs:
                            tile = dst[:, bass.ds(t, 1), :].rearrange("p a d -> p (a d)")
                            c.fence(dve)
                            dve.tensor_tensor(tile, tile, src[0:TP, 0:D], ALU.add).then_inc(unturned, 1)
                dve.wait_ge(unturned, NT * (1 + first) + 1)
                if first:
                    do = Chain(dve, step_ready)
                    do(dve.tensor_reduce(mean, c.C[:, :, :], AX.X, ALU.add))
                    do(dve.tensor_scalar(mean, mean, 1.0 / D, None, ALU.mult))
                    do(dve.tensor_tensor(c.C[:, :, :], c.C[:, :, :], bc(mean, 2, D), ALU.subtract))
                    do(dve.tensor_tensor(agg2, c.C[:, :, :], c.C[:, :, :], ALU.mult))
                    do(dve.tensor_reduce(var, agg2, AX.X, ALU.add))
                    dve.tensor_scalar(var, var, 1.0 / D, EPS, ALU.mult, ALU.add).then_inc(var_ready, 1)
                    dve.wait_ge(std_ready, 1)
                    dve.wait_ge(loaded, 32)
                    do(dve.reciprocal(rstd, std))
                    do(dve.tensor_tensor(c.C[:, :, :], c.C[:, :, :], bc(rstd, 2, D), ALU.mult))
                    do(dve.tensor_tensor(c.C[:, :, :], c.C[:, :, :], bc(gb[:, 0, :], 1, NT), ALU.mult))
                    do(dve.tensor_tensor(c.C[:, :, :], c.C[:, :, :], bc(gb[:, 1, :], 1, NT), ALU.add))
                    do(dve.tensor_tensor(c.X[:, :, :], c.X[:, :, :], c.C[:, :, :], ALU.add))
                    do(dve.tensor_tensor(c.X[:, :, :], c.X[:, :, :], bc(c.mix_c[0:TP, :], 1, NT), ALU.add))


class Router:

    def __init__(self, c, tag, n, ctx):
        self.c, self.n = c, n
        self.rank = c.sb(tag + "rank", [TP, n], ctx=ctx)
        self.eq = c.sb(tag + "eq", [TP, NT, n], ctx=ctx)
        self.hot = [c.sb(tag + f"hot{i}", [TP, NT, n], ctx=ctx) for i in range(2)]
        self.best = [c.sb(tag + f"best{i}", [TP, NT], ctx=ctx) for i in range(2)]
        self.top = c.sb(tag + "top", [TP, NT], ctx=ctx)

    def choose(self, dve, do, s, away):
        n = self.n
        do(dve.tensor_scalar(self.rank[:, :], self.c.iota[0:TP, 0:n], -1.0, float(n), ALU.mult, ALU.add))
        for i in range(2):
            hot, best, eq, top = self.hot[i], self.best[i], self.eq, self.top
            do(dve.tensor_reduce(best[:, :], s, AX.X, ALU.max))
            do(dve.tensor_tensor(eq[:, :, :], s, bc(best[:, :], 2, n), ALU.is_equal))
            do(dve.tensor_tensor(eq[:, :, :], eq[:, :, :], bc(self.rank[:, :], 1, NT), ALU.mult))
            do(dve.tensor_reduce(top[:, :], eq[:, :, :], AX.X, ALU.max))
            do(dve.tensor_tensor(hot[:, :, :], eq[:, :, :], bc(top[:, :], 2, n), ALU.is_equal))
            if i == 0:
                do(dve.scalar_tensor_tensor(out=s, in0=hot[:, :, :], scalar=-away, in1=s, op0=ALU.mult, op1=ALU.add))


def stage_route(c, tag):
    nc = c.nc
    ctx = ExitStack()
    with ctx:
        r = Router(c, tag, E0, ctx)
        total, inv = c.sb(tag + "total", [TP, NT], ctx=ctx), c.sb(tag + "inv", [TP, NT], ctx=ctx)
        steps, shifted, exped = c.sem(tag + "steps"), c.sem(tag + "shifted"), c.sem(tag + "exped")
        L = c.gate[:, :, 0:E0]
        with nc.Block() as block:
            @block.scalar
            def _(act):
                act.wait_ge(shifted, 1)
                act.activation(L, L, ACT.Exp).then_inc(exped, 1)

            @block.vector
            def _(dve):
                do = Chain(dve, steps)
                do(dve.tensor_reduce(total[:, :], L, AX.X, ALU.max))
                dve.tensor_tensor(L, L, bc(total[:, :], 2, E0), ALU.subtract).then_inc(shifted, 1)
                dve.wait_ge(exped, 1)
                do(dve.tensor_reduce(total[:, :], L, AX.X, ALU.add))
                do(dve.reciprocal(inv[:, :], total[:, :]))
                do(dve.tensor_tensor(L, L, bc(inv[:, :], 2, E0), ALU.mult))
                r.choose(dve, do, L, 2.0)
                do(dve.tensor_tensor(total[:, :], r.best[0][:, :], r.best[1][:, :], ALU.add))
                do(dve.tensor_scalar(total[:, :], total[:, :], 1e-12, None, ALU.max))
                do(dve.reciprocal(inv[:, :], total[:, :]))
                for i in range(2):
                    do(dve.tensor_tensor(r.best[i][:, :], r.best[i][:, :], inv[:, :], ALU.mult))
                    do(dve.tensor_tensor(r.hot[i][:, :, :], r.hot[i][:, :, :], bc(r.best[i][:, :], 2, E0), ALU.mult))
                do(dve.tensor_tensor(L, r.hot[0][:, :, :], r.hot[1][:, :, :], ALU.add))


def stage_experts(c, tag, n_exp, F, out):
    nc = c.nc
    ctx = ExitStack()
    FB = F // 128
    NG = NT // GROUP
    UNITS = 2 * NG
    H = len(HALVES) * FB
    with ctx:
        def sb(name, shape, dt=F32):
            return c.sb(tag + name, shape, dt, ctx=ctx)

        w1, w2 = sb("w1", [128, 2, KB, F]), sb("w2", [128, 2, FB, D])
        b1, b2 = sb("b1", [128, 2, FB]), sb("b2", [TP, 2, D])
        tmp = sb("tmp", [TP, 2, D])
        hid = c.big[:, 0:2 * FB * GC].rearrange("p (j f n) -> p j f n", j=2, f=FB)
        w_in = [c.sem(tag + f"w_in{j}") for j in range(2)]
        h_psum, h_ready, y_psum, y_half, y_added = (c.sem(tag + n) for n in ("h_psum", "h_ready", "y_psum", "y_half", "y_added"))
        n_body = n_exp // 2

        with nc.Block() as block:
            @block.sync
            def _(sp):
                def load(e, j):
                    for dst, src in ((w1[:, j, :, :], blocks3(c.i[tag + "w1"], e)), (w2[:, j, :, :], blocks3(c.i[tag + "w2"], e)),
                                     (b1[:, j, :], one(c.i[tag + "b1"], e)), (b2[:, j, :], one(c.i[tag + "b2"], e))):
                        sp.dma_start(dst, src).then_inc(w_in[j], 16)

                def one(ap, e):
                    return ap[bass.ds(e, 1)].rearrange("a p n -> (a p) n")

                def blocks3(ap, e):
                    return ap[bass.ds(e, 1)].rearrange("a (b p) n -> p (a b) n", p=128)
                load(0, 0)
                load(1, 1)
                with sp.Fori(1, n_body) as b:
                    for j in range(2):
                        sp.wait_ge(y_added, (b - 1) * 2 * NT + (j + 1) * NT + 2)
                        c.fence(sp)
                        load(b * 2 + j, j)

            @block.tensor
            def _(pe):
                pe.sem_inc(y_psum, GROUP + 1)

                def hidden(b, v):
                    if v == UNITS:
                        b, v = b + 1, 0
                    j, g = divmod(v, NG)
                    if g == 0:
                        pe.wait_ge(w_in[j], (b + 1) * 64)
                    n = 0
                    for h0, cols in HALVES:
                        for f in range(FB):
                            i = (b * UNITS + v) * H + n
                            pe.wait_ge(h_ready, i + 1)
                            for kb in range(KB):
                                last = pe.matmul(c.ps[n % 4][:, 0:cols], w1[:, j, kb, f * 128:(f + 1) * 128],
                                                 c.CT[:, kb, g * GC + h0:g * GC + h0 + cols], start=(kb == 0),
                                                 stop=(kb == KB - 1))
                            last.then_inc(h_psum, 1)
                            n += 1

                def output(b, v):
                    j, g = divmod(v, NG)
                    unit = b * UNITS + v
                    pe.wait_ge(h_ready, (unit + 1) * H + 4)
                    for q in range(GROUP):
                        i = unit * GROUP + q
                        pe.wait_ge(y_half, i + (4 if q == 0 else 1 if q == 4 else 0))
                        for f in range(FB):
                            last = pe.matmul(c.ps[4 + q % 4][0:TP, 0:D], hid[:, v % 2, f, q * TP:(q + 1) * TP],
                                             w2[:, j, f, :], start=(f == 0), stop=(f == FB - 1))
                        last.then_inc(y_psum, 1)

                hidden(0, 0)
                with pe.Fori(0, n_body - 1) as b:
                    for v in range(UNITS):
                        hidden(b, v + 1)
                        output(b, v)
                for v in range(UNITS):
                    if v + 1 < UNITS:
                        hidden(n_body - 1, v + 1)
                    output(n_body - 1, v)

            @block.scalar
            def _(act):
                act.sem_inc(h_ready, 4)
                with act.Fori(0, n_body) as b:
                    for v in range(UNITS):
                        j, g = divmod(v, NG)
                        n = 0
                        act.wait_ge(y_psum, (b * UNITS + v) * GROUP + 1)
                        for h0, cols in HALVES:
                            for f in range(FB):
                                act.wait_ge(h_psum, (b * UNITS + v) * H + n + 1)
                                act.activation(hid[:, v % 2, f, h0:h0 + cols], c.ps[n % 4][:, 0:cols], ACT.Gelu,
                                               bias=b1[:, j, f:f + 1]).then_inc(h_ready, 1)
                                n += 1

            @block.vector
            def _(dve):
                dve.sem_inc(y_half, 4)
                dve.sem_inc(y_added, 2)

                def biased(b, n):
                    j, g, q = n // NT, n % NT // GROUP, n % GROUP
                    i = b * UNITS * GROUP + n
                    if n % NT == 0:
                        dve.wait_ge(w_in[j], (b + 1) * 64)
                    dve.wait_ge(y_psum, i + 2 + GROUP)
                    dve.wait_ge(y_added, i + 1)
                    dve.tensor_tensor(tmp[:, n % 2, :], c.ps[4 + q % 4][0:TP, 0:D], b2[:, j, :],
                                      ALU.add).then_inc(y_half, 1)

                with dve.Fori(0, n_body) as b:
                    biased(b, 0)
                    for n in range(2 * NT):
                        if n + 1 < 2 * NT:
                            biased(b, n + 1)
                        i = b * UNITS * GROUP + n
                        t = n % NT
                        dve.wait_ge(y_half, i + 5)
                        c.fence(dve)
                        dve.scalar_tensor_tensor(out=out[:, t, :], in0=tmp[:, n % 2, :],
                                                 scalar=c.gate[:, t, bass.ds(b * 2 + n // NT, 1)], in1=out[:, t, :],
                                                 op0=ALU.mult, op1=ALU.add).then_inc(y_added, 1)


def stage_add(c, tag):
    done = c.sem(tag + "done")
    with c.nc.Block() as block:
        @block.vector
        def _(dve):
            Chain(dve, done)(dve.tensor_tensor(c.X[:, :, :], c.X[:, :, :], c.C[:, :, :], ALU.add))


def stage_attention_router(c, tag):
    nc = c.nc
    ctx = ExitStack()
    CH = GH + GH * E1
    BODY = 2 * SUP
    NB = GSUP // 2
    SETS, TURNS = 5, 7
    ROUNDS = SETS * TURNS
    assert TURNS * (GSUP // 2) * 2 * SUP * 16 < 2 ** 16
    with ctx:
        def sb(name, shape, dt=F32):
            return c.sb(tag + name, shape, dt, ctx=ctx)

        def heads(ap):
            return ap.rearrange("p t (h e) -> p t h e", h=GH)

        rows_s, rows_d = sb("rows_s", [TP, NT, CH]), sb("rows_d", [TP, NT, 2 * GH])
        att = sb("att", [TP, 5, GH * E1])
        t16, agg = sb("t16", [TP, NT, 16]), sb("agg", [TP, NT, 16])
        ends, ends_t, ends_d, ends_all = sb("ends", [TP, 2 * GH]), sb("ends_t", [2 * GH, 1]), sb("ends_d", [2 * GH, 2 * GH]), sb("ends_all", [TP, 2 * GH])
        low, high, mid = sb("low", [TP, NT, GH]), sb("high", [TP, NT, GH]), sb("mid", [TP, NT, GH])
        x4, y4, own = sb("x4", [TP, NT, GH]), sb("y4", [TP, NT, GH]), sb("own", [TP, NT, GH])
        far, far_i = sb("far", [1, 2]), sb("far_i", [1, 1], I32)
        src_i, dst_i = sb("src_i", [128, GSUP * SUP], I32), sb("dst_i", [128, GSUP * SUP], I32)
        lo, hi = sb("lo", [128, GSUP * SUP]), sb("hi", [128, GSUP * SUP])
        idx = sb("idx", [128, 2, 2, SUP], I32)
        S, T = sb("S", [128, 2, SUP, CH]), sb("T", [128, 2, SUP, 2 * GH])
        w, R = sb("w", [128, 2, SUP, GH]), sb("R", [128, 2, SUP, CH])
        row_hot, spread = sb("row_hot", [128, 2, TP]), sb("spread", [128, 2, NT, CH])
        router = Router(c, tag, E1, ctx)
        st = sb("st", [TP, 4, NT])
        h = c.gate[:, :, 0:16]
        a_src, a_dst, m_dst = rows_s[:, :, 0:GH], rows_d[:, :, 0:GH], rows_d[:, :, GH:2 * GH]
        loads = [(att[:, :, :], c.i["gat_vectors"]), (src_i[:, :], c.i["gat_src"]), (dst_i[:, :], c.i["gat_dst"])]
        loaded, steps, ends_ready, turned, diag_ready, all_ready, flag, tables, tables_in = (
            c.sem(tag + n) for n in ("loaded", "steps", "ends", "turned", "diag", "all", "flag", "tables", "tables_in"))
        gsrc_v, gdst_v = (a.rearrange("(t p) d -> p t d", p=TP) for a in (c.gsrc, c.gdst))

        def leaky(do, dve, out, x):
            do(dve.scalar_tensor_tensor(out=out, in0=x, scalar=0.2, in1=x, op0=ALU.mult, op1=ALU.max))

        with nc.Block() as block:
            @block.sync
            def _(sp):
                for dst, src in loads:
                    sp.dma_start(dst, src).then_inc(loaded, 16)
                sp.wait_ge(tables, 1)
                sp.dma_start(gsrc_v, rows_s[:, :, :]).then_inc(tables_in, 16)
                sp.dma_start(gdst_v, rows_d[:, :, :]).then_inc(tables_in, 16)
                sp.wait_ge(tables_in, 32)

            @block.vector
            def _(dve):
                dve.wait_ge(loaded, 16 * len(loads))
                do = Chain(dve, steps)
                for n, out in ((0, a_src), (1, a_dst)):
                    do(dve.tensor_tensor(t16[:, :, :], h, bc(att[:, n, :], 1, NT), ALU.mult))
                    do(dve.tensor_reduce(out, heads(t16[:, :, :]), AX.X, ALU.add))
                do(dve.tensor_copy(rows_s[:, :, GH:CH], h))
                do(dve.tensor_reduce(ends[:, 0:GH], a_src.rearrange("p t h -> p h t"), AX.X, ALU.max))
                do(dve.tensor_reduce(ends[:, GH:2 * GH], a_src.rearrange("p t h -> p h t"), AX.X, ALU.min))
                dve.tensor_scalar(ends[:, GH:2 * GH], ends[:, GH:2 * GH], -1.0, None, ALU.mult).then_inc(ends_ready, 1)
                dve.wait_ge(turned, 1)
                do(dve.tensor_reduce(ends_t[:, :], c.ps[0][0:2 * GH, 0:TP], AX.X, ALU.max))
                dve.tensor_scalar(ends_d[:, :], c.ident[0:2 * GH, 0:2 * GH], ends_t[:, 0:1], None,
                                  ALU.mult).then_inc(diag_ready, 1)
                dve.wait_ge(all_ready, 1)
                do(dve.tensor_copy(ends_all[:, :], c.ps[1][0:TP, 0:2 * GH]))
                top = bc(ends_all[:, 0:GH], 1, NT)
                do(dve.tensor_tensor(x4[:, :, :], a_dst, top, ALU.add))
                leaky(do, dve, m_dst, x4[:, :, :])
                do(dve.tensor_copy(low[:, :, :], a_src))
                do(dve.tensor_tensor(high[:, :, :], bc(ends_all[:, 0:GH], 1, NT), bc(ends_all[:, 0:GH], 1, NT), ALU.max))
                do(dve.tensor_tensor(ends[:, 0:GH], ends_all[:, 0:GH], ends_all[:, GH:2 * GH], ALU.add))
                do(dve.tensor_reduce(far[:, 0:1], ends[0:1, 0:GH], AX.X, ALU.max))
                do(dve.tensor_scalar(far[:, 1:2], far[:, 0:1], SPAN, None, ALU.is_gt))
                do(dve.tensor_copy(far_i[:, :], far[:, 1:2]))
                dve.sem_inc(tables, 1)
                do(dve.tensor_copy(hi[:, :], dst_i[:, :]))
                do(dve.memset(lo[:, :], 0.0))
                for k in range(1, NT + 1):
                    do(dve.scalar_tensor_tensor(out=lo[:, :], in0=hi[:, :], scalar=float(k * TP), in1=lo[:, :],
                                                op0=ALU.is_ge, op1=ALU.add))
                do(dve.scalar_tensor_tensor(out=hi[:, :], in0=lo[:, :], scalar=-float(TP), in1=hi[:, :], op0=ALU.mult,
                                            op1=ALU.add))
                do(dve.tensor_scalar(src_i[:, :], src_i[:, :], float(NODES - 1), None, ALU.min))
                do(dve.tensor_scalar(dst_i[:, :], dst_i[:, :], float(NODES - 1), None, ALU.min))

            @block.tensor
            def _(pe):
                pe.wait_ge(ends_ready, 1)
                pe.transpose(c.ps[0][0:2 * GH, 0:TP], ends[:, :], c.ident[0:TP, 0:TP]).then_inc(turned, 1)
                pe.wait_ge(diag_ready, 1)
                pe.matmul(c.ps[1][0:TP, 0:2 * GH], c.ones[0:2 * GH, 0:TP], ends_d[:, :], start=True,
                          stop=True).then_inc(all_ready, 1)

        def sums(mode, s):
            def tiles(eng, p, step):
                step(p, 0, 0, True)
                with eng.Fori(1, NB) as k:
                    step(p, k, 0, False)

            def pool_pass(pool, p, turn, g):
                with pool.Fori(0, NB) as k:
                    for j in range(2):
                        n = p * GSUP + k * 2 + j
                        pool.wait_ge(s["idx_ready"], n + 1)
                        pool.wait_ge(s["R_ready"], n + 1)
                        pool.sem_inc(s["begun"], 1)
                        for q in range(SUP):
                            pool.indirect_dma_start(S[:, j, q, :], None, c.gsrc,
                                                    bass.IndirectOffsetOnAxis(idx[:, j, 0, q:q + 1], 0)).then_inc(
                                g[j], 16)
                            pool.indirect_dma_start(T[:, j, q, :], None, c.gdst,
                                                    bass.IndirectOffsetOnAxis(idx[:, j, 1, q:q + 1], 0)).then_inc(
                                g[j], 16)

            def act_pass(act, p):
                with act.Fori(0, NB) as k:
                    for j in range(2):
                        n = p * GSUP + k * 2 + j
                        act.wait_ge(s["e_ready"], n + 1)
                        act.activation(w[:, j, :, :], w[:, j, :, :], ACT.Exp).then_inc(s["w_ready"], 1)

            def dve_pass(dve, p, turn, g):
                def indices(k, j):
                    c.fence(dve)
                    dve.tensor_copy(idx[:, j, 0, :], src_i[:, bass.ds((k * 2 + j) * SUP, SUP)]).then_inc(s["idx_half"], 1)
                    c.fence(dve)
                    dve.tensor_copy(idx[:, j, 1, :], dst_i[:, bass.ds((k * 2 + j) * SUP, SUP)]).then_inc(s["idx_ready"], 1)

                def logits(k, j):
                    n = p * GSUP + k * 2 + j
                    dve.wait_ge(g[j], (turn * NB + k + 1) * 16 * 2 * SUP)
                    src, dst, m = S[:, j, :, 0:GH], T[:, j, :, 0:GH], T[:, j, :, GH:2 * GH]
                    dve.wait_ge(s["R_ready"], n + 1)
                    if mode == "above":
                        dve.tensor_tensor(w[:, j, :, :], src, m, ALU.is_gt).then_inc(s["w_ready"], 1)
                        return
                    dve.tensor_tensor(w[:, j, :, :], src, dst, ALU.add).then_inc(s["e_steps"], 1)
                    dve.wait_ge(s["e_steps"], n * 2 + 1)
                    dve.scalar_tensor_tensor(out=w[:, j, :, :], in0=w[:, j, :, :], scalar=0.2, in1=w[:, j, :, :],
                                             op0=ALU.mult, op1=ALU.max).then_inc(s["e_steps"], 1)
                    dve.wait_ge(s["e_steps"], n * 2 + 2)
                    dve.tensor_tensor(w[:, j, :, :], w[:, j, :, :], m, ALU.subtract).then_inc(s["e_ready"], 1)

                def weighted(k, j):
                    n = p * GSUP + k * 2 + j
                    dve.wait_ge(s["w_ready"], n + 1)
                    dve.wait_ge(s["spread_ready"], n * SUP + 1)
                    dve.tensor_copy(R[:, j, :, 0:GH], w[:, j, :, :]).then_inc(s["R_half"], 1)
                    dve.tensor_tensor(R[:, j, :, GH:CH].rearrange("p q (h e) -> p q h e", h=GH),
                                      S[:, j, :, GH:CH].rearrange("p q (h e) -> p q h e", h=GH),
                                      bc(w[:, j, :, :], 3, E1), ALU.mult).then_inc(s["R_ready"], 1)

                def hots(k, j):
                    for q in range(SUP):
                        i = p * GSUP * SUP + k * BODY + j * SUP + q
                        at = k * BODY + j * SUP + q
                        dve.wait_ge(s["tile_used"], i + 1)
                        if q == 0:
                            dve.wait_ge(s["R_half"], p * GSUP + k * 2 + j + 1)
                            dve.wait_ge(s["R_ready"], p * GSUP + k * 2 + j + 3)
                        c.fence(dve)
                        dve.tensor_scalar(row_hot[:, q % 2, :], c.iota[:, 0:TP], hi[:, bass.ds(at, 1)], None,
                                          ALU.is_equal).then_inc(s["hot_ready"], 1)
                        c.fence(dve)
                        dve.scalar_tensor_tensor(out=spread[:, q % 2, :, :], in0=bc(c.iota[:, 0:NT], 2, CH),
                                                 scalar=lo[:, bass.ds(at, 1)], in1=bc(R[:, j, q, :], 1, NT),
                                                 op0=ALU.is_equal, op1=ALU.mult).then_inc(s["spread_ready"], 1)

                def supertile(k, j, last=False):
                    weighted(k, j)
                    if not last:
                        indices(k + 1, j)
                    if not (last and j == 1):
                        logits(k + j, 1 - j)
                    hots(k, j)

                indices(0, 0)
                indices(0, 1)
                logits(0, 0)
                with dve.Fori(0, NB - 1) as k:
                    for j in range(2):
                        supertile(k, j)
                for j in range(2):
                    supertile(NB - 1, j, last=True)

            def pe_pass(pe, p):
                def body(k, first, last):
                    for u in range(BODY):
                        i = p * GSUP * SUP + k * BODY + u
                        pe.wait_ge(s["hot_ready"], i + 1)
                        pe.wait_ge(s["spread_ready"], i + 2)
                        pe.matmul(c.ps[7][0:TP, 0:NT * CH], row_hot[:, u % 2, :],
                                  spread[:, u % 2, :, :].rearrange("p t c -> p (t c)"),
                                  start=first and u == 0, stop=last and u == BODY - 1).then_inc(s["tile_used"], 1)
                body(0, True, False)
                with pe.Fori(1, NB - 1) as k:
                    body(k, False, False)
                body(NB - 1, False, True)

            return pool_pass, act_pass, dve_pass, pe_pass

        names = ("idx_half", "idx_ready", "begun", "R_half", "R_ready", "e_steps", "e_ready", "w_ready",
                 "spread_ready", "hot_ready", "tile_used", "moved", "stored")
        acc = c.ps[7][0:TP, 0:NT * CH].rearrange("p (t c) -> p t c", t=NT)

        s = {n: c.sem(tag + "g_" + n) for n in names}
        pool_pass, _, dve_pass, pe_pass = sums("above", s)
        gathered = [[c.sem(f"{tag}g_in{n}_{j}") for j in range(2)] for n in range(SETS)]

        def if_far(eng, work):
            more = eng.value_load(far_i[0:1, 0:1], min_val=0, max_val=1)
            with eng.If(more > 0):
                work(eng)

        with nc.Block() as block:
            @block.sync
            def _(sp):
                def work(sp):
                    with sp.Fori(0, ROUNDS + 1) as p:
                        sp.wait_ge(s["moved"], p + 1)
                        c.fence(sp)
                        sp.dma_start(gdst_v, rows_d[:, :, :]).then_inc(s["stored"], 16)
                if_far(sp, work)

            @block.gpsimd
            def _(pool):
                def work(pool):
                    with pool.Fori(0, TURNS) as turn:
                        for n in range(SETS):
                            p = turn * SETS + n
                            pool.wait_ge(s["stored"], 16 * p + 16)
                            pool.sem_inc(s["begun"], 1)
                            pool_pass(pool, p, turn, gathered[n])
                if_far(pool, work)

            @block.tensor
            def _(pe):
                def work(pe):
                    pe.sem_inc(s["tile_used"], 2)
                    with pe.Fori(0, ROUNDS) as p:
                        pe.wait_ge(s["moved"], p + 1)
                        pe_pass(pe, p)
                if_far(pe, work)

            @block.vector
            def _(dve):
                def work(dve):
                    step = c.sem(tag + "g_steps")
                    PER = 10

                    def halve(do):
                        do(dve.tensor_tensor(mid[:, :, :], high[:, :, :], low[:, :, :], ALU.subtract))
                        do(dve.scalar_tensor_tensor(out=mid[:, :, :], in0=mid[:, :, :], scalar=0.5, in1=low[:, :, :],
                                                    op0=ALU.mult, op1=ALU.add))
                        do(dve.tensor_copy(m_dst, mid[:, :, :]))
                        dve.sem_inc(s["moved"], 1)
                    dve.sem_inc(s["R_ready"], 2)
                    dve.sem_inc(s["spread_ready"], 1)
                    first = Chain(dve, step)
                    halve(first)
                    def one_round(turn, n, g):
                        p = turn * SETS + n
                        dve.wait_ge(s["stored"], 16 * p + 16)
                        dve_pass(dve, p, turn, g)
                        dve.wait_ge(s["tile_used"], (p + 1) * GSUP * SUP + 2)
                        do = Chain(dve, step, p * PER + first.n)
                        do(dve.tensor_scalar(x4[:, :, :], acc[:, :, 0:GH], 0.5, None, ALU.is_gt))
                        do(dve.tensor_tensor(y4[:, :, :], mid[:, :, :], low[:, :, :], ALU.subtract))
                        do(dve.tensor_tensor(y4[:, :, :], y4[:, :, :], x4[:, :, :], ALU.mult))
                        do(dve.tensor_tensor(low[:, :, :], low[:, :, :], y4[:, :, :], ALU.add))
                        do(dve.tensor_scalar(x4[:, :, :], x4[:, :, :], -1.0, 1.0, ALU.mult, ALU.add))
                        do(dve.tensor_tensor(y4[:, :, :], mid[:, :, :], high[:, :, :], ALU.subtract))
                        do(dve.tensor_tensor(y4[:, :, :], y4[:, :, :], x4[:, :, :], ALU.mult))
                        do(dve.tensor_tensor(high[:, :, :], high[:, :, :], y4[:, :, :], ALU.add))
                        do(dve.tensor_tensor(x4[:, :, :], a_dst, high[:, :, :], ALU.add))
                        leaky(do, dve, own[:, :, :], x4[:, :, :])
                        assert do.n == PER
                        do = Chain(dve, half_steps, p * 3)
                        halve(do)

                    with dve.Fori(0, TURNS) as turn:
                        for n in range(SETS):
                            one_round(turn, n, gathered[n])
                    dve.wait_ge(s["stored"], 16 * ROUNDS + 16)
                    do = Chain(dve, step, ROUNDS * PER + first.n)
                    do(dve.tensor_copy(m_dst, own[:, :, :]))
                half_steps = c.sem(tag + "g_half")
                if_far(dve, work)

        s = {n: c.sem(tag + "w_" + n) for n in names}
        w_in = [c.sem(f"{tag}w_in{j}") for j in range(2)]
        wpool, wact, wdve, wpe = sums("weights", s)
        own_in, own_ready, var_ready, std_ready, e_in, e_ready, chosen, guarded = (
            c.sem(tag + n) for n in ("own_in", "own_ready", "var", "std", "e_in", "e_out", "chosen", "guarded"))
        done2 = c.sem(tag + "steps2")
        with nc.Block() as block:
            @block.sync
            def _(sp):
                def work(sp):
                    sp.dma_start(gdst_v, rows_d[:, :, :]).then_inc(guarded, 16)
                    sp.wait_ge(guarded, 16)
                if_far(sp, work)
                sp.sem_inc(tables, 1)

            @block.gpsimd
            def _(pool):
                pool.wait_ge(tables, 2)
                wpool(pool, 0, 0, w_in)

            @block.tensor
            def _(pe):
                pe.sem_inc(s["tile_used"], 2)
                wpe(pe, 0)

            @block.scalar
            def _(act):
                act.wait_ge(own_in, 1)
                act.activation(own[:, :, :], own[:, :, :], ACT.Exp).then_inc(own_ready, 1)
                wact(act, 0)
                act.wait_ge(var_ready, 1)
                act.activation(st[:, 2, :], st[:, 1, :], ACT.Sqrt).then_inc(std_ready, 1)
                act.wait_ge(e_in, 1)
                act.activation(router.best[1][:, :], router.best[1][:, :], ACT.Exp).then_inc(e_ready, 1)

            @block.vector
            def _(dve):
                do = Chain(dve, done2)
                dve.sem_inc(s["R_ready"], 2)
                dve.sem_inc(s["spread_ready"], 1)
                do(dve.tensor_tensor(x4[:, :, :], a_src, a_dst, ALU.add))
                leaky(do, dve, y4[:, :, :], x4[:, :, :])
                dve.tensor_tensor(own[:, :, :], y4[:, :, :], m_dst, ALU.subtract).then_inc(own_in, 1)
                wdve(dve, 0, 0, w_in)
                dve.wait_ge(own_ready, 1)
                dve.wait_ge(s["tile_used"], GSUP * SUP + 2)
                do(dve.tensor_tensor(x4[:, :, :], acc[:, :, 0:GH], own[:, :, :], ALU.add))
                do(dve.tensor_scalar(x4[:, :, :], x4[:, :, :], 1e-16, None, ALU.add))
                do(dve.reciprocal(y4[:, :, :], x4[:, :, :]))
                do(dve.tensor_tensor(heads(t16[:, :, :]), heads(h), bc(own[:, :, :], 3, E1), ALU.mult))
                do(dve.tensor_tensor(t16[:, :, :], t16[:, :, :], acc[:, :, GH:CH], ALU.add))
                do(dve.tensor_tensor(heads(agg[:, :, :]), heads(t16[:, :, :]), bc(y4[:, :, :], 3, E1), ALU.mult))
                do(dve.tensor_tensor(agg[:, :, :], agg[:, :, :], bc(att[:, 2, :], 1, NT), ALU.add))
                mean, var, std, rstd = (st[:, n, :] for n in range(4))
                do(dve.tensor_reduce(mean, agg[:, :, :], AX.X, ALU.add))
                do(dve.tensor_scalar(mean, mean, 1.0 / 16, None, ALU.mult))
                do(dve.tensor_tensor(agg[:, :, :], agg[:, :, :], bc(mean, 2, 16), ALU.subtract))
                do(dve.tensor_tensor(t16[:, :, :], agg[:, :, :], agg[:, :, :], ALU.mult))
                do(dve.tensor_reduce(var, t16[:, :, :], AX.X, ALU.add))
                dve.tensor_scalar(var, var, 1.0 / 16, EPS, ALU.mult, ALU.add).then_inc(var_ready, 1)
                dve.wait_ge(std_ready, 1)
                do(dve.reciprocal(rstd, std))
                do(dve.tensor_tensor(agg[:, :, :], agg[:, :, :], bc(rstd, 2, 16), ALU.mult))
                do(dve.tensor_tensor(agg[:, :, :], agg[:, :, :], bc(att[:, 3, :], 1, NT), ALU.mult))
                do(dve.tensor_tensor(agg[:, :, :], agg[:, :, :], bc(att[:, 4, :], 1, NT), ALU.add))
                do(dve.tensor_reduce(x4[:, :, :], agg[:, :, :].rearrange("p t (h e) -> p t e h", h=GH), AX.X, ALU.add))
                do(dve.tensor_scalar(x4[:, :, :], x4[:, :, :], 1.0 / GH, None, ALU.mult))
                router.choose(dve, do, x4[:, :, :], HUGE)
                first, second = (router.best[i][:, :] for i in range(2))
                dve.tensor_tensor(second, second, first, ALU.subtract).then_inc(e_in, 1)
                dve.wait_ge(e_ready, 1)
                do(dve.tensor_scalar(first, second, 1.0, None, ALU.add))
                do(dve.reciprocal(router.top[:, :], first))
                do(dve.tensor_tensor(second, second, router.top[:, :], ALU.mult))
                for i, wt in ((0, router.top[:, :]), (1, second)):
                    do(dve.tensor_tensor(router.hot[i][:, :, :], router.hot[i][:, :, :], bc(wt, 2, E1), ALU.mult))
                do(dve.tensor_tensor(c.gate[:, :, 0:E1], router.hot[0][:, :, :], router.hot[1][:, :, :], ALU.add))


def stage_output(c, what=None):
    nc = c.nc
    done = c.sem("output_stored")
    with nc.Block() as block:
        @block.sync
        def _(sp):
            sp.dma_start(c.out.rearrange("(t p) d -> p t d", p=TP), (c.X if what is None else what)[:, :, :]).then_inc(done, 16)
            sp.wait_ge(done, 16)


def build(nc, ins, out, stop=99):
    ctx = ExitStack()
    with ctx:
        c = Core(nc, ctx, ins, out)
        stage_constants(c)
        with ExitStack() as sub:
            w = c.wt[:, :, 0:1024]
            bias = c.sb("bias0", [TP, 1024], ctx=sub)
            stage_norm(c, "n0_", [
                dict(w=w[:, :, 0:512], w_in=blocks(ins["node_w0"]), n=512, bias=bias[:, 0:512], bias_in=ins["node_b0"], out=None),
                dict(w=w[:, :, 512:1024], w_in=blocks(ins["kv_w0"]), n=512, bias=bias[:, 512:1024], bias_in=ins["kv_b0"], out=c.kv)])
        if stop == 1:
            return stage_output(c, c.C)
        stage_context(c, "c0_", True)
        stage_edges(c, "e0_", False)
        stage_sum(c, "s0_", True)
        c.retire()
        if stop == 3:
            return stage_output(c)
        stage_norm(c, "n1_", [dict(w=c.wt[:, :, 0:E0], w_in=blocks(ins["route_w"]), n=E0, bias=None, bias_in=None, out=c.gate)])
        stage_route(c, "r0_")
        stage_experts(c, "m0_", E0, D, c.C)
        stage_add(c, "a0_")
        c.retire()
        if stop == 4:
            return stage_output(c)
        with ExitStack() as sub:
            kvw = c.sb("kv_w1", [128, KB, 512], ctx=sub)
            no_bias = dict(bias=None, bias_in=None)
            stage_norm(c, "n2_", [dict(w=c.wt[:, :, n * 512:(n + 1) * 512],
                                       w_in=blocks(ins["rel_w"])[:, :, n * 512:(n + 1) * 512], n=512, out=None, **no_bias)
                                  for n in range(RELS // 2)]
                       + [dict(w=kvw[:, :, :], w_in=blocks(ins["kv_w1"]), n=512, out=c.kv, **no_bias)])
        stage_context(c, "c1_", False)
        c.retire()
        stage_edges(c, "e1_", True)
        stage_attend(c, "t1_")
        stage_sum(c, "s1_", False)
        c.retire()
        if stop == 5:
            return stage_output(c)
        stage_norm(c, "n3_", [dict(w=c.wt[:, :, 0:16], w_in=blocks(ins["gat_w"]), n=16, bias=None, bias_in=None, out=c.gate)])
        stage_attention_router(c, "g1_")
        stage_experts(c, "m1_", E1, F1, c.X)
        stage_output(c)


def prepare(i):
    import numpy as np

    def rep(v, n):
        return np.ascontiguousarray(np.broadcast_to(v, (n, v.size)))

    def cols(v):
        return np.ascontiguousarray(v.reshape(-1, 128).T)

    def edges(v, fill):
        full = np.full(NET * ET, fill, v.dtype)
        full[:EDGES] = v.reshape(-1)
        return full

    a = {"x": i["x"]}
    dst = edges(i["dst"], -4000)
    a["dst_t"] = np.ascontiguousarray(dst.reshape(NET, ET).T)
    a["dst_base"] = rep(dst[::ES], 128)
    a["src_t"] = np.ascontiguousarray(edges(i["src"], 0).reshape(NET, ET).T)
    a["type_t"] = np.ascontiguousarray(edges(i["edge_type_16"], 0).reshape(NET, ET).T)
    a["norm_t"] = np.ascontiguousarray(edges(i["edge_weight1"], 0).reshape(NET, ET).T)
    attr = np.zeros((DE, NET * ET), np.float32)
    attr[:, :EDGES] = i["edge_attr_64"].T
    a["attr_t"] = attr
    a["node_w0"] = np.concatenate([i["L0_gnn_W1"][:D], i["L0_gnn_Wg"][:D]], 1)
    a["edge_w0"] = np.concatenate([i["L0_gnn_W1"][D:], i["L0_gnn_Wg"][D:]], 1)
    a["node_b0"] = rep(np.concatenate([i["L0_gnn_b1"], i["L0_gnn_bg"]]), TP)
    a["w2_0"], a["b2_0"] = i["L0_gnn_W2"], rep(i["L0_gnn_b2"], 128)
    a["gnn0_gamma"], a["gnn0_beta"] = rep(i["L0_gnn_gamma"], TP), rep(i["L0_gnn_beta"], TP)
    a["kv_w0"] = np.concatenate([i["L0_mix_W_qk"][1], i["L0_mix_W_v"]], 1)
    a["kv_b0"] = rep(np.concatenate([i["L0_mix_b_qk"][1], i["L0_mix_b_v"]]), TP)
    a["wq0_t"] = np.ascontiguousarray(i["L0_mix_W_qk"][0].T)
    a["bq0"] = np.ascontiguousarray(rep(i["L0_mix_b_qk"][0], TP).T)
    a["mix0_gamma"], a["mix0_beta"] = cols(i["L0_mix_gamma"]), cols(i["L0_mix_beta"])
    a["kv_w1"] = np.ascontiguousarray(i["L1_mix_Wkv"].T)
    a["wq1_t"], a["wproj_t"] = np.ascontiguousarray(i["L1_mix_Wq"].T), np.ascontiguousarray(i["L1_mix_Wproj"].T)
    a["bproj"] = cols(i["L1_mix_bproj"])
    a["rel_w"] = np.ascontiguousarray(i["L1_gnn_weight"].transpose(1, 0, 2).reshape(D, RELS * D))
    a["route_w"] = np.ascontiguousarray(i["L0_ffn_router_w"].T)
    a["gat_w"] = i["L1_ffn_W_gat"]
    for tag, name, n in (("m0_", "L0_ffn_", E0), ("m1_", "L1_ffn_", E1)):
        ws = [i[name + ("w1" if n == E0 else "W1")], i[name + ("w2" if n == E0 else "W2")]]
        a[tag + "w1"], a[tag + "w2"] = ws
        a[tag + "b1"] = np.ascontiguousarray(i[name + "b1"].reshape(n, -1, 128).transpose(0, 2, 1))
        a[tag + "b2"] = np.ascontiguousarray(np.broadcast_to(i[name + "b2"][:, None, :], (n, TP, D)))
    a["gat_vectors"] = np.ascontiguousarray(np.broadcast_to(np.stack([i["L1_ffn_" + n].reshape(-1) for n in (
        "att_src", "att_dst", "b_gat", "ln_gamma", "ln_beta")]), (TP, 5, 16)))
    for n, row in (("gat_src", 0), ("gat_dst", 1)):
        a[n] = np.ascontiguousarray(i["L1_ffn_edge_index"][row].reshape(-1, ET).T)
    return a


def kernel(**inputs):
    import numpy as np
    import concourse.bacc as bacc
    from concourse.bass_utils import run_bass_kernel_spmd as run

    nc = bacc.Bacc("TRN2", target_bir_lowering=False, num_devices=1)
    arrays = prepare({k: np.asarray(v) for k, v in inputs.items()})
    ins = {n: nc.dram_tensor(f"in_{n}", a.shape, mybir.dt.from_np(a.dtype), kind="ExternalInput").ap()
           for n, a in arrays.items()}
    out = nc.dram_tensor("out", (NODES, D), F32, kind="ExternalOutput").ap()
    build(nc, ins, out)
    r = run(nc, [{f"in_{n}": a for n, a in arrays.items()}], core_ids=[0])
    return r.results[0]["out"]
```

```python
import concourse.bass as bass
from concourse import mybir
from contextlib import ExitStack

F32, F32R, I32 = mybir.dt.float32, mybir.dt.float32r, mybir.dt.int32
ALU, ACT = mybir.AluOpType, mybir.ActivationFunctionType
AX = mybir.AxisListType

NODES, D, EDGES, DE = 3125, 256, 100000, 64
TP = 125
NT = NODES // TP
GROUP = 5
KB = D // 128
HALVES = ((0, 313), (313, 312))
GC = GROUP * TP
ET = 128
SUP = 4
ES = ET * SUP
NSUP = -(-EDGES // ES)
NET = NSUP * SUP
RELS, HEADS, HD = 16, 8, 32
WIN = 64
FAR_WIN = 512
PASSES = 1 - -(NODES - WIN) // FAR_WIN
WRAP = WIN + (PASSES - 1) * FAR_WIN
AGGW = 2 * WRAP
E0, E1 = 8, 4
F1 = 2 * D
GE, GSUP = 65536, 65536 // (128 * 4)
GH = 4
EPS = 1e-5
HUGE = 1e30
SPAN = 60.0


class Chain:

    def __init__(self, eng, sem, base=0):
        self.eng, self.sem, self.base, self.n = eng, sem, base, 0

    def __call__(self, ins):
        self.n += 1
        ins.then_inc(self.sem, 1)
        self.eng.wait_ge(self.sem, self.base + self.n)


def bc(ap, dim, n):
    a = ap.unsqueeze(dim)
    shape = list(a.shape)
    shape[dim] = n
    return a.broadcast_to(shape)


def blocks(ap):
    return ap.rearrange("(b p) n -> p b n", p=128)


class Core:

    def __init__(self, nc, ctx, ins, out):
        self.nc, self.ctx, self.i, self.out = nc, ctx, ins, out
        self.live = []
        self.X = self.sb("X", [TP, NT, D])
        self.C = self.sb("C", [TP, NT, D])
        self.CT = self.sb("CT", [128, KB, NODES])
        self.big = self.sb("big", [128, 21504])
        self.ident = self.sb("ident", [128, 128])
        self.same_head = self.sb("same_head", [128, 128])
        self.mix = self.sb("mix", [128, KB, D])
        self.mix_c = self.sb("mix_c", [128, D])
        self.ones = self.sb("ones", [128, 128])
        self.iota = self.sb("iota", [128, 128])
        self.gate = self.sb("gate", [TP, NT, 16])
        self.eps = self.sb("eps", [128, 1])
        self.agg = self.big[:, 0:KB * AGGW].rearrange("p (b n) -> p b n", b=KB)
        self.kv = self.big[0:TP, 0:NT * 514].rearrange("p (t n) -> p t n", t=NT)
        self.sq = self.big[0:TP, 0:NT * D].rearrange("p (t n) -> p t n", t=NT)
        self.wt = self.big[:, 12864:12864 + 8192].rearrange("p (b n) -> p b n", b=KB)
        self.ready = nc.alloc_semaphore("constants_ready")
        self.psum = ctx.enter_context(nc.psum_tensor("psum", [128, 8, 512], F32))
        self.ps = [self.psum[:, i, :] for i in range(8)]
        self.table0 = nc.dram_tensor("table0", (NODES, 2 * D), F32, kind="Internal").ap()
        self.table1 = nc.dram_tensor("table1", (NODES * RELS, D), F32, kind="Internal").ap()
        self.gsrc = nc.dram_tensor("gsrc", (NODES, 20), F32, kind="Internal").ap()
        self.experts = nc.dram_tensor("experts", (E1, NODES, D), F32, kind="Internal").ap()
        self.gdst = nc.dram_tensor("gdst", (NODES, 8), F32, kind="Internal").ap()

    def sb(self, name, shape, dt=F32, ctx=None):
        return (ctx or self.ctx).enter_context(self.nc.sbuf_tensor(name, shape, dt))

    def sem(self, name):
        self.live.append(self.nc.alloc_semaphore(name))
        return self.live[-1]

    def retire(self):
        self.nc.clear_and_free_semaphores(self.live)
        self.live = []
        self.nc.all_engine_barrier()

    def fence(self, eng):
        eng.wait_ge(self.ready, 1)


def stage_constants(c):
    nc = c.nc
    made, x_in = c.sem("const_steps"), c.sem("x_loaded")
    with nc.Block() as block:
        @block.sync
        def _(sp):
            sp.dma_start(c.X[:, :, :], c.i["x"].rearrange("(t p) d -> p t d", p=TP)).then_inc(x_in, 16)
            sp.wait_ge(x_in, 16)

        @block.gpsimd
        def _(pool):
            step = Chain(pool, made)
            step(pool.memset(c.ident[:, :], 0.0))
            step(pool.affine_select(out=c.ident[:, :], in_=c.ident[:, :], compare_op=ALU.not_equal, fill=1.0,
                                    base=0, pattern=[[-1, 128]], channel_multiplier=1))
            step(pool.memset(c.ones[:, :], 1.0))
            step(pool.memset(c.eps[:, :], EPS))
            step(pool.iota(c.iota[:, :], pattern=[[1, 128]], base=0, channel_multiplier=0,
                           allow_small_or_imprecise_dtypes=True))
            step(pool.memset(c.same_head[:, :], 0.0))
            for h in range(128 // HD):
                step(pool.memset(c.same_head[h * HD:(h + 1) * HD, h * HD:(h + 1) * HD], 1.0))
            pool.sem_inc(c.ready, 1)


class Moments:

    def __init__(self, c, tag, ctx):
        self.raw = c.sb(tag + "raw", [TP, NT, 6], ctx=ctx)
        arrays = c.sb(tag + "moments", [TP, 6, NT], ctx=ctx)
        self.mean, self.gap, self.var, self.std, self.rstd, self.shift = (arrays[:, n, :] for n in range(6))

    def variance(self, do):
        even, odd = (self.raw[:, :, n] for n in (1, 4))
        do(do.eng.tensor_tensor(self.mean, even, odd, ALU.add))
        do(do.eng.tensor_scalar(self.mean, self.mean, 0.5, None, ALU.mult))
        do(do.eng.tensor_tensor(self.gap, even, odd, ALU.subtract))
        do(do.eng.tensor_tensor(self.gap, self.gap, self.gap, ALU.mult))
        do(do.eng.tensor_tensor(self.var, self.raw[:, :, 2], self.raw[:, :, 5], ALU.add))
        do(do.eng.scalar_tensor_tensor(out=self.var, in0=self.gap, scalar=D / 4.0, in1=self.var, op0=ALU.mult, op1=ALU.add))
        return do.eng.tensor_scalar(self.var, self.var, 1.0 / D, EPS, ALU.mult, ALU.add)

    def factors(self, do):
        do(do.eng.reciprocal(self.rstd, self.std))
        return do.eng.scalar_tensor_tensor(out=self.shift, in0=self.mean, scalar=-1.0, in1=self.rstd, op0=ALU.mult,
                                           op1=ALU.mult)


def stage_norm(c, tag, groups, keep):
    nc = c.nc
    ctx = ExitStack()
    with ctx:
        m = Moments(c, tag, ctx)
        measured = c.sem(tag + "measured")
        stage = c.sb(tag + "stage", [TP, GROUP, D], ctx=ctx)
        stage_t = c.sb(tag + "stageT", [128, GROUP, KB, TP], ctx=ctx)
        dram = [g for g in groups if g["out"] is None]
        width = sum(g["n"] for g in dram)
        table = c.table0 if width == 512 else c.table1.rearrange("(n r) d -> n (r d)", r=RELS)
        rows = c.sb(tag + "rows", [TP, 2, max(width // 2, 1)], ctx=ctx)
        loads = [(g["w"], g["w_in"]) for g in groups] + [(g["bias"], g["bias_in"]) for g in groups if g["bias"] is not None]
        n_act = sum(g["bias"] is None and i % 2 == 0 for i, g in enumerate(groups))
        n_dve = len(groups) - n_act
        who, seen = [], [0, 0]
        for i, g in enumerate(groups):
            e = 0 if g["bias"] is None and i % 2 == 0 else 1
            seen[e] += 1
            who.append((e, seen[e]))
        w_in, dve_step = c.sem(tag + "w_in"), c.sem(tag + "dve_step")
        var_ready, std_ready, c_ready = c.sem(tag + "var"), c.sem(tag + "std"), c.sem(tag + "c_ready")
        staged, kept = c.sem(tag + "staged"), c.sem(tag + "kept")
        turned, unturned = c.sem(tag + "turned"), c.sem(tag + "unturned")
        t_ready = c.sem(tag + "t_ready")
        prod, ev = c.sem(tag + "prod"), [c.sem(tag + "ev_act"), c.sem(tag + "ev_dve")]
        stored, rows_free = ([c.sem(f"{tag}{n}{h}") for h in range(2)] for n in ("stored", "rows_free"))
        nev = (n_act, n_dve)
        begun = c.sem(tag + "begun_storing")
        banks = 6

        def in_order(eng, first, then):
            first(0, 0)
            with eng.Fori(0, NT // GROUP - 1) as k:
                for u in range(GROUP):
                    first(*((k, u + 1) if u + 1 < GROUP else (k + 1, 0)))
                    then(k, u)
            k = NT // GROUP - 1
            for u in range(GROUP):
                if u + 1 < GROUP:
                    first(k, u + 1)
                then(k, u)

        def turned_bank(u):
            return c.ps[0 if u % 2 == 0 else 7]

        def evac(eng, k, u, mine):
            t = k * GROUP + u
            col = 0
            for i, g in enumerate(groups):
                n = g["n"]
                if who[i][0] == mine:
                    eng.wait_ge(prod, (t + GROUP) * len(groups) + i + 1)
                    src = c.ps[1 + i % banks][0:TP, 0:n]
                    if g["out"] is None:
                        h, off = divmod(col, max(width // 2, 1))
                        if width > 512:
                            eng.wait_ge(rows_free[h], t + 1)
                            dst = rows[:, h, off:off + n]
                        else:
                            eng.wait_ge(rows_free[0], t + 1)
                            dst = rows[:, :, :].rearrange("p a b -> p (a b)")
                    else:
                        dst = g["out"][:, bass.ds(t, 1), 0:n].rearrange("p a n -> p (a n)")
                    c.fence(eng)
                    if mine == 0:
                        ins = eng.activation(dst, src, ACT.Copy)
                    elif g["bias"] is not None:
                        ins = eng.tensor_tensor(dst, src, g["bias"], ALU.add)
                    else:
                        ins = eng.tensor_copy(dst, src)
                    ins.then_inc(ev[mine], 1)
                if g["out"] is None:
                    col += n

        with nc.Block() as block:
            @block.sync
            def _(sp):
                for dst, src in loads:
                    sp.dma_start(dst, src).then_inc(w_in, 16)
                if dram:
                    for h in range(2 if width > 512 else 1):
                        sp.sem_inc(rows_free[h], 1)
                    with sp.Fori(0, NT) as t:
                        for h in range(2 if width > 512 else 1):
                            for e in range(2):
                                last = max([who[i][1] for i in range((len(dram) // 2) * (h + 1) if width > 512 else 1)
                                            if who[i][0] == e], default=0)
                                if last:
                                    sp.wait_ge(ev[e], t * nev[e] + nev[e] + last)
                                    sp.sem_inc(begun, 1)
                            if width > 512:
                                sp.dma_start(table[bass.ds(t * TP, TP), h * (width // 2):(h + 1) * (width // 2)],
                                             rows[:, h, :]).then_inc(stored[h], 16)
                            else:
                                sp.dma_start(table[bass.ds(t * TP, TP), :],
                                             rows[:, :, :].rearrange("p a b -> p (a b)")).then_inc(stored[0], 16)
                            sp.wait_ge(stored[h], 16 * t + 16)
                            sp.sem_inc(rows_free[h], 1)

            @block.vector
            def _(dve):
                dve.sem_inc(unturned, 1)
                if nev[1]:
                    dve.sem_inc(ev[1], nev[1])
                step = Chain(dve, dve_step)
                for t in range(NT):
                    dve.bn_stats(m.raw[:, t, :], c.X[:, t, :]).then_inc(measured, 1)
                dve.wait_ge(measured, NT)
                m.variance(step).then_inc(var_ready, 1)
                dve.wait_ge(std_ready, 1)
                m.factors(step).then_inc(c_ready, 1)
                if loads:
                    dve.wait_ge(w_in, 16 * len(loads))

                def keep_turned(k, u):
                    t = k * GROUP + u
                    psT = turned_bank(u)[:, 0:KB * TP].rearrange("p (b n) -> p b n", b=KB)
                    dve.wait_ge(turned, t + 1 + GROUP)
                    dve.wait_ge(prod, (t + 1) * len(groups))
                    c.fence(dve)
                    dve.tensor_copy(stage_t[:, u, :, :], psT).then_inc(t_ready, 1)
                    c.fence(dve)
                    dve.tensor_copy(c.CT[:, :, bass.ds(t * TP, TP)], psT).then_inc(unturned, 1)
                in_order(dve, keep_turned, lambda k, u: evac(dve, k, u, 1))

            @block.scalar
            def _(act):
                if nev[0]:
                    act.sem_inc(ev[0], nev[0])
                act.wait_ge(var_ready, 1)
                act.activation(m.std, m.var, ACT.Sqrt).then_inc(std_ready, 1)
                act.wait_ge(c_ready, 1)

                def scale(k, u):
                    t = k * GROUP + u
                    act.wait_ge(turned, t + 1)
                    row = c.X[:, bass.ds(t, 1), :].rearrange("p a d -> p (a d)")
                    c.fence(act)
                    act.activation(stage[:, u, :], row, ACT.Identity, scale=m.rstd[:, bass.ds(t, 1)],
                                   bias=m.shift[:, bass.ds(t, 1)]).then_inc(staged, 1)
                    if keep:
                        act.wait_ge(staged, t + 1)
                        c.fence(act)
                        act.activation(c.C[:, bass.ds(t, 1), :].rearrange("p a d -> p (a d)"), stage[:, u, :],
                                       ACT.Copy).then_inc(kept, 1)
                in_order(act, scale, lambda k, u: evac(act, k, u, 0))

            @block.tensor
            def _(pe):
                pe.sem_inc(turned, GROUP)
                if groups:
                    pe.sem_inc(prod, GROUP * len(groups))
                if loads:
                    pe.wait_ge(w_in, 16 * len(loads))

                def turn(k, u):
                    t = k * GROUP + u
                    pe.wait_ge(staged, t + 1)
                    pe.wait_ge(unturned, t + 1 if u == 0 else t)
                    for b in range(KB):
                        last = pe.transpose(turned_bank(u)[:, b * TP:(b + 1) * TP], stage[:, u, b * 128:(b + 1) * 128],
                                            c.ident[0:TP, 0:TP])
                    last.then_inc(turned, 1)

                def products(k, u):
                    t = k * GROUP + u
                    pe.wait_ge(t_ready, t + 1)
                    for i, g in enumerate(groups):
                        if i >= banks:
                            e, n = who[i - banks]
                            pe.wait_ge(ev[e], t * nev[e] + nev[e] + n)
                        else:
                            e, n = who[max(j for j in range(len(groups)) if j % banks == i % banks)]
                            pe.wait_ge(ev[e], t * nev[e] + n)
                        for b in range(KB):
                            last = pe.matmul(c.ps[1 + i % banks][0:TP, 0:g["n"]], stage_t[:, u, b, :],
                                             g["w"][:, b, :], start=(b == 0), stop=(b == KB - 1))
                        last.then_inc(prod, 1)
                in_order(pe, turn, products)


class Attention:
    TURNS = 2 * (NT // GROUP)
    PE_STEPS = {(0, 0): "queries", (0, 3): "read", (1, 4): "project"}
    DVE_STEPS = {(0, 2): "lower", (0, 3): "feature", (0, 6): "guard", (0, 7): "invert0", (1, 1): "invert1",
                 (1, 3): "divide", (1, 6): "add"}

    def __init__(self, c, tag, ctx):
        N = HALVES[0][1]

        def sb(name, shape):
            return c.sb(tag + name, shape, ctx=ctx)
        self.c = c
        self.wq, self.wp, self.bp = sb("wq", [128, KB, D]), sb("wp", [128, KB, D]), sb("bp", [128, KB])
        self.low, self.q = sb("low", [128, KB, N]), sb("q", [128, KB, N])
        self.inv, self.at = sb("inv", [128, KB, N]), sb("at", [128, KB, N])
        self.loaded, self.q_in, self.low_ready, self.exp_ready, self.q_ready = (
            c.sem(tag + n) for n in ("loaded", "q_in", "low", "exp", "q_ready"))
        self.ctx_ready, self.at_ready, self.out_ready, self.halfway, self.added, self.part = (
            c.sem(tag + n) for n in ("ctx", "at", "out", "halfway", "added", "part"))

    def load(self, sp):
        c = self.c
        sp.dma_start(self.wq[:, :, :], blocks(c.i["wq1_t"])).then_inc(self.loaded, 16)
        sp.dma_start(self.wp[:, :, :], blocks(c.i["wproj_t"])).then_inc(self.loaded, 16)
        sp.dma_start(self.bp[:, :], c.i["bproj"]).then_inc(self.loaded, 16)

    def on_tensor(self, pe, step, g, h):
        c, (h0, n), i = self.c, HALVES[h], g * 2 + h
        col = g * GC + h0
        if step == "queries":
            pe.wait_ge(self.added, i + 1)
            for b in range(KB):
                for kb in range(KB):
                    last = pe.matmul(c.ps[b][:, 0:n], self.wq[:, kb, b * 128:(b + 1) * 128],
                                     c.CT[:, kb, bass.ds(col, n)], start=(kb == 0), stop=(kb == KB - 1))
            last.then_inc(self.q_in, 1)
        elif step == "read":
            pe.wait_ge(self.q_ready, i + 1)
            pe.wait_ge(self.at_ready, i + 1)
            for b in range(KB):
                pe.matmul(c.ps[2 + b][:, 0:n], c.mix[:, b, 0:128], self.q[:, b, 0:n], start=True, stop=True)
                last = pe.matmul(c.ps[4 + b][:, 0:n], c.mix[:, b, 128:256], self.q[:, b, 0:n], start=True, stop=True)
            last.then_inc(self.ctx_ready, 1)
        else:
            pe.wait_ge(self.at_ready, i + 2)
            for b in range(KB):
                for kb in range(KB):
                    last = pe.matmul(c.ps[b][:, 0:n], self.wp[:, kb, b * 128:(b + 1) * 128], self.at[:, kb, 0:n],
                                     start=(kb == 0), stop=(kb == KB - 1))
            last.then_inc(self.out_ready, 1)

    def on_scalar(self, act):
        with act.Fori(0, NT // GROUP) as g:
            for h, (h0, n) in enumerate(HALVES):
                act.wait_ge(self.low_ready, g * 2 + h + 1)
                act.activation(self.low[:, :, 0:n], self.low[:, :, 0:n], ACT.Exp).then_inc(self.exp_ready, 1)

    def on_vector(self, dve, step, g, h, before):
        c, (h0, n), i = self.c, HALVES[h], g * 2 + h
        col = g * GC + h0
        low, q, inv, at = (a[:, :, 0:n] for a in (self.low, self.q, self.inv, self.at))
        if step == "lower":
            dve.wait_ge(self.q_in, i + 1)
            dve.tensor_scalar(low, c.psum[:, 0:2, 0:n], 0.0, None, ALU.min).then_inc(self.low_ready, 1)
        elif step == "feature":
            dve.wait_ge(self.exp_ready, i + 1)
            dve.scalar_tensor_tensor(out=q, in0=c.psum[:, 0:2, 0:n], scalar=0.0, in1=low, op0=ALU.max,
                                     op1=ALU.add).then_inc(self.q_ready, 1)
        elif step == "guard":
            dve.wait_ge(self.ctx_ready, i + 1)
            dve.tensor_scalar(inv, c.psum[:, 4:6, 0:n], 1e-6, None, ALU.max).then_inc(self.part, 1)
        elif step in ("invert0", "invert1"):
            b = int(step[-1])
            dve.wait_ge(self.part, i * 3 + 1)
            dve.reciprocal(inv[:, b, :], inv[:, b, :]).then_inc(self.part, 1)
        elif step == "divide":
            dve.wait_ge(self.part, i * 3 + 3)
            dve.tensor_tensor(at, c.psum[:, 2:4, 0:n], inv, ALU.mult).then_inc(self.at_ready, 1)
        else:
            dve.wait_ge(self.out_ready, i + 1)
            before()
            for b in range(KB):
                cols = c.agg[:, b, bass.ds(col, n)]
                c.fence(dve)
                ins = dve.scalar_tensor_tensor(out=cols, in0=c.ps[b][:, 0:n], scalar=self.bp[:, b:b + 1], in1=cols,
                                               op0=ALU.add, op1=ALU.add)
                if b < KB - 1:
                    ins.then_inc(self.halfway, 1)
            ins.then_inc(self.added, 1)
            dve.wait_ge(self.added, i + 2)
            dve.wait_ge(self.halfway, i + 1)


def stage_edges(c, tag, relational):
    nc = c.nc
    ctx = ExitStack()
    W = D if relational else 2 * D
    BODY = 2 * SUP
    NB = NET // BODY
    with ctx:
        def sb(name, shape, dt=F32):
            return c.sb(tag + name, shape, dt, ctx=ctx)

        base_i, base_f = sb("base_i", [128, NSUP], I32), sb("base_f", [128, NSUP])
        src_i, rel = sb("src_i", [128, NET], I32), sb("rel", [128, NET])
        dst_i, neg = sb("dst_i", [128, NET], I32), sb("neg", [128, NET])
        far, far_i, most = sb("far", [1, 1]), sb("far_i", [1, 1], I32), sb("most", [128, 1])
        idx = sb("idx", [128, 2, SUP], I32)
        G = c.big[:, KB * AGGW:KB * AGGW + 2 * SUP * W].rearrange("p (j q w) -> p j q w", j=2, q=SUP)
        near_hot = sb("near_hot", [128, 2, WIN])
        far_hot = c.big[:, KB * AGGW + 2 * SUP * 2 * D + 2 * ES:][:, 0:2 * FAR_WIN].rearrange("p (j n) -> p j n", j=2)

        wide_iota = c.big[:, KB * AGGW + 2 * SUP * 2 * D + 2 * ES + 2 * FAR_WIN:][:, 0:FAR_WIN]

        def window(s, j):
            if s is sems[0]:
                return WIN, near_hot, c.ps[6 + j].rearrange("p (b n) -> p b n", b=KB)[:, :, 0:WIN]
            return FAR_WIN, far_hot, c.psum[:, 6:6 + KB, 0:FAR_WIN]

        loads = [(base_i[:, :], c.i["dst_base"]), (src_i[:, :], c.i["src_t"]), (dst_i[:, :], c.i["dst_t"])]
        if relational:
            type_i, norm = sb("type_i", [128, NET], I32), sb("norm", [128, NET])
            loads += [(type_i[:, :], c.i["type_t"]), (norm[:, :], c.i["norm_t"])]
        else:
            wb_hi, wb_lo = sb("wb_hi", [128, W], F32R), sb("wb_lo", [128, W], F32R)
            w2_hi, w2_lo = sb("w2_hi", [128, KB, D], F32R), sb("w2_lo", [128, KB, D], F32R)
            b2_parts, two = sb("b2_parts", [128, D], F32R), sb("two", [128, 128], F32R)
            parts = sb("attr_parts", [128, 2, ES], F32R)
            attr = c.big[:, KB * AGGW + 2 * SUP * W:][:, 0:2 * ES].rearrange("p (j e) -> p j e", j=2)
            Z, gate = sb("Z", [128, 2, W]), sb("gate", [128, 2, D])
            hT_hi, hT_lo = sb("hT_hi", [128, 2, KB, 128], F32R), sb("hT_lo", [128, 2, KB, 128], F32R)
            msg = sb("msg", [128, 2, D])
            w2_in = Z[:, 0, :].rearrange("p (b n) -> p b n", b=KB)
            loads += [(Z[0:DE, 1, :], c.i["edge_w0"]), (Z[DE:2 * DE, 1, :], c.i["edge_w0"]), (w2_in, blocks(c.i["w2_0"])),
                      (gate[:, 0, :], c.i["b2_0"])]
        attention = Attention(c, tag + "t_", ctx) if relational else None
        loaded, prep, maxed, turned, flag, zeroed, first_done, cut = (
            c.sem(tag + n) for n in ("loaded", "prep", "maxed", "max_turned", "flag", "zeroed", "first_done", "cut"))
        names = ("idx_ready", "G_in0", "G_in1", "hot_ready", "hot_used", "added", "attr_in0",
                 "attr_in1", "attr_rounded", "attr_ready", "z_ready", "zs_ready", "z_turned",
                 "h_rounded", "h_ready", "gate_ready", "core_ready", "msg_ready", "shifted")
        if relational:
            names = ("idx_ready", "G_in0", "G_in1", "hot_ready", "hot_used", "added", "shifted")
        sems = [{n: c.sem(f"{tag}{n}_{j}") for n in names} for j in range(2)]
        begun_adding, begun_gathering = c.sem(tag + "begun_adding"), c.sem(tag + "begun_gathering")
        table = c.table1 if relational else c.table0

        def loop(step):
            def whole(eng):
                for u in range(-3, BODY):
                    step(0, u)
                with eng.Fori(1, NB - 1) as k:
                    for u in range(BODY):
                        step(k, u)
                for u in range(BODY + 3):
                    step(NB - 1, u)
            return whole

        def loop_beside(step, aside):
            PER = (NB - 2) // Attention.TURNS
            def whole(eng):
                for u in range(-3, BODY):
                    step(0, u)
                with eng.Fori(0, NT // GROUP) as g:
                    for h in range(2):
                        k = g * (2 * PER) + (h * PER + 1)
                        for body in range(2):
                            for u in range(BODY):
                                step(k + body, u)
                                aside(eng, body, u, g, h, k + body)
                        with eng.Fori(2, PER) as r:
                            for u in range(BODY):
                                step(k + r, u)
                with eng.Fori(1 + PER * Attention.TURNS, NB - 1) as k:
                    for u in range(BODY):
                        step(k, u)
                for u in range(BODY + 3):
                    step(NB - 1, u)
            return whole

        def at(k, u):
            k, u = k + u // BODY, u % BODY
            if isinstance(k, int) and not 0 <= k < NB:
                return None
            return k, u, k * BODY + u, k * 2 + u // SUP, u // SUP, u % SUP

        def sp_pass(sp, s, p):
            if not relational:
                with sp.Fori(0, NSUP // 2) as k:
                    for j in range(2):
                        sp.wait_ge(s["attr_ready"], p * NSUP + k * 2 + j + 1)
                        for half in range(2):
                            c.fence(sp)
                            sp.dma_start(attr[half * DE:(half + 1) * DE, j, :],
                                         c.i["attr_t"][:, bass.ds((k * 2 + j) * ES, ES)]).then_inc(s[f"attr_in{j}"], 16)

        def pool_pass(pool, s, p):
            with pool.Fori(0, NSUP // 2) as k:
                for j in range(2):
                    pool.wait_ge(s["idx_ready"], p * NSUP + k * 2 + j + 1)
                    if relational:
                        pool.wait_ge(s["added"], p * NSUP + k * 2 + j + 1)
                    else:
                        pool.wait_ge(s["zs_ready"], p * NET + (k * 2 + j) * SUP + SUP)
                    pool.sem_inc(begun_gathering, 1)
                    for q in range(SUP):
                        pool.indirect_dma_start(G[:, j, q, :], None, table,
                                                bass.IndirectOffsetOnAxis(idx[:, j, q:q + 1], 0)).then_inc(
                            s[f"G_in{j}"], 16)

        def pe_pass(pe, s, p):
            def edge_part(a):
                k, u, i, sp_, j, q = a
                if q == 0:
                    pe.wait_ge(s["attr_ready"], p * NSUP + sp_ + 3)
                pe.wait_ge(s["zs_ready"], p * NET + i + 2 * SUP - 1)
                tile = parts[:, j, q * ET:(q + 1) * ET]
                pe.matmul(c.ps[u % 2], tile, wb_hi[:, :], start=True, stop=False)
                pe.matmul(c.ps[u % 2], tile, wb_lo[:, :], start=False, stop=True).then_inc(s["z_ready"], 1)

            def turn(a):
                k, u, i, sp_, j, q = a
                pe.wait_ge(s["zs_ready"], p * NET + i + 2 * SUP + 1)
                pe.wait_ge(s["h_ready"], p * NET + i + 1)
                for b in range(KB):
                    last = pe.transpose(c.ps[2 + u % 2][:, b * 128:(b + 1) * 128], Z[:, u % 2, b * 128:(b + 1) * 128], c.ident[:, :])
                last.then_inc(s["z_turned"], 1)

            def core(a):
                k, u, i, sp_, j, q = a
                pe.wait_ge(s["h_ready"], p * NET + i + 3)
                pe.wait_ge(s["msg_ready"], p * NET + i + 1)
                pe.matmul(c.ps[4 + u % 2][:, 0:D], two[:, :], b2_parts[:, :], start=True, stop=False)
                for b in range(KB):
                    hi, lo = hT_hi[:, u % 2, b, :], hT_lo[:, u % 2, b, :]
                    for x, y in ((hi, w2_hi), (hi, w2_lo), (lo, w2_hi)):
                        last = pe.matmul(c.ps[4 + u % 2][:, 0:D], x, y[:, b, :], start=False, stop=b == KB - 1 and x is lo)
                last.then_inc(s["core_ready"], 1)

            def total(a):
                k, u, i, sp_, j, q = a
                pe.wait_ge(s["hot_ready"], p * NET + i + 1)
                if relational:
                    if q == 0:
                        pe.wait_ge(s[f"G_in{j}"], (p * (NSUP // 2) + k + 1) * 64)
                else:
                    pe.wait_ge(s["msg_ready"], p * NET + i + 3)
                if q == 0:
                    pe.wait_ge(s["added"], p * NSUP + sp_ + (1 if s is sems[0] else 2))
                _, onehot, acc = window(s, j)
                for b in range(KB):
                    lhs = G[:, j, q, b * 128:(b + 1) * 128] if relational else msg[:, u % 2, b * 128:(b + 1) * 128]
                    last = pe.matmul(acc[:, b, :], lhs, onehot[:, u % 2, :], start=q == 0 and (b == 0 or s is sems[1]),
                                     stop=q == SUP - 1, skip_group_check=True)
                last.then_inc(s["hot_used"], 1)

            def step(k, u):
                for ahead, part in ((1, turn), (-1 if relational else -2, total), (0, core), (3, edge_part)):
                    a = at(k, u + ahead)
                    if a and (part is total or not relational):
                        part(a)

            def aside(pe, body, u, g, h, k):
                if (body, u) in Attention.PE_STEPS:
                    attention.on_tensor(pe, Attention.PE_STEPS[body, u], g, h)
            (loop_beside(step, aside) if relational and s is sems[0] else loop(step))(pe)

        def act_pass(act, s, p):
            def step(k, u):
                a = at(k, u + 1)
                if not a:
                    return
                k, u, i, sp_, j, q = a
                act.wait_ge(s["z_turned"], p * NET + i + 3)
                act.wait_ge(s["core_ready"], p * NET + i + 1)
                act.activation(hT_hi[:, u % 2, :, :].rearrange("p b n -> p (b n)"),
                               c.ps[2 + u % 2][:, 0:KB * 128], ACT.Relu).then_inc(s["h_rounded"], 1)
                act.wait_ge(s["zs_ready"], p * NET + i + 2 * SUP + 1)
                act.wait_ge(s["msg_ready"], p * NET + i + 1)
                act.activation(gate[:, u % 2, :], Z[:, u % 2, D:2 * D], ACT.Sigmoid).then_inc(s["gate_ready"], 1)
                if q == SUP - 1 and not (isinstance(k, int) and sp_ + 2 >= NSUP):
                    rounded(sp_ + 2, j, k + 1)

            def rounded(sup, j, k):
                act.wait_ge(s["z_ready"], p * NET + sup * SUP + SUP)
                act.wait_ge(s[f"attr_in{j}"], (p * (NSUP // 2) + k + 1) * 32)
                act.activation(parts[:, j, :], attr[:, j, :], ACT.Copy).then_inc(s["attr_rounded"], 1)
            if not relational:
                rounded(0, 0, 0)
                rounded(1, 1, 0)
                loop(step)(act)

        def dve_pass(dve, s, p):
            def indices(sup, j, uses):
                if relational and not (isinstance(uses, int) and uses == 0):
                    dve.wait_ge(s[f"G_in{j}"], (p * (NSUP // 2) + uses) * 64)
                c.fence(dve)
                dve.tensor_copy(idx[:, j, :], src_i[:, bass.ds(sup * SUP, SUP)]).then_inc(s["idx_ready"], 1)

            def whole_row(a):
                k, u, i, sp_, j, q = a
                dve.wait_ge(s["z_ready"], p * NET + i + 2 * SUP + 1)
                if q == 0:
                    dve.wait_ge(s[f"G_in{j}"], (p * (NSUP // 2) + k + 1) * 64)
                dve.wait_ge(s["z_turned"], p * NET + i + 1)
                dve.wait_ge(s["gate_ready"], p * NET + i + 1)
                dve.tensor_tensor(Z[:, u % 2, :], c.ps[u % 2], G[:, j, q, :], ALU.add).then_inc(s["zs_ready"], 1)
                if q == SUP - 1:
                    nxt = at(k, u + BODY)
                    if nxt and not (isinstance(k, int) and sp_ + 2 >= NSUP):
                        indices(sp_ + 2, j, k + 1)

            def attr_lo(sup, j):
                dve.wait_ge(s["attr_rounded"], p * NSUP + sup + 1)
                dve.tensor_tensor(parts[DE:2 * DE, j, :], attr[DE:2 * DE, j, :], parts[DE:2 * DE, j, :].bitcast(F32),
                                  ALU.subtract).then_inc(s["attr_ready"], 1)

            def hidden_lo(a):
                k, u, i, sp_, j, q = a
                dve.wait_ge(s["h_rounded"], p * NET + i + 1)
                dve.wait_ge(s["core_ready"], p * NET + i + 1)
                dve.scalar_tensor_tensor(out=hT_lo[:, u % 2, :, :].rearrange("p b n -> p (b n)"),
                                         in0=c.ps[2 + u % 2][:, 0:KB * 128], scalar=0.0,
                                         in1=hT_hi[:, u % 2, :, :].rearrange("p b n -> p (b n)").bitcast(F32),
                                         op0=ALU.max, op1=ALU.subtract).then_inc(s["h_ready"], 1)

            def hot(a):
                k, u, i, sp_, j, q = a
                dve.wait_ge(s["hot_used"], p * NET + i + 1)
                width, onehot, _ = window(s, j)
                c.fence(dve)
                if relational:
                    dve.tensor_scalar(onehot[:, u % 2, :], wide_iota[:, 0:width], rel[:, bass.ds(i, 1)],
                                      norm[:, bass.ds(i, 1)], ALU.is_equal, ALU.mult).then_inc(s["hot_ready"], 1)
                else:
                    dve.tensor_scalar(onehot[:, u % 2, :], wide_iota[:, 0:width], rel[:, bass.ds(i, 1)], None,
                                      ALU.is_equal).then_inc(s["hot_ready"], 1)

            def message(a):
                k, u, i, sp_, j, q = a
                dve.wait_ge(s["gate_ready"], p * NET + i + 3)
                dve.wait_ge(s["core_ready"], p * NET + i + 3)
                dve.wait_ge(s["hot_used"], p * NET + i + 1)
                dve.tensor_tensor(msg[:, u % 2, :], c.ps[4 + u % 2][:, 0:D], gate[:, u % 2, :], ALU.mult).then_inc(
                    s["msg_ready"], 1)

            def add_window(a):
                k, u, i, sp_, j, q = a
                dve.wait_ge(s["hot_used"], p * NET + i + 3)
                dve.wait_ge(s["added"], p * NSUP + sp_ + 2)
                dve.sem_inc(begun_adding, 1)
                at_node = dve.value_load(base_i[0:1, bass.ds(sp_, 1)], min_val=0, max_val=NODES - 1)
                width, _, acc = window(s, j)
                cols = c.agg[:, :, bass.ds(at_node + (0 if s is sems[0] else WIN + p * FAR_WIN), width)]
                c.fence(dve)
                dve.tensor_tensor(cols, cols, acc, ALU.add).then_inc(s["added"], 1)

            def step(k, u):
                if relational:
                    a = at(k, u)
                    if a:
                        hot(a)
                        if a[5] == 0 and not (isinstance(a[0], int) and a[3] + 1 >= NSUP):
                            indices(a[3] + 1, 1 - a[4], a[0] + a[4])
                else:
                    for ahead, part in ((-1, message), (2, whole_row), (-1, hot), (1, hidden_lo)):
                        a = at(k, u + ahead)
                        if a:
                            part(a)
                    a = at(k, u)
                    if a and a[5] == SUP - 1 and not (isinstance(a[0], int) and a[3] + 2 >= NSUP):
                        attr_lo(a[3] + 2, a[4])
                a = at(k, u - (2 if relational else 3))
                if a and a[5] == SUP - 1:
                    add_window(a)

            indices(0, 0, 0)
            if not relational:
                indices(1, 1, 0)
                attr_lo(0, 0)
                attr_lo(1, 1)

            def aside(dve, body, u, g, h, k):
                def windows_added():
                    assert u > SUP
                    dve.wait_ge(s["added"], k * 2 + 3)
                if (body, u) in Attention.DVE_STEPS:
                    attention.on_vector(dve, Attention.DVE_STEPS[body, u], g, h, windows_added)
            (loop_beside(step, aside) if relational and s is sems[0] else loop(step))(dve)

        def both(eng, one):
            one(eng, sems[0], 0)
            eng.wait_ge(flag, 1)
            more = eng.value_load(far_i[0:1, 0:1], min_val=0, max_val=1)
            with eng.If(more > 0):
                eng.wait_ge(first_done, 1)
                with eng.Fori(0, PASSES - 1) as p:
                    one(eng, sems[1], p)

        with nc.Block() as block:
            @block.sync
            def _(sp):
                for dst, src in loads:
                    sp.dma_start(dst, src).then_inc(loaded, 16)
                if relational:
                    attention.load(sp)
                both(sp, sp_pass)

            @block.gpsimd
            def _(pool):
                both(pool, pool_pass)

            @block.vector
            def _(dve):
                for s in sems:
                    dve.sem_inc(s["added"], 2)
                    if not relational:
                        dve.sem_inc(s["zs_ready"], 2 * SUP)
                        dve.sem_inc(s["msg_ready"], 2)
                        dve.sem_inc(s["h_ready"], 2)
                        dve.sem_inc(s["attr_ready"], 2)
                dve.memset(c.agg, 0.0).then_inc(zeroed, 1)
                dve.wait_ge(loaded, 16 * len(loads))
                if relational:
                    dve.wait_ge(attention.loaded, 48)
                do = Chain(dve, prep)
                for n in range(FAR_WIN // 128):
                    do(dve.tensor_scalar(wide_iota[:, n * 128:(n + 1) * 128], c.iota[:, :], float(n * 128), None, ALU.add))
                do(dve.tensor_copy(base_f[:, :], base_i[:, :]))
                do(dve.tensor_copy(rel[:, :], dst_i[:, :]))
                rel3 = rel[:, :].rearrange("p (s q) -> p s q", q=SUP)
                do(dve.tensor_tensor(rel3, rel3, bc(base_f[:, :], 2, SUP), ALU.subtract))
                do(dve.tensor_scalar(neg[:, :], rel[:, :], 0.0, float(WRAP), ALU.is_lt, ALU.mult))
                do(dve.tensor_tensor(rel[:, :], rel[:, :], neg[:, :], ALU.add))
                if relational:
                    do(dve.tensor_scalar(neg[:, :], src_i[:, :], float(RELS), None, ALU.mult))
                    do(dve.tensor_tensor(src_i[:, :], neg[:, :], type_i[:, :], ALU.add))
                else:
                    for hi, lo, w in ((wb_hi[:, :], wb_lo[:, :], Z[:, 1, :]), (w2_hi[:, :, :], w2_lo[:, :, :], w2_in)):
                        do(dve.tensor_copy(hi, w))
                        do(dve.tensor_tensor(lo, w, hi.bitcast(F32), ALU.subtract))
                    do(dve.tensor_copy(b2_parts[:, :], gate[:, 0, :]))
                    low = b2_parts[32:64, :]
                    do(dve.tensor_tensor(low, gate[32:64, 0, :], low.bitcast(F32), ALU.subtract))
                    do(dve.memset(two[:, :].bitcast(F32), 0.0))
                    for row in (0, 32):
                        do(dve.memset(two[row:row + 1, :].bitcast(F32), 1.0))
                    dve.sem_inc(cut, 1)
                dve.tensor_reduce(most[:, :], rel[:, :], AX.X, ALU.max).then_inc(maxed, 1)
                dve.wait_ge(turned, 1)
                do(dve.tensor_reduce(far[:, :], c.ps[7][0:1, 0:128], AX.X, ALU.max))
                do(dve.tensor_scalar(far[:, :], far[:, :], float(WIN), None, ALU.is_ge))
                dve.tensor_copy(far_i[:, :], far[:, :]).then_inc(flag, 1)
                dve.wait_ge(zeroed, 1)

                def one(dve, s, p):
                    dve_pass(dve, s, p)
                    dve.wait_ge(s["added"], (p + 1) * NSUP + 2)
                    if s is sems[0]:
                        dve.sem_inc(first_done, 1)
                    dve.tensor_scalar(rel[:, :], rel[:, :], -float(WIN if s is sems[0] else FAR_WIN), None,
                                      ALU.add).then_inc(s["shifted"], 1)
                    dve.wait_ge(s["shifted"], p + 1)
                both(dve, one)

            @block.scalar
            def _(act):
                if not relational:
                    for s in sems:
                        act.sem_inc(s["gate_ready"], 2)
                    act.wait_ge(cut, 1)
                else:
                    attention.on_scalar(act)
                both(act, act_pass)

            @block.tensor
            def _(pe):
                for s in sems:
                    pe.sem_inc(s["hot_used"], 2)
                    if not relational:
                        pe.sem_inc(s["z_ready"], 2 * SUP)
                        pe.sem_inc(s["z_turned"], 2)
                        pe.sem_inc(s["core_ready"], 2)
                pe.wait_ge(maxed, 1)
                pe.transpose(c.ps[7][0:1, 0:128], most[:, :], c.ident[:, :]).then_inc(turned, 1)
                pe.wait_ge(loaded, 16 * len(loads))
                if relational:
                    pe.sem_inc(attention.added, 1)
                    pe.sem_inc(attention.at_ready, 1)
                    pe.wait_ge(attention.loaded, 48)
                else:
                    pe.wait_ge(cut, 1)
                both(pe, pe_pass)


def stage_context(c, tag, softmax):
    nc = c.nc
    ctx = ExitStack()
    with ctx:
        def sb(name, shape, dt=F32):
            return c.sb(tag + name, shape, dt, ctx=ctx)

        stage = sb("stage", [TP, GROUP, D])
        k_top, top = sb("k_top", [TP, D]), sb("top", [128, KB])
        diag, top_all = sb("diag", [128, KB, 128]), sb("top_all", [TP, D])
        lam, lam_sq = sb("lam", [128, KB, D]), sb("lam_sq", [128, KB, D])
        st = sb("stats", [128, 8, KB])
        gb, wqT, bq = sb("gb", [128, 2, KB]), sb("wqT", [128, KB, D]), sb("bq", [128, KB, TP])
        K, V1 = c.kv[:, :, 0:D], c.kv[:, :, D:2 * D + 1]
        tmp = c.big[0:TP, 12864:12864 + NT * D].rearrange("p (t d) -> p t d", t=NT)
        loaded, do_dve = c.sem(tag + "loaded"), c.sem(tag + "dve_step")
        top_ready, turned, diag_ready, spread = (c.sem(tag + n) for n in ("top", "turned", "diag", "spread"))
        low_ready, exp_ready, k_ready = (c.sem(tag + n) for n in ("low", "exp", "k_ready"))
        staged, unstaged, summed = (c.sem(tag + n) for n in ("staged", "unstaged", "summed"))
        var_ready, std_ready, bn_ready, mixed = (c.sem(tag + n) for n in ("var", "std", "bn", "mixed"))

        with nc.Block() as block:
            @block.sync
            def _(sp):
                if softmax:
                    sp.dma_start(gb[:, 0, :], c.i["mix0_gamma"]).then_inc(loaded, 16)
                    sp.dma_start(gb[:, 1, :], c.i["mix0_beta"]).then_inc(loaded, 16)
                    sp.dma_start(wqT[:, :, :], blocks(c.i["wq0_t"])).then_inc(loaded, 16)
                    sp.dma_start(bq[:, :, :], blocks(c.i["bq0"])).then_inc(loaded, 16)

            @block.vector
            def _(dve):
                do = Chain(dve, do_dve)
                do(dve.memset(c.kv[:, :, 2 * D:2 * D + 2], 1.0))
                if softmax:
                    dve.tensor_reduce(k_top[:, :], K.rearrange("p t d -> p d t"), AX.X, ALU.max).then_inc(top_ready, 1)
                    dve.wait_ge(turned, 1)
                    do(dve.tensor_reduce(top[:, :], c.ps[0][:, 0:KB * TP].rearrange("p (b n) -> p b n", b=KB),
                                         AX.X, ALU.max))
                    for b in range(KB):
                        dve.tensor_scalar(diag[:, b, :], c.ident[:, :], top[:, b:b + 1], None,
                                          ALU.mult).then_inc(diag_ready, 1)
                    dve.wait_ge(spread, 1)
                    do(dve.tensor_copy(top_all[:, :], c.ps[1][0:TP, 0:D]))
                    dve.tensor_tensor(K, K, bc(top_all[:, :], 1, NT), ALU.subtract).then_inc(k_ready, 1)
                else:
                    dve.tensor_scalar(tmp, K, 0.0, None, ALU.min).then_inc(low_ready, 1)
                    dve.wait_ge(exp_ready, 1)
                    dve.scalar_tensor_tensor(out=K, in0=K, scalar=0.0, in1=tmp, op0=ALU.max,
                                             op1=ALU.add).then_inc(k_ready, 1)
                dve.wait_ge(summed, 1)
                sums = c.psum[:, 2:4, 0:D]
                if softmax:
                    dve.wait_ge(loaded, 64)
                    mean, var, std, rstd, sc, rs = (st[:, n, :] for n in range(6))
                    do(dve.reciprocal(rs, c.psum[:, 2:4, D:D + 1].rearrange("p b o -> p (b o)")))
                    do(dve.tensor_tensor(lam[:, :, :], sums, bc(rs, 2, D), ALU.mult))
                    do(dve.tensor_reduce(mean, lam[:, :, :], AX.X, ALU.add))
                    do(dve.tensor_scalar(mean, mean, 1.0 / D, None, ALU.mult))
                    do(dve.tensor_tensor(lam[:, :, :], lam[:, :, :], bc(mean, 2, D), ALU.subtract))
                    do(dve.tensor_tensor(lam_sq[:, :, :], lam[:, :, :], lam[:, :, :], ALU.mult))
                    do(dve.tensor_reduce(var, lam_sq[:, :, :], AX.X, ALU.add))
                    dve.tensor_scalar(var, var, 1.0 / D, EPS, ALU.mult, ALU.add).then_inc(var_ready, 1)
                    dve.wait_ge(std_ready, 1)
                    do(dve.reciprocal(rstd, std))
                    do(dve.tensor_tensor(sc, rstd, gb[:, 0, :], ALU.mult))
                    for b in range(KB):
                        dve.tensor_scalar(lam[:, b, :], lam[:, b, :], sc[:, b:b + 1], gb[:, 1, b:b + 1], ALU.mult,
                                          ALU.add).then_inc(bn_ready, 1)
                    dve.wait_ge(mixed, 1)
                    do(dve.tensor_copy(c.mix[:, :, :], c.psum[:, 4:6, 0:D]))
                    do(dve.tensor_copy(c.mix_c[0:TP, :], c.ps[6][0:TP, 0:D]))
                else:
                    for b in range(KB):
                        do(dve.tensor_tensor(c.mix[:, b, 0:128], c.psum[:, 2 + b, b * 128:(b + 1) * 128],
                                             c.same_head[:, :], ALU.mult))
                        do(dve.tensor_copy(st[:, b, 0:1], c.psum[:, 2 + b, D:D + 1]))
                        do(dve.tensor_scalar(c.mix[:, b, 128:256], c.same_head[:, :], st[:, b, 0:1], None, ALU.mult))

            @block.scalar
            def _(act):
                if not softmax:
                    act.wait_ge(low_ready, 1)
                    act.activation(tmp, tmp, ACT.Exp).then_inc(exp_ready, 1)
                act.wait_ge(k_ready, 1)
                with act.Fori(0, NT // GROUP) as k:
                    for u in range(GROUP):
                        t = k * GROUP + u
                        act.wait_ge(unstaged, t + 1)
                        c.fence(act)
                        act.activation(stage[:, u, :], c.kv[:, bass.ds(t, 1), 0:D].rearrange("p a d -> p (a d)"),
                                       ACT.Exp if softmax else ACT.Copy).then_inc(staged, 1)
                if softmax:
                    act.wait_ge(var_ready, 1)
                    act.activation(st[:, 2, :], st[:, 1, :], ACT.Sqrt).then_inc(std_ready, 1)

            @block.tensor
            def _(pe):
                pe.sem_inc(unstaged, GROUP)
                if softmax:
                    pe.wait_ge(top_ready, 1)
                    for b in range(KB):
                        last = pe.transpose(c.ps[0][:, b * TP:(b + 1) * TP], k_top[:, b * 128:(b + 1) * 128],
                                            c.ident[0:TP, 0:TP])
                    last.then_inc(turned, 1)
                    pe.wait_ge(diag_ready, KB)
                    for b in range(KB):
                        last = pe.matmul(c.ps[1][0:TP, b * 128:(b + 1) * 128], c.ones[:, 0:TP], diag[:, b, :],
                                         start=True, stop=True)
                    last.then_inc(spread, 1)
                pe.wait_ge(do_dve, 1)

                def group(k, first=False, final=False):
                    for u in range(GROUP):
                        t = k * GROUP + u
                        pe.wait_ge(staged, t + 1)
                        for b in range(KB):
                            last = pe.matmul(c.ps[2 + b][:, 0:D + 1], stage[:, u, b * 128:(b + 1) * 128],
                                             V1[:, bass.ds(t, 1), :].rearrange("p a n -> p (a n)"),
                                             start=first and u == 0, stop=final and u == GROUP - 1)
                        last.then_inc(unstaged, 1)
                group(0, first=True)
                with pe.Fori(1, NT // GROUP - 1) as k:
                    group(k)
                group(NT // GROUP - 1, final=True)
                pe.wait_ge(unstaged, NT + GROUP)
                pe.sem_inc(summed, 1)
                if softmax:
                    pe.wait_ge(bn_ready, KB)
                    pe.wait_ge(loaded, 64)
                    for kb in range(KB):
                        for b in range(KB):
                            pe.matmul(c.ps[4 + kb][:, 0:D], wqT[:, b, kb * 128:(kb + 1) * 128], lam[:, b, :],
                                      start=(b == 0), stop=(b == KB - 1))
                    for b in range(KB):
                        last = pe.matmul(c.ps[6][0:TP, 0:D], bq[:, b, :], lam[:, b, :], start=(b == 0),
                                         stop=(b == KB - 1))
                    last.then_inc(mixed, 1)


def stage_sum(c, tag, first):
    nc = c.nc
    ctx = ExitStack()
    with ctx:
        stage = c.sb(tag + "stage", [128, GROUP, 2 * KB, TP], ctx=ctx)
        m = Moments(c, tag, ctx)
        gb = c.sb(tag + "gb", [TP, 2, D], ctx=ctx)
        factors, scaled, measured = c.sem(tag + "factors"), c.sem(tag + "scaled"), c.sem(tag + "measured")
        folded, staged, turned, unturned, step_ready, var_ready, std_ready, loaded = (
            c.sem(tag + n) for n in ("folded", "staged", "turned", "unturned", "step", "var", "std", "loaded"))
        with nc.Block() as block:
            @block.sync
            def _(sp):
                if first:
                    sp.dma_start(gb[:, 0, :], c.i["gnn0_gamma"]).then_inc(loaded, 16)
                    sp.dma_start(gb[:, 1, :], c.i["gnn0_beta"]).then_inc(loaded, 16)

            @block.scalar
            def _(act):
                act.wait_ge(folded, 1)
                with act.Fori(0, NT // GROUP) as k:
                    for u in range(GROUP):
                        t = k * GROUP + u
                        act.wait_ge(turned, t + 1)
                        c.fence(act)
                        act.activation(stage[:, u, 0:KB, :], c.agg[:, :, bass.ds(t * TP, TP)], ACT.Copy).then_inc(staged, 1)
                        if first:
                            c.fence(act)
                            act.activation(stage[:, u, KB:2 * KB, :], c.CT[:, :, bass.ds(t * TP, TP)],
                                           ACT.Copy).then_inc(staged, 1)
                if first:
                    act.wait_ge(var_ready, 1)
                    act.activation(m.std, m.var, ACT.Sqrt).then_inc(std_ready, 1)
                    act.wait_ge(factors, 1)
                    for t in range(NT):
                        act.activation(c.C[:, t, :], c.C[:, t, :], ACT.Identity, scale=m.rstd[:, t:t + 1],
                                       bias=m.shift[:, t:t + 1]).then_inc(scaled, 1)

            @block.tensor
            def _(pe):
                pe.sem_inc(turned, GROUP)
                with pe.Fori(0, NT // GROUP) as k:
                    for u in range(GROUP):
                        t = k * GROUP + u
                        pe.wait_ge(staged, (t + 1) * (1 + first))
                        pe.wait_ge(unturned, (t if u == 0 else t - 1) * (1 + first) + 1)
                        for b in range(KB):
                            last = pe.transpose(c.ps[u % 2 * 2][0:TP, b * 128:(b + 1) * 128], stage[:, u, b, :], c.ident[:, :])
                        if first:
                            for b in range(KB):
                                last = pe.matmul(c.ps[u % 2 * 2 + 1][0:TP, 0:D], stage[:, u, KB + b, :], c.mix[:, b, :],
                                                 start=(b == 0), stop=(b == KB - 1))
                        last.then_inc(turned, 1)

            @block.vector
            def _(dve):
                cols = c.agg[:, :, 0:NODES]
                dve.tensor_tensor(cols, cols, c.agg[:, :, WRAP:WRAP + NODES], ALU.add).then_inc(folded, 1)
                dve.sem_inc(unturned, 1)
                with dve.Fori(0, NT // GROUP) as k:
                    for u in range(GROUP):
                        t = k * GROUP + u
                        dve.wait_ge(turned, t + 1 + GROUP)
                        pairs = ((c.ps[u % 2 * 2], c.C if first else c.X),)
                        if first:
                            pairs += ((c.ps[u % 2 * 2 + 1], c.X),)
                        for src, dst in pairs:
                            tile = dst[:, bass.ds(t, 1), :].rearrange("p a d -> p (a d)")
                            c.fence(dve)
                            dve.tensor_tensor(tile, tile, src[0:TP, 0:D], ALU.add).then_inc(unturned, 1)
                dve.wait_ge(unturned, NT * (1 + first) + 1)
                if first:
                    do = Chain(dve, step_ready)
                    for t in range(NT):
                        dve.bn_stats(m.raw[:, t, :], c.C[:, t, :]).then_inc(measured, 1)
                    dve.wait_ge(measured, NT)
                    m.variance(do).then_inc(var_ready, 1)
                    dve.wait_ge(loaded, 32)
                    do(dve.tensor_tensor(gb[:, 1, :], gb[:, 1, :], c.mix_c[0:TP, :], ALU.add))
                    dve.wait_ge(std_ready, 1)
                    m.factors(do).then_inc(factors, 1)
                    do(dve.tensor_tensor(c.X[:, :, :], c.X[:, :, :], bc(gb[:, 1, :], 1, NT), ALU.add))
                    for g in range(NT // GROUP):
                        rows = slice(g * GROUP, (g + 1) * GROUP)
                        dve.wait_ge(scaled, (g + 1) * GROUP)
                        do(dve.tensor_tensor(c.C[:, rows, :], c.C[:, rows, :], bc(gb[:, 0, :], 1, GROUP), ALU.mult))
                        do(dve.tensor_tensor(c.X[:, rows, :], c.X[:, rows, :], c.C[:, rows, :], ALU.add))


class Router:

    def __init__(self, c, tag, n, ctx):
        self.c, self.n = c, n
        self.rank = c.sb(tag + "rank", [TP, n], ctx=ctx)
        self.eq = c.sb(tag + "eq", [TP, NT, n], ctx=ctx)
        self.hot = [c.sb(tag + f"hot{i}", [TP, NT, n], ctx=ctx) for i in range(2)]
        self.best = [c.sb(tag + f"best{i}", [TP, NT], ctx=ctx) for i in range(2)]
        self.top = c.sb(tag + "top", [TP, NT], ctx=ctx)

    def choose(self, dve, do, s, away):
        n = self.n
        do(dve.tensor_scalar(self.rank[:, :], self.c.iota[0:TP, 0:n], -1.0, float(n), ALU.mult, ALU.add))
        for i in range(2):
            hot, best, eq, top = self.hot[i], self.best[i], self.eq, self.top
            do(dve.tensor_reduce(best[:, :], s, AX.X, ALU.max))
            do(dve.tensor_tensor(eq[:, :, :], s, bc(best[:, :], 2, n), ALU.is_equal))
            do(dve.tensor_tensor(eq[:, :, :], eq[:, :, :], bc(self.rank[:, :], 1, NT), ALU.mult))
            do(dve.tensor_reduce(top[:, :], eq[:, :, :], AX.X, ALU.max))
            do(dve.tensor_tensor(hot[:, :, :], eq[:, :, :], bc(top[:, :], 2, n), ALU.is_equal))
            if i == 0:
                do(dve.scalar_tensor_tensor(out=s, in0=hot[:, :, :], scalar=-away, in1=s, op0=ALU.mult, op1=ALU.add))


def stage_route(c, tag):
    nc = c.nc
    ctx = ExitStack()
    with ctx:
        r = Router(c, tag, E0, ctx)
        total, inv = c.sb(tag + "total", [TP, NT], ctx=ctx), c.sb(tag + "inv", [TP, NT], ctx=ctx)
        steps, shifted, exped = c.sem(tag + "steps"), c.sem(tag + "shifted"), c.sem(tag + "exped")
        L = c.gate[:, :, 0:E0]
        with nc.Block() as block:
            @block.scalar
            def _(act):
                act.wait_ge(shifted, 1)
                act.activation(L, L, ACT.Exp).then_inc(exped, 1)

            @block.vector
            def _(dve):
                do = Chain(dve, steps)
                do(dve.tensor_reduce(total[:, :], L, AX.X, ALU.max))
                dve.tensor_tensor(L, L, bc(total[:, :], 2, E0), ALU.subtract).then_inc(shifted, 1)
                dve.wait_ge(exped, 1)
                do(dve.tensor_reduce(total[:, :], L, AX.X, ALU.add))
                do(dve.reciprocal(inv[:, :], total[:, :]))
                do(dve.tensor_tensor(L, L, bc(inv[:, :], 2, E0), ALU.mult))
                r.choose(dve, do, L, 2.0)
                do(dve.tensor_tensor(total[:, :], r.best[0][:, :], r.best[1][:, :], ALU.add))
                do(dve.tensor_scalar(total[:, :], total[:, :], 1e-12, None, ALU.max))
                do(dve.reciprocal(inv[:, :], total[:, :]))
                for i in range(2):
                    do(dve.tensor_tensor(r.best[i][:, :], r.best[i][:, :], inv[:, :], ALU.mult))
                    do(dve.tensor_tensor(r.hot[i][:, :, :], r.hot[i][:, :, :], bc(r.best[i][:, :], 2, E0), ALU.mult))
                do(dve.tensor_tensor(L, r.hot[0][:, :, :], r.hot[1][:, :, :], ALU.add))


def stage_experts(c, tag, n_exp, F, out):
    nc = c.nc
    ctx = ExitStack()
    FB = F // 128
    NG = NT // GROUP
    UNITS = 2 * NG
    H = len(HALVES) * FB
    with ctx:
        def sb(name, shape, dt=F32):
            return c.sb(tag + name, shape, dt, ctx=ctx)

        w1, w2 = sb("w1", [128, 2, KB, F]), sb("w2", [128, 2, FB, D])
        b1, b2 = sb("b1", [128, 2, FB]), sb("b2", [TP, 2, D])
        tmp = sb("tmp", [TP, 2, D])
        hid = c.big[:, 0:2 * FB * GC].rearrange("p (j f n) -> p j f n", j=2, f=FB)
        w_in = [c.sem(tag + f"w_in{j}") for j in range(2)]
        h_psum, h_ready, y_psum, y_half, y_added = (c.sem(tag + n) for n in ("h_psum", "h_ready", "y_psum", "y_half", "y_added"))
        n_body = n_exp // 2

        with nc.Block() as block:
            @block.sync
            def _(sp):
                def load(e, j):
                    for dst, src in ((w1[:, j, :, :], blocks3(c.i[tag + "w1"], e)), (w2[:, j, :, :], blocks3(c.i[tag + "w2"], e)),
                                     (b1[:, j, :], one(c.i[tag + "b1"], e)), (b2[:, j, :], one(c.i[tag + "b2"], e))):
                        sp.dma_start(dst, src).then_inc(w_in[j], 16)

                def one(ap, e):
                    return ap[bass.ds(e, 1)].rearrange("a p n -> (a p) n")

                def blocks3(ap, e):
                    return ap[bass.ds(e, 1)].rearrange("a (b p) n -> p (a b) n", p=128)
                load(0, 0)
                load(1, 1)
                with sp.Fori(1, n_body) as b:
                    for j in range(2):
                        sp.wait_ge(y_added, (b - 1) * 2 * NT + (j + 1) * NT + 2)
                        c.fence(sp)
                        load(b * 2 + j, j)

            @block.tensor
            def _(pe):
                pe.sem_inc(y_psum, GROUP + 1)

                def hidden(b, v):
                    if v == UNITS:
                        b, v = b + 1, 0
                    j, g = divmod(v, NG)
                    if g == 0:
                        pe.wait_ge(w_in[j], (b + 1) * 64)
                    n = 0
                    for h0, cols in HALVES:
                        for f in range(FB):
                            i = (b * UNITS + v) * H + n
                            pe.wait_ge(h_ready, i + 1)
                            for kb in range(KB):
                                last = pe.matmul(c.ps[n % 4][:, 0:cols], w1[:, j, kb, f * 128:(f + 1) * 128],
                                                 c.CT[:, kb, g * GC + h0:g * GC + h0 + cols], start=(kb == 0),
                                                 stop=(kb == KB - 1))
                            last.then_inc(h_psum, 1)
                            n += 1

                def output(b, v):
                    j, g = divmod(v, NG)
                    unit = b * UNITS + v
                    pe.wait_ge(h_ready, (unit + 1) * H + 4)
                    for q in range(GROUP):
                        i = unit * GROUP + q
                        pe.wait_ge(y_half, i + (4 if q == 0 else 1 if q == 4 else 0))
                        for f in range(FB):
                            last = pe.matmul(c.ps[4 + q % 4][0:TP, 0:D], hid[:, v % 2, f, q * TP:(q + 1) * TP],
                                             w2[:, j, f, :], start=(f == 0), stop=(f == FB - 1))
                        last.then_inc(y_psum, 1)

                hidden(0, 0)
                with pe.Fori(0, n_body - 1) as b:
                    for v in range(UNITS):
                        hidden(b, v + 1)
                        output(b, v)
                for v in range(UNITS):
                    if v + 1 < UNITS:
                        hidden(n_body - 1, v + 1)
                    output(n_body - 1, v)

            @block.scalar
            def _(act):
                act.sem_inc(h_ready, 4)
                with act.Fori(0, n_body) as b:
                    for v in range(UNITS):
                        j, g = divmod(v, NG)
                        n = 0
                        act.wait_ge(y_psum, (b * UNITS + v) * GROUP + 1)
                        for h0, cols in HALVES:
                            for f in range(FB):
                                act.wait_ge(h_psum, (b * UNITS + v) * H + n + 1)
                                act.activation(hid[:, v % 2, f, h0:h0 + cols], c.ps[n % 4][:, 0:cols], ACT.Gelu,
                                               bias=b1[:, j, f:f + 1]).then_inc(h_ready, 1)
                                n += 1

            @block.vector
            def _(dve):
                dve.sem_inc(y_half, 4)
                dve.sem_inc(y_added, 2)

                def biased(b, n):
                    j, g, q = n // NT, n % NT // GROUP, n % GROUP
                    i = b * UNITS * GROUP + n
                    if n % NT == 0:
                        dve.wait_ge(w_in[j], (b + 1) * 64)
                    dve.wait_ge(y_psum, i + 2 + GROUP)
                    dve.wait_ge(y_added, i + 1)
                    dve.tensor_tensor(tmp[:, n % 2, :], c.ps[4 + q % 4][0:TP, 0:D], b2[:, j, :],
                                      ALU.add).then_inc(y_half, 1)

                with dve.Fori(0, n_body) as b:
                    biased(b, 0)
                    for n in range(2 * NT):
                        if n + 1 < 2 * NT:
                            biased(b, n + 1)
                        i = b * UNITS * GROUP + n
                        t = n % NT
                        dve.wait_ge(y_half, i + 5)
                        c.fence(dve)
                        dve.scalar_tensor_tensor(out=out[:, t, :], in0=tmp[:, n % 2, :],
                                                 scalar=c.gate[:, t, bass.ds(b * 2 + n // NT, 1)], in1=out[:, t, :],
                                                 op0=ALU.mult, op1=ALU.add).then_inc(y_added, 1)


def stage_add(c, tag):
    done = c.sem(tag + "done")
    with c.nc.Block() as block:
        @block.vector
        def _(dve):
            Chain(dve, done)(dve.tensor_tensor(c.X[:, :, :], c.X[:, :, :], c.C[:, :, :], ALU.add))


def stage_router_and_experts(c, tag, F):
    nc = c.nc
    ctx = ExitStack()
    CH = GH + GH * E1
    BODY = 2 * SUP
    NB = GSUP // 2
    ROW_SLOTS = 4
    SETS, TURNS = 3, 12
    ROUNDS = SETS * TURNS
    assert TURNS * (GSUP // ROW_SLOTS) * 2 * SUP * 16 < 2 ** 16
    with ctx:
        def sb(name, shape, dt=F32):
            return c.sb(tag + name, shape, dt, ctx=ctx)

        def heads(ap):
            return ap.rearrange("p t (h e) -> p t h e", h=GH)

        rows_s, rows_d = sb("rows_s", [TP, NT, CH]), sb("rows_d", [TP, NT, 2 * GH])
        att = sb("att", [TP, 5, GH * E1])
        t16, agg = sb("t16", [TP, NT, 16]), sb("agg", [TP, NT, 16])
        ends, ends_t, ends_d, ends_all = sb("ends", [TP, 2 * GH]), sb("ends_t", [2 * GH, 1]), sb("ends_d", [2 * GH, 2 * GH]), sb("ends_all", [TP, 2 * GH])
        low, high, mid = sb("low", [TP, NT, GH]), sb("high", [TP, NT, GH]), sb("mid", [TP, NT, GH])
        x4, y4, own = sb("x4", [TP, NT, GH]), sb("y4", [TP, NT, GH]), sb("own", [TP, NT, GH])
        far, far_i = sb("far", [1, 2]), sb("far_i", [1, 1], I32)
        src_i, dst_i = sb("src_i", [128, GSUP * SUP], I32), sb("dst_i", [128, GSUP * SUP], I32)
        lo, hi = sb("lo", [128, GSUP * SUP]), sb("hi", [128, GSUP * SUP])
        idx = sb("idx", [128, ROW_SLOTS, 2, SUP], I32)
        S, T = sb("S", [128, ROW_SLOTS, SUP, CH]), sb("T", [128, ROW_SLOTS, SUP, 2 * GH])
        w, R = sb("w", [128, 2, SUP, GH]), sb("R", [128, 2, SUP, CH])
        row_hot, spread = sb("row_hot", [128, 2, TP]), sb("spread", [128, 2, NT, CH])
        router = Router(c, tag, E1, ctx)
        st = sb("st", [TP, 4, NT])
        FB, NG = F // 128, NT // GROUP
        H = len(HALVES) * FB
        SLOTS = (0, 1, 0, 1, 2)
        STEPS = 6
        w1, w2, b1, b2 = sb("w1", [128, KB, F]), sb("w2", [128, FB, D]), sb("b1", [128, FB]), sb("b2", [1, D])
        hid = c.big[:, 0:3 * FB * GC].rearrange("p (j f n) -> p j f n", j=3, f=FB)
        y = c.big[0:TP, 3 * FB * GC:][:, 0:3 * GROUP * D].rearrange("p (j q d) -> p j q d", j=3, q=GROUP)
        Y = [c.big[0:TP, e * NT * D:(e + 1) * NT * D].rearrange("p (t d) -> p t d", t=NT) for e in range(E1 - 1)] + [c.C]
        zeros = sb("zeros", [1, NT * CH])
        h = c.gate[:, :, 0:16]
        a_src, a_dst, m_dst = rows_s[:, :, 0:GH], rows_d[:, :, 0:GH], rows_d[:, :, GH:2 * GH]
        loads = [(att[:, :, :], c.i["gat_vectors"]), (src_i[:, :], c.i["gat_src"]), (dst_i[:, :], c.i["gat_dst"])]
        loaded, steps, ends_ready, turned, diag_ready, all_ready, flag, tables, tables_in = (
            c.sem(tag + n) for n in ("loaded", "steps", "ends", "turned", "diag", "all", "flag", "tables", "tables_in"))
        gsrc_v, gdst_v = (a.rearrange("(t p) d -> p t d", p=TP) for a in (c.gsrc, c.gdst))

        def leaky(do, dve, out, x):
            do(dve.scalar_tensor_tensor(out=out, in0=x, scalar=0.2, in1=x, op0=ALU.mult, op1=ALU.max))

        with nc.Block() as block:
            @block.sync
            def _(sp):
                for dst, src in loads:
                    sp.dma_start(dst, src).then_inc(loaded, 16)
                sp.wait_ge(tables, 1)
                sp.dma_start(gsrc_v, rows_s[:, :, :]).then_inc(tables_in, 16)
                sp.dma_start(gdst_v, rows_d[:, :, :]).then_inc(tables_in, 16)
                sp.wait_ge(tables_in, 32)

            @block.vector
            def _(dve):
                dve.wait_ge(loaded, 16 * len(loads))
                do = Chain(dve, steps)
                for n, out in ((0, a_src), (1, a_dst)):
                    do(dve.tensor_tensor(t16[:, :, :], h, bc(att[:, n, :], 1, NT), ALU.mult))
                    do(dve.tensor_reduce(out, heads(t16[:, :, :]), AX.X, ALU.add))
                do(dve.tensor_copy(rows_s[:, :, GH:CH], h))
                do(dve.tensor_reduce(ends[:, 0:GH], a_src.rearrange("p t h -> p h t"), AX.X, ALU.max))
                do(dve.tensor_reduce(ends[:, GH:2 * GH], a_src.rearrange("p t h -> p h t"), AX.X, ALU.min))
                dve.tensor_scalar(ends[:, GH:2 * GH], ends[:, GH:2 * GH], -1.0, None, ALU.mult).then_inc(ends_ready, 1)
                dve.wait_ge(turned, 1)
                do(dve.tensor_reduce(ends_t[:, :], c.ps[0][0:2 * GH, 0:TP], AX.X, ALU.max))
                dve.tensor_scalar(ends_d[:, :], c.ident[0:2 * GH, 0:2 * GH], ends_t[:, 0:1], None,
                                  ALU.mult).then_inc(diag_ready, 1)
                dve.wait_ge(all_ready, 1)
                do(dve.tensor_copy(ends_all[:, :], c.ps[1][0:TP, 0:2 * GH]))
                top = bc(ends_all[:, 0:GH], 1, NT)
                do(dve.tensor_tensor(x4[:, :, :], a_dst, top, ALU.add))
                leaky(do, dve, m_dst, x4[:, :, :])
                do(dve.tensor_copy(low[:, :, :], a_src))
                do(dve.tensor_tensor(high[:, :, :], bc(ends_all[:, 0:GH], 1, NT), bc(ends_all[:, 0:GH], 1, NT), ALU.max))
                do(dve.tensor_tensor(ends[:, 0:GH], ends_all[:, 0:GH], ends_all[:, GH:2 * GH], ALU.add))
                do(dve.tensor_reduce(far[:, 0:1], ends[0:1, 0:GH], AX.X, ALU.max))
                do(dve.tensor_scalar(far[:, 1:2], far[:, 0:1], SPAN, None, ALU.is_gt))
                do(dve.tensor_copy(far_i[:, :], far[:, 1:2]))
                dve.sem_inc(tables, 1)
                do(dve.tensor_copy(hi[:, :], dst_i[:, :]))
                do(dve.memset(lo[:, :], 0.0))
                for k in range(1, NT + 1):
                    do(dve.scalar_tensor_tensor(out=lo[:, :], in0=hi[:, :], scalar=float(k * TP), in1=lo[:, :],
                                                op0=ALU.is_ge, op1=ALU.add))
                do(dve.scalar_tensor_tensor(out=hi[:, :], in0=lo[:, :], scalar=-float(TP), in1=hi[:, :], op0=ALU.mult,
                                            op1=ALU.add))
                do(dve.tensor_scalar(src_i[:, :], src_i[:, :], float(NODES - 1), None, ALU.min))
                do(dve.tensor_scalar(dst_i[:, :], dst_i[:, :], float(NODES - 1), None, ALU.min))

            @block.tensor
            def _(pe):
                pe.wait_ge(ends_ready, 1)
                pe.transpose(c.ps[0][0:2 * GH, 0:TP], ends[:, :], c.ident[0:TP, 0:TP]).then_inc(turned, 1)
                pe.wait_ge(diag_ready, 1)
                pe.matmul(c.ps[1][0:TP, 0:2 * GH], c.ones[0:2 * GH, 0:TP], ends_d[:, :], start=True,
                          stop=True).then_inc(all_ready, 1)

        def sums(mode, s):
            def pool_pass(pool, p, turn, g):
                with pool.Fori(0, GSUP // ROW_SLOTS) as k:
                    for j in range(ROW_SLOTS):
                        n = p * GSUP + k * ROW_SLOTS + j
                        pool.wait_ge(s["idx_ready"], n + 1)
                        pool.wait_ge(s["R_ready"], n + 1)
                        pool.sem_inc(s["begun"], 1)
                        for q in range(SUP):
                            pool.indirect_dma_start(S[:, j, q, :], None, c.gsrc,
                                                    bass.IndirectOffsetOnAxis(idx[:, j, 0, q:q + 1], 0)).then_inc(
                                g[j], 16)
                            pool.indirect_dma_start(T[:, j, q, :], None, c.gdst,
                                                    bass.IndirectOffsetOnAxis(idx[:, j, 1, q:q + 1], 0)).then_inc(
                                g[j], 16)

            def dve_pass(dve, p, turn, g):
                def indices(k, j):
                    c.fence(dve)
                    dve.tensor_copy(idx[:, j, 0, :], src_i[:, bass.ds((k * ROW_SLOTS + j) * SUP, SUP)]).then_inc(s["idx_half"], 1)
                    c.fence(dve)
                    dve.tensor_copy(idx[:, j, 1, :], dst_i[:, bass.ds((k * ROW_SLOTS + j) * SUP, SUP)]).then_inc(s["idx_ready"], 1)

                def logits(k, j):
                    n = p * GSUP + k * ROW_SLOTS + j
                    dve.wait_ge(g[j], (turn * (GSUP // ROW_SLOTS) + k + 1) * 16 * 2 * SUP)
                    src, dst, m = S[:, j, :, 0:GH], T[:, j, :, 0:GH], T[:, j, :, GH:2 * GH]
                    dve.wait_ge(s["R_ready"], n + ROW_SLOTS - 1)
                    if mode == "above":
                        dve.tensor_tensor(w[:, j % 2, :, :], src, m, ALU.is_gt).then_inc(s["w_ready"], 1)
                        return
                    dve.tensor_tensor(w[:, j % 2, :, :], src, dst, ALU.add).then_inc(s["e_steps"], 1)
                    dve.wait_ge(s["e_steps"], n * 3 + 1)
                    dve.scalar_tensor_tensor(out=w[:, j % 2, :, :], in0=w[:, j % 2, :, :], scalar=0.2, in1=w[:, j % 2, :, :],
                                             op0=ALU.mult, op1=ALU.max).then_inc(s["e_steps"], 1)
                    dve.wait_ge(s["e_steps"], n * 3 + 2)
                    dve.tensor_tensor(w[:, j % 2, :, :], w[:, j % 2, :, :], m, ALU.subtract).then_inc(s["e_steps"], 1)
                    dve.wait_ge(s["e_steps"], n * 3 + 3)
                    dve.tensor_scalar(w[:, j % 2, :, :], w[:, j % 2, :, :], 0.0, None, ALU.min).then_inc(s["e_ready"], 1)

                def weighted(k, j):
                    n = p * GSUP + k * ROW_SLOTS + j
                    dve.wait_ge(s["w_ready"], n + 1)
                    dve.wait_ge(s["spread_ready"], n * SUP + 1)
                    dve.tensor_copy(R[:, j % 2, :, 0:GH], w[:, j % 2, :, :]).then_inc(s["R_half"], 1)
                    dve.tensor_tensor(R[:, j % 2, :, GH:CH].rearrange("p q (h e) -> p q h e", h=GH),
                                      S[:, j, :, GH:CH].rearrange("p q (h e) -> p q h e", h=GH),
                                      bc(w[:, j % 2, :, :], 3, E1), ALU.mult).then_inc(s["R_ready"], 1)

                def hots(k, j):
                    for q in range(SUP):
                        i = p * GSUP * SUP + (k * ROW_SLOTS + j) * SUP + q
                        at = (k * ROW_SLOTS + j) * SUP + q
                        dve.wait_ge(s["tile_used"], i + 1)
                        if q == 0:
                            dve.wait_ge(s["R_half"], p * GSUP + k * ROW_SLOTS + j + 1)
                            dve.wait_ge(s["R_ready"], p * GSUP + k * ROW_SLOTS + j + 1 + ROW_SLOTS)
                        c.fence(dve)
                        dve.tensor_scalar(row_hot[:, q % 2, :], c.iota[:, 0:TP], hi[:, bass.ds(at, 1)], None,
                                          ALU.is_equal).then_inc(s["hot_ready"], 1)
                        c.fence(dve)
                        dve.scalar_tensor_tensor(out=spread[:, q % 2, :, :], in0=bc(c.iota[:, 0:NT], 2, CH),
                                                 scalar=lo[:, bass.ds(at, 1)], in1=bc(R[:, j % 2, q, :], 1, NT),
                                                 op0=ALU.is_equal, op1=ALU.mult).then_inc(s["spread_ready"], 1)

                def supertile(k, j, last=False):
                    weighted(k, j)
                    if not last:
                        indices(k + 1, j)
                    if not (last and j == ROW_SLOTS - 1):
                        logits(*((k, j + 1) if j + 1 < ROW_SLOTS else (k + 1, 0)))
                    hots(k, j)

                for j in range(ROW_SLOTS):
                    indices(0, j)
                logits(0, 0)
                with dve.Fori(0, GSUP // ROW_SLOTS - 1) as k:
                    for j in range(ROW_SLOTS):
                        supertile(k, j)
                for j in range(ROW_SLOTS):
                    supertile(GSUP // ROW_SLOTS - 1, j, last=True)

            def pe_pass(pe, p):
                def body(k, first, last):
                    for u in range(BODY):
                        i = p * GSUP * SUP + k * BODY + u
                        pe.wait_ge(s["hot_ready"], i + 1)
                        pe.wait_ge(s["spread_ready"], i + 2)
                        pe.matmul(c.ps[7][0:TP, 0:NT * CH], row_hot[:, u % 2, :],
                                  spread[:, u % 2, :, :].rearrange("p t c -> p (t c)"),
                                  start=first and u == 0, stop=last and u == BODY - 1).then_inc(s["tile_used"], 1)
                body(0, True, False)
                with pe.Fori(1, NB - 1) as k:
                    body(k, False, False)
                body(NB - 1, False, True)

            return pool_pass, dve_pass, pe_pass

        names = ("idx_half", "idx_ready", "begun", "R_half", "R_ready", "e_steps", "e_ready", "w_ready",
                 "spread_ready", "hot_ready", "tile_used", "moved", "stored")
        acc = c.ps[7][0:TP, 0:NT * CH].rearrange("p (t c) -> p t c", t=NT)

        s = {n: c.sem(tag + "g_" + n) for n in names}
        pool_pass, dve_pass, pe_pass = sums("above", s)
        gathered = [[c.sem(f"{tag}g_in{n}_{j}") for j in range(ROW_SLOTS)] for n in range(SETS)]

        def if_far(eng, work):
            more = eng.value_load(far_i[0:1, 0:1], min_val=0, max_val=1)
            with eng.If(more > 0):
                work(eng)

        with nc.Block() as block:
            @block.sync
            def _(sp):
                def work(sp):
                    with sp.Fori(0, ROUNDS + 1) as p:
                        sp.wait_ge(s["moved"], p + 1)
                        c.fence(sp)
                        sp.dma_start(gdst_v, rows_d[:, :, :]).then_inc(s["stored"], 16)
                if_far(sp, work)

            @block.gpsimd
            def _(pool):
                def work(pool):
                    with pool.Fori(0, TURNS) as turn:
                        for n in range(SETS):
                            p = turn * SETS + n
                            pool.wait_ge(s["stored"], 16 * p + 16)
                            pool.sem_inc(s["begun"], 1)
                            pool_pass(pool, p, turn, gathered[n])
                if_far(pool, work)

            @block.tensor
            def _(pe):
                def work(pe):
                    pe.sem_inc(s["tile_used"], 2)
                    with pe.Fori(0, ROUNDS) as p:
                        pe.wait_ge(s["moved"], p + 1)
                        pe_pass(pe, p)
                if_far(pe, work)

            @block.vector
            def _(dve):
                def work(dve):
                    step = c.sem(tag + "g_steps")
                    PER = 10

                    def halve(do):
                        do(dve.tensor_tensor(mid[:, :, :], high[:, :, :], low[:, :, :], ALU.subtract))
                        do(dve.scalar_tensor_tensor(out=mid[:, :, :], in0=mid[:, :, :], scalar=0.5, in1=low[:, :, :],
                                                    op0=ALU.mult, op1=ALU.add))
                        do(dve.tensor_copy(m_dst, mid[:, :, :]))
                        dve.sem_inc(s["moved"], 1)
                    dve.sem_inc(s["R_ready"], ROW_SLOTS)
                    dve.sem_inc(s["spread_ready"], 1)
                    first = Chain(dve, step)
                    halve(first)
                    def one_round(turn, n, g):
                        p = turn * SETS + n
                        dve.wait_ge(s["stored"], 16 * p + 16)
                        dve_pass(dve, p, turn, g)
                        dve.wait_ge(s["tile_used"], (p + 1) * GSUP * SUP + 2)
                        do = Chain(dve, step, p * PER + first.n)
                        do(dve.tensor_scalar(x4[:, :, :], acc[:, :, 0:GH], 0.5, None, ALU.is_gt))
                        do(dve.tensor_tensor(y4[:, :, :], mid[:, :, :], low[:, :, :], ALU.subtract))
                        do(dve.tensor_tensor(y4[:, :, :], y4[:, :, :], x4[:, :, :], ALU.mult))
                        do(dve.tensor_tensor(low[:, :, :], low[:, :, :], y4[:, :, :], ALU.add))
                        do(dve.tensor_scalar(x4[:, :, :], x4[:, :, :], -1.0, 1.0, ALU.mult, ALU.add))
                        do(dve.tensor_tensor(y4[:, :, :], mid[:, :, :], high[:, :, :], ALU.subtract))
                        do(dve.tensor_tensor(y4[:, :, :], y4[:, :, :], x4[:, :, :], ALU.mult))
                        do(dve.tensor_tensor(high[:, :, :], high[:, :, :], y4[:, :, :], ALU.add))
                        do(dve.tensor_tensor(x4[:, :, :], a_dst, high[:, :, :], ALU.add))
                        leaky(do, dve, own[:, :, :], x4[:, :, :])
                        assert do.n == PER
                        do = Chain(dve, half_steps, p * 3)
                        halve(do)

                    with dve.Fori(0, TURNS) as turn:
                        for n in range(SETS):
                            one_round(turn, n, gathered[n])
                    dve.wait_ge(s["stored"], 16 * ROUNDS + 16)
                    do = Chain(dve, step, ROUNDS * PER + first.n)
                    do(dve.tensor_copy(m_dst, own[:, :, :]))
                half_steps = c.sem(tag + "g_half")
                if_far(dve, work)

        s = {n: c.sem(tag + "w_" + n) for n in names}
        w_in = [c.sem(f"{tag}w_in{j}") for j in range(ROW_SLOTS)]
        wpool, wdve, _ = sums("weights", s)
        own_in, own_ready, var_ready, std_ready, e_in, e_ready, chosen, guarded = (
            c.sem(tag + n) for n in ("own_in", "own_ready", "var", "std", "e_in", "e_out", "chosen", "guarded"))
        done2 = c.sem(tag + "steps2")
        w1_in, w2_in, zeroed, h_psum, h_ready, y_psum, y_kept, Y_in = (
            c.sem(tag + n) for n in ("w1_in", "w2_in", "zeroed", "h_psum", "h_ready", "y_psum", "y_kept", "Y_in"))
        y_stored = [c.sem(f"{tag}y_stored{j}") for j in range(3)]
        USES = [SLOTS.count(j) for j in range(3)]
        h_list = [(f, h) for h in range(len(HALVES)) for f in range(FB)]

        def by_block(ap):
            return ap.rearrange("a (b p) n -> p (a b) n", p=128)

        def pieces(step):
            return [n for n in (2 * step, 2 * step + 1) if n < H], step if step < GROUP else None

        def program(eng, do_step):
            def expert(e):
                for g in range(NG):
                    for step in range(STEPS):
                        do_step((e * NG + g) * STEPS + step, e, g, step)
            with eng.Fori(0, E1 - 1) as e:
                expert(e)
            expert(E1 - 1)
            for n in range(E1 * NG * STEPS, GSUP):
                do_step(n, None, None, None)

        def after(e, g):
            if g + 1 < NG:
                return e, g + 1
            return None if isinstance(e, int) and e == E1 - 1 else (e + 1, 0)

        def load_w1(sp, e):
            sp.dma_start(w1[:, :, :], by_block(c.i["m1_w1"][bass.ds(e, 1)])).then_inc(w1_in, 16)
            c.fence(sp)
            sp.dma_start(b1[:, :], c.i["m1_b1"][bass.ds(e, 1)].rearrange("a p n -> (a p) n")).then_inc(w1_in, 16)

        def load_w2(sp, e):
            sp.dma_start(w2[:, :, :], by_block(c.i["m1_w2"][bass.ds(e, 1)])).then_inc(w2_in, 16)
            c.fence(sp)
            sp.dma_start(b2[:, :], c.i["m1_b2"][bass.ds(e, 1), 0:1].rearrange("a p n -> (a p) n")).then_inc(w2_in, 16)

        def sp_experts(sp):
            load_w1(sp, 0)
            load_w2(sp, 0)

            def expert(e, more):
                for g in range(NG):
                    if more and g == NG - 2:
                        sp.wait_ge(h_ready, (e + 1) * NG * H + 4)
                        c.fence(sp)
                        load_w1(sp, e + 1)
                    sp.wait_ge(y_kept, (e * NG + g + 1) * GROUP + 2)
                    if more and g == NG - 1:
                        c.fence(sp)
                        load_w2(sp, e + 1)
                    c.fence(sp)
                    sp.dma_start(c.experts[bass.ds(e, 1), g * GC:(g + 1) * GC].rearrange("a (t p) d -> p (a t) d", p=TP),
                                 y[:, SLOTS[g], :, :]).then_inc(y_stored[SLOTS[g]], 16)
            with sp.Fori(0, E1 - 1) as e:
                expert(e, True)
            expert(E1 - 1, False)
            for j in range(3):
                sp.wait_ge(y_stored[j], 16 * (E1 * USES[j] + 1))
            for e in range(E1):
                sp.dma_start(Y[e][:, :, :], c.experts[e].rearrange("(t p) d -> p t d", p=TP)).then_inc(Y_in, 16)

        def pe_experts(pe):
            def hidden(e, g, n):
                f, h = h_list[n]
                h0, cols = HALVES[h]
                if g == 0 and n == 0:
                    pe.wait_ge(w1_in, (e + 1) * 32)
                pe.wait_ge(h_ready, (e * NG + g) * H + n + 1)
                for kb in range(KB):
                    last = pe.matmul(c.ps[n % 4][:, 0:cols], w1[:, kb, f * 128:(f + 1) * 128],
                                     c.CT[:, kb, g * GC + h0:g * GC + h0 + cols], start=(kb == 0), stop=(kb == KB - 1))
                last.then_inc(h_psum, 1)

            def output(e, g, q):
                if q == 0:
                    if g == 0:
                        pe.wait_ge(w2_in, (e + 1) * 32)
                    pe.wait_ge(h_ready, (e * NG + g + 1) * H + 4)
                pe.wait_ge(y_kept, (e * NG + g) * GROUP + q + 1)
                bank = c.ps[4 + q % 3][0:TP, 0:D]
                pe.matmul(bank, c.ones[0:1, 0:TP], b2[0:1, :], start=True, stop=False)
                for f in range(FB):
                    last = pe.matmul(bank, hid[:, SLOTS[g], f, q * TP:(q + 1) * TP], w2[:, f, :], start=False,
                                     stop=(f == FB - 1))
                last.then_inc(y_psum, 1)

            def do_step(n, e, g, step):
                work = []
                if e is not None:
                    ahead, q = pieces(step)
                    if after(e, g):
                        work += [(hidden, *after(e, g), m) for m in ahead]
                    if q is not None:
                        work += [(output, e, g, q)]
                for u in range(SUP):
                    i = n * SUP + u
                    pe.wait_ge(s["hot_ready"], i + 1)
                    pe.wait_ge(s["spread_ready"], i + 2)
                    pe.matmul(c.ps[7][0:TP, 0:NT * CH], row_hot[:, u % 2, :],
                              spread[:, u % 2, :, :].rearrange("p t c -> p (t c)"), start=False,
                              stop=isinstance(n, int) and i == GSUP * SUP - 1).then_inc(s["tile_used"], 1)
                    if u < len(work):
                        work[u][0](*work[u][1:])

            pe.wait_ge(zeroed, 1)
            pe.matmul(c.ps[7][0:TP, 0:NT * CH], c.ones[0:1, 0:TP], zeros[0:1, :], start=True, stop=False)
            for n in range(H):
                hidden(0, 0, n)
            program(pe, do_step)

        def act_experts(act):
            def gelu(e, g, n):
                f, h = h_list[n]
                h0, cols = HALVES[h]
                if g == 0 and n == 0:
                    act.wait_ge(w1_in, (e + 1) * 32)
                if n == 0:
                    act.wait_ge(y_psum, (e * NG + g) * GROUP + 1)
                act.wait_ge(h_psum, (e * NG + g) * H + n + 1)
                act.activation(hid[:, SLOTS[g], f, h0:h0 + cols], c.ps[n % 4][:, 0:cols], ACT.Gelu,
                               bias=b1[:, f:f + 1]).then_inc(h_ready, 1)

            def keep(e, g, q):
                if q == 0:
                    j = SLOTS[g]
                    act.wait_ge(y_stored[j], 16 * (e * USES[j] + SLOTS[:g].count(j) + 1))
                act.wait_ge(y_psum, (e * NG + g) * GROUP + q + 1 + 2 * GROUP)
                act.activation(y[:, SLOTS[g], q, :], c.ps[4 + q % 3][0:TP, 0:D], ACT.Copy).then_inc(y_kept, 1)

            def do_step(n, e, g, step):
                if not (isinstance(n, int) and n == GSUP - 1):
                    j = 1 - (n if step is None else step) % 2
                    act.wait_ge(s["e_ready"], n + 2)
                    act.activation(w[:, j, :, :], w[:, j, :, :], ACT.Exp).then_inc(s["w_ready"], 1)
                if e is not None and step > 0:
                    made, q = pieces(step - 1)
                    if after(e, g):
                        for m in made:
                            gelu(*after(e, g), m)
                    if q is not None:
                        keep(e, g, q)

            for n in range(H):
                gelu(0, 0, n)
            act.wait_ge(s["e_ready"], 1)
            act.activation(w[:, 0, :, :], w[:, 0, :, :], ACT.Exp).then_inc(s["w_ready"], 1)
            program(act, do_step)

        with nc.Block() as block:
            @block.sync
            def _(sp):
                def work(sp):
                    sp.dma_start(gdst_v, rows_d[:, :, :]).then_inc(guarded, 16)
                    sp.wait_ge(guarded, 16)
                if_far(sp, work)
                sp.sem_inc(tables, 1)
                sp_experts(sp)

            @block.gpsimd
            def _(pool):
                pool.wait_ge(tables, 2)
                wpool(pool, 0, 0, w_in)

            @block.tensor
            def _(pe):
                pe.sem_inc(s["tile_used"], 2)
                pe.sem_inc(y_psum, 2 * GROUP)
                pe_experts(pe)

            @block.scalar
            def _(act):
                act.sem_inc(h_ready, 4)
                act.sem_inc(y_kept, 2)
                for j in range(3):
                    act.sem_inc(y_stored[j], 16)
                act.wait_ge(own_in, 1)
                act.activation(own[:, :, :], own[:, :, :], ACT.Exp).then_inc(own_ready, 1)
                act_experts(act)
                act.wait_ge(var_ready, 1)
                act.activation(st[:, 2, :], st[:, 1, :], ACT.Sqrt).then_inc(std_ready, 1)
                act.wait_ge(e_in, 1)
                act.activation(router.best[1][:, :], router.best[1][:, :], ACT.Exp).then_inc(e_ready, 1)

            @block.vector
            def _(dve):
                do = Chain(dve, done2)
                dve.memset(zeros[:, :], 0.0).then_inc(zeroed, 1)
                dve.sem_inc(s["R_ready"], ROW_SLOTS)
                dve.sem_inc(s["spread_ready"], 1)
                do(dve.tensor_tensor(x4[:, :, :], a_src, a_dst, ALU.add))
                leaky(do, dve, y4[:, :, :], x4[:, :, :])
                dve.tensor_tensor(own[:, :, :], y4[:, :, :], m_dst, ALU.subtract).then_inc(own_in, 1)
                wdve(dve, 0, 0, w_in)
                dve.wait_ge(own_ready, 1)
                dve.wait_ge(s["tile_used"], GSUP * SUP + 2)
                do(dve.tensor_tensor(x4[:, :, :], acc[:, :, 0:GH], own[:, :, :], ALU.add))
                do(dve.tensor_scalar(x4[:, :, :], x4[:, :, :], 1e-16, None, ALU.add))
                do(dve.reciprocal(y4[:, :, :], x4[:, :, :]))
                do(dve.tensor_tensor(heads(t16[:, :, :]), heads(h), bc(own[:, :, :], 3, E1), ALU.mult))
                do(dve.tensor_tensor(t16[:, :, :], t16[:, :, :], acc[:, :, GH:CH], ALU.add))
                do(dve.tensor_tensor(heads(agg[:, :, :]), heads(t16[:, :, :]), bc(y4[:, :, :], 3, E1), ALU.mult))
                do(dve.tensor_tensor(agg[:, :, :], agg[:, :, :], bc(att[:, 2, :], 1, NT), ALU.add))
                mean, var, std, rstd = (st[:, n, :] for n in range(4))
                do(dve.tensor_reduce(mean, agg[:, :, :], AX.X, ALU.add))
                do(dve.tensor_scalar(mean, mean, 1.0 / 16, None, ALU.mult))
                do(dve.tensor_tensor(agg[:, :, :], agg[:, :, :], bc(mean, 2, 16), ALU.subtract))
                do(dve.tensor_tensor(t16[:, :, :], agg[:, :, :], agg[:, :, :], ALU.mult))
                do(dve.tensor_reduce(var, t16[:, :, :], AX.X, ALU.add))
                dve.tensor_scalar(var, var, 1.0 / 16, EPS, ALU.mult, ALU.add).then_inc(var_ready, 1)
                dve.wait_ge(std_ready, 1)
                do(dve.reciprocal(rstd, std))
                do(dve.tensor_tensor(agg[:, :, :], agg[:, :, :], bc(rstd, 2, 16), ALU.mult))
                do(dve.tensor_tensor(agg[:, :, :], agg[:, :, :], bc(att[:, 3, :], 1, NT), ALU.mult))
                do(dve.tensor_tensor(agg[:, :, :], agg[:, :, :], bc(att[:, 4, :], 1, NT), ALU.add))
                do(dve.tensor_reduce(x4[:, :, :], agg[:, :, :].rearrange("p t (h e) -> p t e h", h=GH), AX.X, ALU.add))
                do(dve.tensor_scalar(x4[:, :, :], x4[:, :, :], 1.0 / GH, None, ALU.mult))
                router.choose(dve, do, x4[:, :, :], HUGE)
                first, second = (router.best[i][:, :] for i in range(2))
                dve.tensor_tensor(second, second, first, ALU.subtract).then_inc(e_in, 1)
                dve.wait_ge(e_ready, 1)
                do(dve.tensor_scalar(first, second, 1.0, None, ALU.add))
                do(dve.reciprocal(router.top[:, :], first))
                do(dve.tensor_tensor(second, second, router.top[:, :], ALU.mult))
                for i, wt in ((0, router.top[:, :]), (1, second)):
                    do(dve.tensor_tensor(router.hot[i][:, :, :], router.hot[i][:, :, :], bc(wt, 2, E1), ALU.mult))
                do(dve.tensor_tensor(c.gate[:, :, 0:E1], router.hot[0][:, :, :], router.hot[1][:, :, :], ALU.add))
                dve.wait_ge(Y_in, 16 * E1)

        added, stored = c.sem(tag + "added"), c.sem(tag + "stored")
        with nc.Block() as block:
            @block.vector
            def _(dve):
                dve.sem_inc(added, GROUP)
                for g in range(NG):
                    for e in range(E1):
                        for t in range(g * GROUP, (g + 1) * GROUP):
                            i = (g * E1 + e) * GROUP + t % GROUP
                            dve.wait_ge(added, i + 1)
                            dve.scalar_tensor_tensor(out=c.X[:, t, :], in0=Y[e][:, t, :], scalar=c.gate[:, t, e:e + 1],
                                                     in1=c.X[:, t, :], op0=ALU.mult, op1=ALU.add).then_inc(added, 1)

            @block.sync
            def _(sp):
                for g in range(NG):
                    sp.wait_ge(added, (g + 1) * E1 * GROUP + GROUP)
                    sp.dma_start(c.out.rearrange("(t p) d -> p t d", p=TP)[:, g * GROUP:(g + 1) * GROUP, :],
                                 c.X[:, g * GROUP:(g + 1) * GROUP, :]).then_inc(stored, 16)
                sp.wait_ge(stored, 16 * NG)


def stage_output(c, what=None):
    nc = c.nc
    done = c.sem("output_stored")
    with nc.Block() as block:
        @block.sync
        def _(sp):
            sp.dma_start(c.out.rearrange("(t p) d -> p t d", p=TP), (c.X if what is None else what)[:, :, :]).then_inc(done, 16)
            sp.wait_ge(done, 16)


def build(nc, ins, out, stop=99):
    ctx = ExitStack()
    with ctx:
        c = Core(nc, ctx, ins, out)
        stage_constants(c)
        with ExitStack() as sub:
            w = c.wt[:, :, 0:1024]
            bias = c.sb("bias0", [TP, 1024], ctx=sub)
            stage_norm(c, "n0_", [
                dict(w=w[:, :, 0:512], w_in=blocks(ins["node_w0"]), n=512, bias=bias[:, 0:512], bias_in=ins["node_b0"], out=None),
                dict(w=w[:, :, 512:1024], w_in=blocks(ins["kv_w0"]), n=512, bias=bias[:, 512:1024], bias_in=ins["kv_b0"], out=c.kv)], keep=True)
        if stop == 1:
            return stage_output(c, c.C)
        stage_context(c, "c0_", True)
        stage_edges(c, "e0_", False)
        stage_sum(c, "s0_", True)
        c.retire()
        if stop == 3:
            return stage_output(c)
        stage_norm(c, "n1_", [dict(w=c.wt[:, :, 0:E0], w_in=blocks(ins["route_w"]), n=E0, bias=None, bias_in=None, out=c.gate)], keep=True)
        stage_route(c, "r0_")
        stage_experts(c, "m0_", E0, D, c.C)
        stage_add(c, "a0_")
        c.retire()
        if stop == 4:
            return stage_output(c)
        with ExitStack() as sub:
            kvw = c.sb("kv_w1", [128, KB, 512], ctx=sub)
            no_bias = dict(bias=None, bias_in=None)
            stage_norm(c, "n2_", [dict(w=c.wt[:, :, n * 512:(n + 1) * 512],
                                       w_in=blocks(ins["rel_w"])[:, :, n * 512:(n + 1) * 512], n=512, out=None, **no_bias)
                                  for n in range(RELS // 2)]
                       + [dict(w=kvw[:, :, :], w_in=blocks(ins["kv_w1"]), n=512, out=c.kv, **no_bias)], keep=False)
        stage_context(c, "c1_", False)
        c.retire()
        stage_edges(c, "e1_", True)
        stage_sum(c, "s1_", False)
        c.retire()
        if stop == 5:
            return stage_output(c)
        stage_norm(c, "n3_", [dict(w=c.wt[:, :, 0:16], w_in=blocks(ins["gat_w"]), n=16, bias=None, bias_in=None, out=c.gate)], keep=False)
        stage_router_and_experts(c, "g1_", F1)


def prepare(i):
    import numpy as np

    def rep(v, n):
        return np.ascontiguousarray(np.broadcast_to(v, (n, v.size)))

    def cols(v):
        return np.ascontiguousarray(v.reshape(-1, 128).T)

    def edges(v, fill):
        full = np.full(NET * ET, fill, v.dtype)
        full[:EDGES] = v.reshape(-1)
        return full

    a = {"x": i["x"]}
    dst = edges(i["dst"], -4000)
    a["dst_t"] = np.ascontiguousarray(dst.reshape(NET, ET).T)
    a["dst_base"] = rep(dst[::ES], 128)
    a["src_t"] = np.ascontiguousarray(edges(i["src"], 0).reshape(NET, ET).T)
    a["type_t"] = np.ascontiguousarray(edges(i["edge_type_16"], 0).reshape(NET, ET).T)
    a["norm_t"] = np.ascontiguousarray(edges(i["edge_weight1"], 0).reshape(NET, ET).T)
    attr = np.zeros((DE, NET * ET), np.float32)
    attr[:, :EDGES] = i["edge_attr_64"].T
    a["attr_t"] = attr
    a["node_w0"] = np.concatenate([i["L0_gnn_W1"][:D], i["L0_gnn_Wg"][:D]], 1)
    a["edge_w0"] = np.concatenate([i["L0_gnn_W1"][D:], i["L0_gnn_Wg"][D:]], 1)
    a["node_b0"] = rep(np.concatenate([i["L0_gnn_b1"], i["L0_gnn_bg"]]), TP)
    a["w2_0"], a["b2_0"] = i["L0_gnn_W2"], rep(i["L0_gnn_b2"], 128)
    a["gnn0_gamma"], a["gnn0_beta"] = rep(i["L0_gnn_gamma"], TP), rep(i["L0_gnn_beta"], TP)
    a["kv_w0"] = np.concatenate([i["L0_mix_W_qk"][1], i["L0_mix_W_v"]], 1)
    a["kv_b0"] = rep(np.concatenate([i["L0_mix_b_qk"][1], i["L0_mix_b_v"]]), TP)
    a["wq0_t"] = np.ascontiguousarray(i["L0_mix_W_qk"][0].T)
    a["bq0"] = np.ascontiguousarray(rep(i["L0_mix_b_qk"][0], TP).T)
    a["mix0_gamma"], a["mix0_beta"] = cols(i["L0_mix_gamma"]), cols(i["L0_mix_beta"])
    a["kv_w1"] = np.ascontiguousarray(i["L1_mix_Wkv"].T)
    a["wq1_t"], a["wproj_t"] = np.ascontiguousarray(i["L1_mix_Wq"].T), np.ascontiguousarray(i["L1_mix_Wproj"].T)
    a["bproj"] = cols(i["L1_mix_bproj"])
    a["rel_w"] = np.ascontiguousarray(i["L1_gnn_weight"].transpose(1, 0, 2).reshape(D, RELS * D))
    a["route_w"] = np.ascontiguousarray(i["L0_ffn_router_w"].T)
    a["gat_w"] = i["L1_ffn_W_gat"]
    for tag, name, n in (("m0_", "L0_ffn_", E0), ("m1_", "L1_ffn_", E1)):
        ws = [i[name + ("w1" if n == E0 else "W1")], i[name + ("w2" if n == E0 else "W2")]]
        a[tag + "w1"], a[tag + "w2"] = ws
        a[tag + "b1"] = np.ascontiguousarray(i[name + "b1"].reshape(n, -1, 128).transpose(0, 2, 1))
        a[tag + "b2"] = np.ascontiguousarray(np.broadcast_to(i[name + "b2"][:, None, :], (n, TP, D)))
    a["gat_vectors"] = np.ascontiguousarray(np.broadcast_to(np.stack([i["L1_ffn_" + n].reshape(-1) for n in (
        "att_src", "att_dst", "b_gat", "ln_gamma", "ln_beta")]), (TP, 5, 16)))
    for n, row in (("gat_src", 0), ("gat_dst", 1)):
        a[n] = np.ascontiguousarray(i["L1_ffn_edge_index"][row].reshape(-1, ET).T)
    return a


def kernel(**inputs):
    import numpy as np
    import concourse.bacc as bacc
    from concourse.bass_utils import run_bass_kernel_spmd as run

    nc = bacc.Bacc("TRN2", target_bir_lowering=False, num_devices=1)
    arrays = prepare({k: np.asarray(v) for k, v in inputs.items()})
    ins = {n: nc.dram_tensor(f"in_{n}", a.shape, mybir.dt.from_np(a.dtype), kind="ExternalInput").ap()
           for n, a in arrays.items()}
    out = nc.dram_tensor("out", (NODES, D), F32, kind="ExternalOutput").ap()
    build(nc, ins, out)
    r = run(nc, [{f"in_{n}": a for n, a in arrays.items()}], core_ids=[0])
    return r.results[0]["out"]
```
